# Optimizing a Trainium2 kernel written in Bass

```python
import numpy as np
import jax
import jax.numpy as jnp

def _softmax(x, axis=-1):
    return jax.nn.softmax(x, axis=axis)

def _gelu(x):
    return jax.nn.gelu(x, approximate=True)

def _silu(x):
    return jax.nn.silu(x)

def _sigmoid(x):
    return jax.nn.sigmoid(x)

def _layernorm(x, axis=-1, eps=1e-05):
    m = jnp.mean(x, axis=axis, keepdims=True)
    v = jnp.var(x, axis=axis, keepdims=True)
    return (x - m) / jnp.sqrt(v + eps)

def _scatter_add(tgt, idx, src, axis=0):
    return tgt.at[idx].add(src)

def _segment_sum(src, seg, n):
    return jax.ops.segment_sum(src, seg, n)
kernel_name = 'mk_gnn_resnorm_d2_gnn_r8_a379b0'

def setup_inputs(seed: int=0):
    np.random.seed(seed)
    _w = jnp.asarray

    def _rec_inputs():
        import jax
        import jax.numpy as jnp
        _gk = jax.random.key(seed)
        x = -0.000929 + 1 * jax.random.normal(jax.random.fold_in(_gk, 1), (12500, 32), jnp.float32)
        src = jax.random.randint(jax.random.fold_in(_gk, 2), (400000,), 0, 12500, jnp.int32)
        dst = jax.random.randint(jax.random.fold_in(_gk, 3), (400000,), 0, 12500, jnp.int32)
        _o = jnp.argsort(dst, stable=True)
        src = src[_o]
        dst = dst[_o]
        edge_attr_3 = jax.random.uniform(jax.random.fold_in(_gk, 11), (400000, 3), jnp.float32, 0.0, 1)
        edge_attr_4 = 0.00086875 + 0.999764 * jax.random.normal(jax.random.fold_in(_gk, 12), (400000, 4), jnp.float32)
        edge_attr_8 = jax.random.uniform(jax.random.fold_in(_gk, 13), (400000, 8), jnp.float32, 0.0, 1)
        return (x, src, dst, edge_attr_3, edge_attr_4, edge_attr_8)
    x, src, dst, edge_attr_3, edge_attr_4, edge_attr_8 = _rec_inputs()

    def _L0_gnn_setup():
        import jax, jax.numpy as jnp
        import numpy as np
        N = 4096
        E = 65536
        MUL = 8
        NB = 8
        HR = 64
        NTP = 4 * MUL * MUL
        AVG_NEI = 16.0
        INV_SQRT3 = 1.0 / np.sqrt(3.0)
        ALPHA = 1.0 / np.sqrt(2.0 * MUL)
        key = jax.random.key(seed)
        ks = jax.random.split(key, 12)
        h = jax.random.normal(ks[0], (N, 4 * MUL), jnp.float32)
        edge_index = jax.random.randint(ks[1], (2, E), 0, N)
        edge_sh = jax.random.normal(ks[2], (E, 4), jnp.float32)
        edge_radial = jax.random.uniform(ks[3], (E, NB), jnp.float32)

        def lin(k, fi, fo):
            return (jax.random.normal(k, (fi, fo), jnp.float32) / np.sqrt(fi)).astype(jnp.float32)
        W1 = lin(ks[4], NB, HR)
        b1 = jnp.zeros((HR,), jnp.float32)
        W2 = lin(ks[5], HR, HR)
        b2 = jnp.zeros((HR,), jnp.float32)
        W3 = lin(ks[6], HR, NTP)
        b3 = jnp.zeros((NTP,), jnp.float32)
        Ws = jax.random.normal(ks[7], (MUL, MUL), jnp.float32)
        Wv = jax.random.normal(ks[8], (MUL, MUL), jnp.float32)
        return dict(h=h, edge_index=edge_index, edge_sh=edge_sh, edge_radial=edge_radial, n_atoms=N, W1=W1, b1=b1, W2=W2, b2=b2, W3=W3, b3=b3, Ws=Ws, Wv=Wv)
    _L0_gnn_all = _L0_gnn_setup()
    _L0_gnn_in = {k: v for k, v in _L0_gnn_all.items() if k in ('W1', 'b1', 'W2', 'b2', 'W3', 'b3', 'Ws', 'Wv')}
    del _L0_gnn_all

    def _L1_gnn_setup():
        import jax, jax.numpy as jnp
        import numpy as np
        N = 6250
        E = 200000
        C = 32
        KS = 4
        DIM = 3
        K3 = KS ** DIM
        NEG = 0.01
        EPS = 1e-05
        _BITS = np.array([[s >> d & 1 for d in range(DIM)] for s in range(2 ** DIM)], dtype=np.int32)

        def _basis(edge_attr):
            v = edge_attr * (KS - 1)
            lo = jnp.floor(v)
            f = v - lo
            lo = lo.astype(jnp.int32)
            bits = jnp.asarray(_BITS)
            idx = jnp.clip(lo[:, None, :] + bits[None], 0, KS - 1)
            w = jnp.where(bits[None] == 1, f[:, None, :], 1.0 - f[:, None, :])
            basis = jnp.prod(w, axis=-1)
            wi = idx[..., 0] + KS * idx[..., 1] + KS * KS * idx[..., 2]
            return (basis, wi)

        def _sconv(x, src, dst, basis, wi, W, R, b):
            n = x.shape[0]
            z = jnp.einsum('nc,kco->nko', x, W)
            msg = jnp.zeros((src.shape[0], W.shape[2]), x.dtype)
            for s in range(basis.shape[1]):
                msg = msg + basis[:, s, None] * z[src, wi[:, s]]
            agg = jax.ops.segment_sum(msg, dst, num_segments=n)
            cnt = jax.ops.segment_sum(jnp.ones((dst.shape[0],), x.dtype), dst, num_segments=n)
            agg = agg / jnp.clip(cnt, 1.0)[:, None]
            return agg + x @ R + b

        def _bn(x, g, be):
            mu = x.mean(0)
            var = x.var(0)
            return (x - mu) * jax.lax.rsqrt(var + EPS) * g + be

        def _leaky(x):
            return jnp.where(x >= 0, x, NEG * x)
        key = jax.random.key(seed)
        ks = jax.random.split(key, 32)
        inp = {'patch_embs': jax.random.normal(ks[0], (N, C), jnp.float32), 'edge_index': jax.random.randint(ks[1], (2, E), 0, N, jnp.int32), 'edge_attr': jax.random.uniform(ks[2], (E, DIM), jnp.float32)}
        i = 3
        for l in (1, 2, 3):
            inp[f'W{l}'] = jax.random.normal(ks[i], (K3, C, C), jnp.float32) * 0.05
            i += 1
            inp[f'R{l}'] = jax.random.normal(ks[i], (C, C), jnp.float32) * 0.1
            i += 1
            inp[f'b{l}'] = jnp.zeros((C,), jnp.float32)
            inp[f'g{l}'] = jnp.ones((C,), jnp.float32)
            inp[f'be{l}'] = jnp.zeros((C,), jnp.float32)
        return inp
    _L1_gnn_all = _L1_gnn_setup()
    _L1_gnn_in = {k: v for k, v in _L1_gnn_all.items() if k in ('W1', 'R1', 'b1', 'g1', 'be1', 'W2', 'R2', 'b2', 'g2', 'be2', 'W3', 'R3', 'b3', 'g3', 'be3')}
    del _L1_gnn_all
    return {'x': x, 'src': src, 'dst': dst, 'edge_attr_3': edge_attr_3, 'edge_attr_4': edge_attr_4, 'edge_attr_8': edge_attr_8, 'L0_gnn_W1': _L0_gnn_in['W1'], 'L0_gnn_b1': _L0_gnn_in['b1'], 'L0_gnn_W2': _L0_gnn_in['W2'], 'L0_gnn_b2': _L0_gnn_in['b2'], 'L0_gnn_W3': _L0_gnn_in['W3'], 'L0_gnn_b3': _L0_gnn_in['b3'], 'L0_gnn_Ws': _L0_gnn_in['Ws'], 'L0_gnn_Wv': _L0_gnn_in['Wv'], 'L1_gnn_W1': _L1_gnn_in['W1'], 'L1_gnn_R1': _L1_gnn_in['R1'], 'L1_gnn_b1': _L1_gnn_in['b1'], 'L1_gnn_g1': _L1_gnn_in['g1'], 'L1_gnn_be1': _L1_gnn_in['be1'], 'L1_gnn_W2': _L1_gnn_in['W2'], 'L1_gnn_R2': _L1_gnn_in['R2'], 'L1_gnn_b2': _L1_gnn_in['b2'], 'L1_gnn_g2': _L1_gnn_in['g2'], 'L1_gnn_be2': _L1_gnn_in['be2'], 'L1_gnn_W3': _L1_gnn_in['W3'], 'L1_gnn_R3': _L1_gnn_in['R3'], 'L1_gnn_b3': _L1_gnn_in['b3'], 'L1_gnn_g3': _L1_gnn_in['g3'], 'L1_gnn_be3': _L1_gnn_in['be3']}

def reference(x, src, dst, edge_attr_3, edge_attr_4, edge_attr_8, L0_gnn_W1, L0_gnn_b1, L0_gnn_W2, L0_gnn_b2, L0_gnn_W3, L0_gnn_b3, L0_gnn_Ws, L0_gnn_Wv, L1_gnn_W1, L1_gnn_R1, L1_gnn_b1, L1_gnn_g1, L1_gnn_be1, L1_gnn_W2, L1_gnn_R2, L1_gnn_b2, L1_gnn_g2, L1_gnn_be2, L1_gnn_W3, L1_gnn_R3, L1_gnn_b3, L1_gnn_g3, L1_gnn_be3):
    import jax
    import jax.numpy as jnp

    def _L0_gnn_ref(h, edge_index, edge_sh, edge_radial, n_atoms, W1, b1, W2, b2, W3, b3, Ws, Wv):
        import jax, jax.numpy as jnp
        import numpy as np
        N = 4096
        E = 65536
        MUL = 8
        NB = 8
        HR = 64
        NTP = 4 * MUL * MUL
        AVG_NEI = 16.0
        INV_SQRT3 = 1.0 / np.sqrt(3.0)
        ALPHA = 1.0 / np.sqrt(2.0 * MUL)
        src, dst = (edge_index[0], edge_index[1])
        x = jax.nn.silu(edge_radial @ W1 + b1)
        x = jax.nn.silu(x @ W2 + b2)
        tpw = x @ W3 + b3
        P = MUL * MUL
        W00 = tpw[:, 0 * P:1 * P].reshape(-1, MUL, MUL)
        W110 = tpw[:, 1 * P:2 * P].reshape(-1, MUL, MUL)
        W01 = tpw[:, 2 * P:3 * P].reshape(-1, MUL, MUL)
        W10 = tpw[:, 3 * P:4 * P].reshape(-1, MUL, MUL)
        hs = h[:, :MUL]
        hv = h[:, MUL:].reshape(-1, MUL, 3)
        hs_e = hs[src]
        hv_e = hv[src]
        sh0 = edge_sh[:, 0]
        sh1 = edge_sh[:, 1:4]
        m0 = ALPHA * (jnp.einsum('eu,euw->ew', hs_e * sh0[:, None], W00) + INV_SQRT3 * jnp.einsum('eui,ei,euw->ew', hv_e, sh1, W110))
        m1 = ALPHA * (jnp.einsum('eu,ei,euw->ewi', hs_e, sh1, W01) + jnp.einsum('eui,euw->ewi', hv_e * sh0[:, None, None], W10))
        messages = jnp.concatenate([m0, m1.reshape(-1, 3 * MUL)], axis=-1)
        agg = jax.ops.segment_sum(messages, dst, num_segments=n_atoms) / np.sqrt(AVG_NEI)
        self0 = hs @ Ws / np.sqrt(MUL)
        self1 = jnp.einsum('nui,uw->nwi', hv, Wv) / np.sqrt(MUL)
        h_self = jnp.concatenate([self0, self1.reshape(-1, 3 * MUL)], axis=-1)
        return h_self + agg

    def _L1_gnn_ref(patch_embs, edge_index, edge_attr, W1, R1, b1, g1, be1, W2, R2, b2, g2, be2, W3, R3, b3, g3, be3):
        import jax, jax.numpy as jnp
        import numpy as np
        N = 6250
        E = 200000
        C = 32
        KS = 4
        DIM = 3
        K3 = KS ** DIM
        NEG = 0.01
        EPS = 1e-05
        _BITS = np.array([[s >> d & 1 for d in range(DIM)] for s in range(2 ** DIM)], dtype=np.int32)

        def _basis(edge_attr):
            v = edge_attr * (KS - 1)
            lo = jnp.floor(v)
            f = v - lo
            lo = lo.astype(jnp.int32)
            bits = jnp.asarray(_BITS)
            idx = jnp.clip(lo[:, None, :] + bits[None], 0, KS - 1)
            w = jnp.where(bits[None] == 1, f[:, None, :], 1.0 - f[:, None, :])
            basis = jnp.prod(w, axis=-1)
            wi = idx[..., 0] + KS * idx[..., 1] + KS * KS * idx[..., 2]
            return (basis, wi)

        def _sconv(x, src, dst, basis, wi, W, R, b):
            n = x.shape[0]
            z = jnp.einsum('nc,kco->nko', x, W)
            msg = jnp.zeros((src.shape[0], W.shape[2]), x.dtype)
            for s in range(basis.shape[1]):
                msg = msg + basis[:, s, None] * z[src, wi[:, s]]
            agg = jax.ops.segment_sum(msg, dst, num_segments=n)
            cnt = jax.ops.segment_sum(jnp.ones((dst.shape[0],), x.dtype), dst, num_segments=n)
            agg = agg / jnp.clip(cnt, 1.0)[:, None]
            return agg + x @ R + b

        def _bn(x, g, be):
            mu = x.mean(0)
            var = x.var(0)
            return (x - mu) * jax.lax.rsqrt(var + EPS) * g + be

        def _leaky(x):
            return jnp.where(x >= 0, x, NEG * x)
        src, dst = (edge_index[0], edge_index[1])
        basis, wi = _basis(edge_attr)
        x = _bn(_leaky(_sconv(patch_embs, src, dst, basis, wi, W1, R1, b1)) + patch_embs, g1, be1)
        x = _bn(_leaky(_sconv(x, src, dst, basis, wi, W2, R2, b2)) + x, g2, be2)
        x = _bn(_sconv(x, src, dst, basis, wi, W3, R3, b3) + x, g3, be3)
        return x
    edge_index = jnp.stack([src, dst])
    x = _layernorm(x + _L0_gnn_ref(x, edge_index, edge_attr_4, edge_attr_8, 12500, L0_gnn_W1, L0_gnn_b1, L0_gnn_W2, L0_gnn_b2, L0_gnn_W3, L0_gnn_b3, L0_gnn_Ws, L0_gnn_Wv), axis=-1)
    x = _layernorm(x + _L1_gnn_ref(x, edge_index, edge_attr_3, L1_gnn_W1, L1_gnn_R1, L1_gnn_b1, L1_gnn_g1, L1_gnn_be1, L1_gnn_W2, L1_gnn_R2, L1_gnn_b2, L1_gnn_g2, L1_gnn_be2, L1_gnn_W3, L1_gnn_R3, L1_gnn_b3, L1_gnn_g3, L1_gnn_be3), axis=-1)
    return x

_drawn_inputs = setup_inputs


def setup_inputs(seed=0):
    import zlib

    import numpy as np

    out = dict(_drawn_inputs(seed))
    spreads = {'L0_gnn_b1': (0.0, 0.1),
     'L0_gnn_b2': (0.0, 0.1),
     'L0_gnn_b3': (0.0, 0.1),
     'L1_gnn_b1': (0.0, 0.329),
     'L1_gnn_g1': (1.0, 0.2),
     'L1_gnn_be1': (0.0, 0.58),
     'L1_gnn_b2': (0.0, 0.3),
     'L1_gnn_g2': (1.0, 0.2),
     'L1_gnn_be2': (0.0, 0.8),
     'L1_gnn_b3': (0.0, 0.8),
     'L1_gnn_g3': (1.0, 0.2),
     'L1_gnn_be3': (0.0, 0.1)}
    factors = {'edge_attr_3': 3.072, 'L1_gnn_W1': 5.662, 'L1_gnn_W2': 5.41, 'L1_gnn_W3': 4.405}
    for name, (base, spread) in spreads.items():
        noise = np.random.default_rng([zlib.crc32(name.encode()), seed]).standard_normal(out[name].shape)
        drawn = base * np.exp(spread * noise) if base else spread * noise
        out[name] = jnp.asarray(drawn.astype(out[name].dtype))
    for name, factor in factors.items():
        out[name] = (out[name] * factor).astype(out[name].dtype)
    return out
```

```python
from contextlib import ExitStack

import concourse.bass as bass
import numpy as np
from concourse import mybir

P = 128
CH = 32
J = 16
GROUP = 4
NG = J // GROUP
TAPS = 64
HID = 64
MUL = 8
ROW = J * CH
STEP = 32
QUART = 8
NEG = 0.01
EPS = 1e-5
BANK = 512


def sizes(nodes, edges):
    tiles = edges // P
    windows = -(-nodes // J)
    items = tiles + windows
    steps = -(-items // STEP)
    item_blocks = -(-steps * STEP // P)
    node_blocks = -(-windows // P)
    return tiles, windows, items, steps, item_blocks, node_blocks


def graph_kernel(nc, nodes, edges, a, out):
    F32, I32 = mybir.dt.float32, mybir.dt.int32
    ALU, ACT, AX = mybir.AluOpType, mybir.ActivationFunctionType, mybir.AxisListType
    TILES, WINDOWS, ITEMS, STEPS, NB, WB = sizes(nodes, edges)
    SLOTS_W = WB * J
    NODE_F = WB * ROW
    ATTR = 15
    META = 9
    LAYERS = 3
    ds = bass.ds

    def dram(name, shape, dt):
        return nc.dram_tensor(name, shape, dt, kind="Internal").ap()

    src_items = dram("src_items", [P, NB * P], I32)
    meta_items = dram("meta_items", [P, NB * 4, META, STEP], F32)
    rad_items = dram("rad_items", [NB * P, MUL * P], F32)
    window_items = dram("window_items", [1 + NB * P], F32)
    carry_items = dram("carry_items", [NB * P], F32)
    agg_rows = dram("agg_rows", [STEPS * STEP, ROW], F32)
    cnt_rows = dram("cnt_rows", [STEPS * STEP, ROW], F32)
    x_rows = dram("x_rows", [WB * P * J, CH], F32)

    ctx = ExitStack()
    with ctx:
        def sb(name, shape, dt=F32):
            return ctx.enter_context(nc.sbuf_tensor(name, shape, dt))

        def sem(name):
            return ctx.enter_context(nc.semaphore(name))

        def sems(name, n):
            return [sem(f"{name}{i}") for i in range(n)]

        ident = sb("ident", [P, P])
        ones = sb("ones", [P, P])
        tap_ids = sb("tap_ids", [P, 4])
        item_ids = sb("item_ids", [P, NB])
        window_ids = sb("window_ids", [P, WB])
        node_mask = sb("node_mask", [P, J])
        w1 = sb("w1", [P, 8, P])
        w2 = sb("w2", [P, 2, HID])
        w3 = sb("w3", [HID + 1, 256])
        w3_scale = sb("w3_scale", [HID + 1, 256])
        b1 = sb("b1", [P, 1])
        b2 = sb("b2", [HID, 1])
        spread = sb("spread", [P, GROUP, J])
        w_self = sb("w_self", [P, P])
        w_root = sb("w_root", [P, LAYERS, P])
        chan = sb("chan", [P, LAYERS, 3, CH])
        w_taps = sb("w_taps", [P, TAPS, P])

        tile_of = sb("tile_of", [P, NB])
        window4 = sb("window4", [P, NB])
        tile_idx = sb("tile_idx", [P, NB], I32)
        last_f = sb("last_f", [P, WB])
        last_idx = sb("last_idx", [P, WB], I32)
        tile_col = sb("tile_col", [P, 1], I32)
        w4_col = sb("w4_col", [P, 1])
        win_now = sb("win_now", [NB, P])
        win_before = sb("win_before", [NB, P])
        goes_on = sb("goes_on", [NB, P])
        minus = sb("minus", [1, 1])

        idx = sb("idx", [P, STEP], I32)
        meta = sb("meta", [P, META, STEP])
        carry = sb("carry", [P, STEP])
        xg = sb("xg", [P, STEP, CH])
        group_hot = sb("group_hot", [P, STEP, NG])
        place_hot = sb("place_hot", [P, STEP, GROUP])
        onehot = sb("onehot", [P, STEP, CH])
        hat = sb("hat", [P, STEP, 3, 4])
        hat2 = sb("hat2", [P, STEP, 3, 4])
        b01 = sb("b01", [P, STEP, 16])
        b01_group = sb("b01_group", [P, STEP, NG, 16])
        R = sb("R", [P, 2, STEP * NG])
        last = sb("last", [P, 2, NG])
        rts = sb("rts", [P, 2, P])

        xw = sb("xw", [P, WB, ROW])
        x1 = sb("x1", [P, WB, ROW])
        rcnt = sb("rcnt", [P, SLOTS_W])
        stat = sb("stat", [P, 4, SLOTS_W])
        bn = sb("bn", [P, 6, CH])
        xt = sb("xt", [P, 2, BANK])

        S_F = STEP * NG * TAPS
        XM_F = 16 * NG * TAPS
        BIG = max(3 * TILES, 2 * S_F + XM_F + 16 * P, 3 * NODE_F, (ATTR + 9 + 2 * META) * P)
        big = sb("big", [P, BIG])
        last_dst = big[:, 0:TILES].bitcast(I32)
        last_window = big[:, TILES:2 * TILES]
        tile_end = big[:, 2 * TILES:3 * TILES]
        src_r = big[:, 0:P].bitcast(I32)
        dst_r = big[:, P:2 * P].bitcast(I32)
        attr_r = big[:, 2 * P:(2 + ATTR) * P]
        at = 2 + ATTR
        src_f = big[:, at * P:(at + 1) * P]
        slot_i = big[:, (at + 1) * P:(at + 3) * P].bitcast(I32)
        table_f = big[:, (at + 3) * P:(at + 8) * P]
        src_t = big[:, (at + 8) * P:(at + 9) * P].bitcast(I32)
        meta_flat = big[:, (at + 9) * P:(at + 9 + META) * P]
        meta_t = meta_flat.rearrange("p (n c i) -> p n c i", n=4, c=META)
        def part(at, shape):
            n = int(np.prod(shape))
            flat = big[:, at:at + n]
            if len(shape) == 1:
                return flat, at + n
            names = "abcde"[:len(shape)]
            return flat.rearrange(f"p ({' '.join(names)}) -> p {' '.join(names)}", **dict(zip(names, shape))), at + n

        prod, at = part(0, (2, 2, ROW))
        feat, at = part(at, (STEP, 64))
        dots, at = part(at, (QUART, 24))
        h1_s, at = part(at, (BANK,))
        h2_s, at = part(at, (2, 2, BANK))
        rad, at = part(at, (2, P))
        sums, at = part(at, (STEP // 4, CH))
        S, at = part(0, (2, STEP, 4, NG, 16))
        bm, at = part(at, (16, 4, NG, 16))
        xm, at = part(at, (16, GROUP, CH))
        agg, at = part(0, (WB, ROW))
        y, at = part(at, (WB, ROW))
        sq, at = part(at, (WB, ROW))

        ps = ctx.enter_context(nc.psum_tensor("ps", [P, 8, BANK], F32))

        loaded, w_loaded, x0_loaded = sem("loaded"), sem("w_loaded"), sem("x0_loaded")
        dve_step = sem("dve_step")
        gathers_go, loads_go = sem("gathers_go"), sem("loads_go")
        count_ready = sem("count_ready")
        win_stored, win_loaded, goes_ready, goes_stored = (sem("win_stored"), sem("win_loaded"),
                                                           sem("goes_ready"), sem("goes_stored"))
        minus_ready = sem("minus_ready")
        col_ready, src_in, dst_in, attr_in = sem("col_ready"), sem("src_in"), sem("dst_in"), sem("attr_in")
        rows_ready, item_tr, item_out = sem("rows_ready"), sem("item_tr"), sem("item_out")
        meta_stored, src_stored, rad_stored = sem("meta_stored"), sem("src_stored"), sem("rad_stored")
        idx_loaded, x_in = sems("idx_loaded", 2), sems("x_in", 4)
        meta_loaded, carry_loaded, rad_loaded = sem("meta_loaded"), sem("carry_loaded"), sem("rad_loaded")
        meta_used = sem("meta_used")
        onehot_ready, feat_ready = sem("onehot_ready"), sems("feat_ready", 4)
        h1_ready, h1_act, h2_ready, h2_act = sem("h1_ready"), sem("h1_act"), sem("h2_ready"), sem("h2_act")
        tpw_ready, prod_ready, q_done, q_out = (sems("tpw_ready", 2), sems("prod_ready", 2),
                                                sems("q_done", 2), sems("q_out", 2))
        deg_done, w3_ready = sem("deg_done"), sem("w3_ready")
        bm_ready, xm_ready, s_done, s_out = (sems("bm_ready", 8), sems("xm_ready", 8),
                                             sems("s_done", 4), sems("s_out", 4))
        part_ready, R_ready, rt_ready, rt_out = sem("part_ready"), sem("R_ready"), sem("rt_ready"), sem("rt_out")
        rows_stored = sem("rows_stored")
        agg_in, cnt_in = sem("agg_in"), sem("cnt_in")
        nt_ready, nt_out = sems("nt_ready", 2), sems("nt_out", 2)
        nx_ready, nx_used = sems("nx_ready", 2), sems("nx_used", 2)
        sum_ready, sum_done, root_in, root_out = sem("sum_ready"), sem("sum_done"), sem("root_in"), sem("root_out")
        x_ready, x_stored, out_ready, out_stored = (sem("x_ready"), sem("x_stored"), sem("out_ready"),
                                                    sem("out_stored"))

        consts = [(ident, "ident"), (ones, "ones"), (tap_ids, "tap_ids"), (item_ids, "item_ids"),
                  (window_ids, "window_ids"), (node_mask, "node_mask"), (w1, "w1"), (w2, "w2"), (w3, "w3"),
                  (w3_scale, "w3_scale"), (b1, "b1"), (b2, "b2"), (spread, "spread"), (w_self, "w_self"),
                  (w_root, "w_root")]
        LOADS = 16 * (len(consts) + 3)
        ROWS0 = 2 * 16 * STEPS
        PAIRS_END = 2 + 2 * ((STEPS - 2) // 2)

        def uses(parity, phase):
            return phase * ((WB + 1) // 2 if parity == 0 else WB // 2)

        def due(value):
            return not isinstance(value, int) or value > 0

        block = ctx.enter_context(nc.Block())

        @block.sync
        def _(sp):
            for tile_, name in consts:
                sp.dma_start(tile_[:], a[name]).then_inc(loaded, 16)
            sp.dma_start(chan[:], a["chan"].to_broadcast([P, LAYERS, 3, CH])).then_inc(loaded, 16)
            sp.dma_start(last_dst, a["last_dst"].to_broadcast([P, TILES])).then_inc(loaded, 16)
            sp.dma_start(tile_end, a["tile_ids"].to_broadcast([P, TILES])).then_inc(loaded, 16)
            x_by_window = a["x"].rearrange("(b p j) c -> p b (j c)", p=P, j=J)
            sp.dma_start(xw[:], x_by_window).then_inc(x0_loaded, 16)
            sp.dma_start(w_taps[:], a["w_taps0"]).then_inc(w_loaded, 16)

            sp.wait_ge(minus_ready, 1)
            sp.dma_start(window_items[0:1].rearrange("(a b) -> a b", a=1), minus[:]).then_inc(win_stored, 16)
            sp.wait_ge(count_ready, 1)
            with nc.allow_non_contiguous_dma(reason="one column per block of items"):
                sp.dma_start(window_items[1:1 + NB * P].rearrange("(b p) -> p b", p=P),
                             tile_of[:]).then_inc(win_stored, 16)
            sp.wait_ge(win_stored, 32)
            sp.dma_start(win_before[:], window_items[0:NB * P].rearrange("(b p) -> b p", p=P)).then_inc(win_loaded, 16)
            sp.dma_start(win_now[:], window_items[1:1 + NB * P].rearrange("(b p) -> b p", p=P)).then_inc(win_loaded, 16)
            sp.wait_ge(goes_ready, 1)
            sp.dma_start(carry_items.rearrange("(b p) -> b p", p=P), goes_on[:]).then_inc(goes_stored, 16)

            def store_block(b):
                sp.wait_ge(attr_in, 16 * (b + 1))
                sp.dma_start(rad_items[ds(b * P, P), :], attr_r[:, 7 * P:15 * P]).then_inc(rad_stored, 16)
                sp.wait_ge(item_out, 4 * (b + 1))
                sp.dma_start(meta_items[:, ds(b * 4, 4), :, :].rearrange("p n c i -> p (n c i)"),
                             meta_flat).then_inc(meta_stored, 16)
                sp.dma_start(src_items[:, ds(b * P, P)], src_t).then_inc(src_stored, 16)

            store_block(0)
            with sp.Fori(1, NB) as b:
                store_block(b)
            sp.wait_ge(rad_stored, 16 * NB)
            sp.wait_ge(meta_stored, 16 * NB)
            sp.wait_ge(src_stored, 16 * NB)
            sp.wait_ge(goes_stored, 16)

            def load_indices(n, i):
                for half in range(2):
                    for q in (2 * half, 2 * half + 1):
                        if due(n):
                            sp.wait_ge(x_in[q], 16 * QUART * n)
                    sp.sem_inc(loads_go, 1)
                    sp.dma_start(idx[:, 16 * half:16 * half + 16],
                                 src_items[:, ds(i * STEP + 16 * half, 16)]).then_inc(idx_loaded[half], 16)

            def load_meta(n, i, first, end):
                if due(n):
                    sp.wait_ge(meta_used, n)
                sp.sem_inc(loads_go, 1)
                sp.dma_start(meta[:, first:end, :], meta_items[:, ds(i, 1), first:end, :]
                             .rearrange("p n c i -> p (n c) i")).then_inc(meta_loaded, 16)

            def load_carry(n, i):
                if due(n):
                    sp.wait_ge(R_ready, n)
                sp.sem_inc(loads_go, 1)
                sp.dma_start(carry[:], carry_items[ds(i * STEP, STEP)].rearrange("(o i) -> o i", o=1)
                             .to_broadcast([P, STEP])).then_inc(carry_loaded, 16)

            def l0_loads(i):
                load_meta(i, i, 3, META)
                if due(i):
                    sp.wait_ge(h1_ready, 4 * i)
                sp.sem_inc(loads_go, 1)
                sp.dma_start(rad, rad_items[ds(i * STEP, STEP), :].rearrange("(t n) (k f) -> (n k) t f", t=2, k=MUL)
                             ).then_inc(rad_loaded, 16)
                load_indices(i, i)

            l0_loads(0)
            with sp.Fori(1, STEPS) as i:
                l0_loads(i)
                load_carry(i - 1, i - 1)
            load_carry(STEPS - 1, STEPS - 1)
            sp.wait_ge(x_ready, 1)
            sp.dma_start(x_rows.rearrange("(b p j) c -> p b (j c)", p=P, j=J), xw[:]).then_inc(x_stored, 16)
            for l in range(LAYERS):
                base = (l + 1) * STEPS
                if l:
                    sp.wait_ge(part_ready, base)
                    sp.dma_start(w_taps[:], a[f"w_taps{l}"]).then_inc(w_loaded, 16)
                    sp.wait_ge(x_ready, l + 1)
                    sp.dma_start(x_rows.rearrange("(b p j) c -> p b (j c)", p=P, j=J), xw[:]).then_inc(x_stored, 16)
                for i in range(2):
                    load_meta(base + i, i, 0, 5)
                    load_indices(base + i, i)
                with sp.Fori(2, STEPS) as i:
                    load_meta(base + i, i, 0, 5)
                    load_indices(base + i, i)
                    load_carry(base + i - 2, i - 2)
                for i in (STEPS - 2, STEPS - 1):
                    load_carry(base + i, i)
            sp.wait_ge(out_ready, 1)
            sp.dma_start(out.rearrange("(b p j) c -> p b (j c)", p=P, j=J), xw[:]).then_inc(out_stored, 16)
            sp.wait_ge(out_stored, 16)

        @block.gpsimd
        def _(pool):
            def gather(dst_tile, table, index):
                return nc.gpsimd.indirect_dma_start(
                    out=dst_tile, out_offset=None, in_=table,
                    in_offset=bass.IndirectOffsetOnAxis(ap=index, axis=0))

            def gather_block(b):
                pool.wait_ge(col_ready, b + 1)
                if due(b):
                    pool.wait_ge(item_tr, b)
                    pool.wait_ge(rad_stored, 16 * b)
                pool.sem_inc(gathers_go, 1)
                gather(src_r, a["src"], tile_col[:]).then_inc(src_in, 16)
                gather(dst_r, a["dst"], tile_col[:]).then_inc(dst_in, 16)
                gather(attr_r, a["attr"], tile_col[:]).then_inc(attr_in, 16)

            gather_block(0)
            with pool.Fori(1, NB) as b:
                gather_block(b)

            def gather_sources(table, n, group_free):
                for q in range(4):
                    if q % 2 == 0:
                        pool.wait_ge(idx_loaded[q // 2], 16 * (n + 1))
                    group_free(q)
                    pool.sem_inc(gathers_go, 1)
                    for r in range(QUART):
                        s = QUART * q + r
                        gather(xg[:, s, :], table, idx[:, s:s + 1]).then_inc(x_in[q], 16)

            def window_totals(table, into, done):
                for b in range(WB):
                    gather(into[:, b, :], table, last_idx[:, b:b + 1]).then_inc(done, 16)

            gather_sources(a["x"], 0, lambda q: None)
            with pool.Fori(1, STEPS) as i:
                gather_sources(a["x"], i, lambda q: pool.wait_ge(feat_ready[q], i))
            pool.wait_ge(rows_stored, ROWS0)
            pool.wait_ge(part_ready, STEPS)
            window_totals(agg_rows, agg, agg_in)
            window_totals(cnt_rows, sq, cnt_in)
            for l in range(LAYERS):
                pool.wait_ge(x_stored, 16 * (l + 1))
                gather_sources(x_rows, (l + 1) * STEPS, lambda q: pool.wait_ge(xm_ready[2 * q + 1], l * STEPS) if l else None)
                with pool.Fori(1, STEPS) as i:
                    gather_sources(x_rows, (l + 1) * STEPS + i,
                                   lambda q: pool.wait_ge(xm_ready[2 * q + 1], l * STEPS + i))
                pool.wait_ge(rows_stored, ROWS0 + 16 * STEPS * (l + 1))
                pool.wait_ge(part_ready, (l + 2) * STEPS)
                window_totals(agg_rows, agg, agg_in)

        @block.scalar
        def _(act):
            act.wait_ge(loaded, LOADS)
            def copy_block(b):
                act.wait_ge(item_tr, b + 1)
                if due(b):
                    act.wait_ge(meta_stored, 16 * b)
                    act.wait_ge(src_stored, 16 * b)
                nc.scalar.copy(meta_t[:, :, 0:4, :].rearrange("p n c i -> p c n i"),
                               ps[:, 0, :].rearrange("p (c n i) -> p c n i", c=4, n=4)).then_inc(item_out, 1)
                nc.scalar.copy(meta_t[:, :, 4:8, :].rearrange("p n c i -> p c n i"),
                               ps[:, 1, :].rearrange("p (c n i) -> p c n i", c=4, n=4)).then_inc(item_out, 1)
                nc.scalar.copy(meta_t[:, :, 8, :], ps[:, 2, 0:P].rearrange("p (n i) -> p n i", n=4)
                               ).then_inc(item_out, 1)
                nc.scalar.copy(src_t, ps[:, 2, P:2 * P]).then_inc(item_out, 1)

            copy_block(0)
            with act.Fori(1, NB) as b:
                copy_block(b)

            def store_rows(n, kinds, bank, col, stored):
                act.wait_ge(rt_ready, n + 1)
                if due(stored):
                    act.wait_ge(rows_stored, stored)
                nc.scalar.copy(rts[:, 0:kinds, :], ps[:, bank, col:col + kinds * P].rearrange("p (k f) -> p k f", k=kinds)
                               ).then_inc(rt_out, 1)
                act.wait_ge(rt_out, n + 1)

            def rows_at(table, i):
                return table[ds(i * STEP, STEP), :].rearrange("i (g f) -> (i g) f", g=NG)

            def l0_step(i):
                def first_layer(f):
                    act.wait_ge(h1_ready, 4 * i + f + 1)
                    if due(8 * i + 2 * f):
                        act.wait_ge(h2_ready, 8 * i + 2 * f)
                    nc.scalar.activation(h1_s, ps[:, 0, :], ACT.Silu, bias=b1[:, 0:1]).then_inc(h1_act, 1)

                def second_layer(f):
                    for h in range(2):
                        act.wait_ge(h2_ready, 8 * i + 2 * f + h + 1)
                        if due(8 * i + 2 * f - 2):
                            act.wait_ge(tpw_ready[1], 8 * i + 2 * f - 2)
                        nc.scalar.activation(h2_s[0:HID, f % 2, h, :], ps[0:HID, (1, 6)[h], :], ACT.Silu,
                                             bias=b2[:, 0:1]).then_inc(h2_act, 1)

                first_layer(0)
                second_layer(0)
                first_layer(1)
                for q in range(16):
                    f = q // 4
                    if q % 4 == 1 and f + 1 < 4:
                        second_layer(f + 1)
                    if q % 4 == 2 and f + 2 < 4:
                        first_layer(f + 2)

            def l0_rows(i):
                store_rows(i, 2, 7, 256, 32 * i)
                act.dma_start(rows_at(agg_rows, i), rts[:, 0, :]).then_inc(rows_stored, 16)
                act.dma_start(rows_at(cnt_rows, i), rts[:, 1, :]).then_inc(rows_stored, 16)

            l0_step(0)
            l0_step(1)
            l0_rows(0)
            with act.Fori(2, STEPS) as i:
                l0_step(i)
                l0_rows(i - 1)
            l0_rows(STEPS - 1)

            roots = [0]

            def square_root(col):
                roots[0] += 1
                act.wait_ge(root_in, roots[0])
                nc.scalar.activation(col, col, ACT.Sqrt).then_inc(root_out, 1)

            def node_copies(phase):
                for b in range(WB):
                    par = b % 2
                    done = uses(par, phase) + b // 2
                    act.wait_ge(nt_ready[par], done + 1)
                    if due(done):
                        act.wait_ge(nx_ready[par], done)
                    nc.scalar.copy(xt[:, par, :], ps[:, par, :]).then_inc(nt_out[par], 1)

            node_copies(0)
            square_root(stat[:, 1, :])

            def l1_step(l, i, par):
                for e in range(16):
                    bank = e % 4
                    if e == 0:
                        act.wait_ge(part_ready, (l + 1) * STEPS + i - 1)
                    act.wait_ge(s_done[bank], 4 * (l * STEPS + i) + e // 4 + 1)
                    nc.scalar.copy(S[:, par, 2 * e:2 * e + 2].rearrange("p n c g a -> p (n c g a)"), ps[:, bank, :]
                                   ).then_inc(s_out[bank], 1)

            def l1_rows(l, i):
                n = (l + 1) * STEPS + i
                store_rows(n, 1, 6, 0, ROWS0 + 16 * (n - STEPS))
                act.dma_start(rows_at(agg_rows, i), rts[:, 0, :]).then_inc(rows_stored, 16)

            for l in range(LAYERS):
                l1_step(l, 0, 0)
                l1_step(l, 1, 1)
                with act.Fori(2, PAIRS_END, 2) as i:
                    for par in range(2):
                        l1_step(l, i + par, par)
                        l1_rows(l, i + par - 2)
                for i in range(PAIRS_END, STEPS):
                    l1_step(l, i, i % 2)
                    l1_rows(l, i - 2)
                for i in (STEPS - 2, STEPS - 1):
                    l1_rows(l, i)
                node_copies(l + 1)
                square_root(bn[:, 2, :])
            square_root(stat[:, 1, :])

        @block.vector
        def _(dve):
            v = nc.vector
            steps = [0]

            def link(ins):
                steps[0] += 1
                ins.then_inc(dve_step, 1)
                dve.wait_ge(dve_step, steps[0])

            dve.wait_ge(loaded, LOADS)
            v.memset(minus[:], -1.0).then_inc(minus_ready, 1)
            link(v.memset(last[:], 0.0))
            v.tensor_tensor(w3[:], w3[:], w3_scale[:], ALU.mult).then_inc(w3_ready, 1)
            link(v.memset(onehot[:], 0.0))
            last_win_i = last_window.bitcast(I32)
            link(v.tensor_scalar(last_win_i, last_dst, J.bit_length() - 1, None, ALU.arith_shift_right))
            link(v.tensor_copy(last_dst.bitcast(F32), last_win_i))
            link(v.tensor_tensor(tile_end, tile_end, last_dst.bitcast(F32), ALU.add))
            ended = last_dst.bitcast(F32)
            for b in range(NB):
                v.tensor_scalar(out=last_window, in0=tile_end, scalar1=item_ids[:, b:b + 1], scalar2=0.0,
                                op0=ALU.is_lt, op1=ALU.add, accum_out=tile_of[:, b:b + 1]).then_inc(dve_step, 1)
                steps[0] += 1
                dve.wait_ge(dve_step, steps[0])
            for b in range(WB):
                link(v.tensor_scalar(out=last_window, in0=ended, scalar1=window_ids[:, b:b + 1], scalar2=0.0,
                                     op0=ALU.is_le, op1=ALU.add, accum_out=last_f[:, b:b + 1]))
            link(v.tensor_tensor(last_f[:], last_f[:], window_ids[:], ALU.add))
            link(v.tensor_scalar(last_idx[:], last_f[:], float(ITEMS - 1), None, ALU.min))
            link(v.tensor_scalar(tile_idx[:], tile_of[:], float(TILES - 1), None, ALU.min))
            link(v.tensor_scalar(window4[:], tile_of[:], float(TILES), float(1 << 20), ALU.is_ge, ALU.mult))
            link(v.tensor_tensor(tile_of[:], item_ids[:], tile_of[:], ALU.subtract))
            v.scalar_tensor_tensor(window4[:], tile_of[:], float(NG), window4[:], ALU.mult,
                                   ALU.add).then_inc(count_ready, 1)
            dve.wait_ge(win_loaded, 32)
            v.tensor_tensor(goes_on[:], win_now[:], win_before[:], ALU.is_equal).then_inc(goes_ready, 1)
            dve.wait_ge(count_ready, 1)

            base = steps[0]
            LINKS = 6

            def table_block(b):
                if due(b):
                    dve.wait_ge(attr_in, 16 * b)
                v.tensor_copy(w4_col[:], window4[:, ds(b, 1)]).then_inc(dve_step, 1)
                v.tensor_copy(tile_col[:], tile_idx[:, ds(b, 1)]).then_inc(col_ready, 1)
                dve.wait_ge(src_in, 16 * (b + 1))
                dve.wait_ge(dst_in, 16 * (b + 1))
                dve.wait_ge(attr_in, 16 * (b + 1))
                if due(b):
                    dve.wait_ge(item_tr, b)
                v.tensor_copy(src_f, src_r).then_inc(dve_step, 1)
                v.tensor_scalar(slot_i[:, 0:P], dst_r, NG.bit_length() - 1, None, ALU.arith_shift_right
                                ).then_inc(dve_step, 1)
                v.tensor_scalar(slot_i[:, P:2 * P], dst_r, NG - 1, None, ALU.bitwise_and).then_inc(dve_step, 1)
                v.tensor_scalar(table_f[:, 0:3 * P], attr_r[:, 0:3 * P], 3.0, 0.0, ALU.mult, ALU.max
                                ).then_inc(dve_step, 1)
                dve.wait_ge(dve_step, base + b * LINKS + 5)
                v.tensor_scalar(table_f[:, 3 * P:4 * P], slot_i[:, 0:P], w4_col[:, 0:1], None, ALU.subtract
                                ).then_inc(rows_ready, 1)
                v.tensor_copy(table_f[:, 4 * P:5 * P], slot_i[:, P:2 * P]).then_inc(rows_ready, 1)
                v.tensor_scalar(table_f[:, 0:3 * P], table_f[:, 0:3 * P], 3.0, None, ALU.min).then_inc(dve_step, 1)
                dve.wait_ge(dve_step, base + b * LINKS + 6)
                v.nop().then_inc(rows_ready, 1)

            table_block(0)
            with dve.Fori(1, NB) as b:
                table_block(b)
            steps[0] += LINKS * NB

            def scan(n, kinds):
                dve.wait_ge(part_ready, n + 1)
                dve.wait_ge(carry_loaded, 16 * (n + 1))
                if due(n):
                    dve.wait_ge(rt_ready, n)
                for kind in range(kinds):
                    part = ps[:, 7, kind * P:kind * P + P].rearrange("p (i g) -> p g i", g=NG)
                    to = R[:, kind, :].rearrange("p (i g) -> p g i", g=NG)
                    for g in range(NG):
                        v.tensor_tensor_scan(to[:, g, :], carry[:], part[:, g, :], last[:, kind, g:g + 1],
                                             ALU.mult, ALU.add).then_inc(dve_step, 1)

            def keep_last(kinds):
                return v.tensor_copy(last[:, 0:kinds, :], R[:, 0:kinds, (STEP - 1) * NG:STEP * NG])

            def slot_masks():
                v.tensor_tensor(group_hot[:], meta[:, 3, :].unsqueeze(2).to_broadcast([P, STEP, NG]),
                                tap_ids[:].unsqueeze(1).to_broadcast([P, STEP, NG]), ALU.is_equal).then_inc(dve_step, 1)
                v.tensor_tensor(place_hot[:], meta[:, 4, :].unsqueeze(2).to_broadcast([P, STEP, GROUP]),
                                tap_ids[:].unsqueeze(1).to_broadcast([P, STEP, GROUP]), ALU.is_equal
                                ).then_inc(dve_step, 1)

            dve.wait_ge(meta_loaded, 16)
            v.memset(h2_s[HID:HID + 1], 1.0).then_inc(w3_ready, 1)
            base0 = steps[0]
            MASKS = 2
            G0 = 4
            SCAN0 = 2 * NG + 1

            def l0_step(i, prior, with_scan):
                dve.wait_ge(meta_loaded, 16 * (i + 1))
                slot_masks()
                dve.wait_ge(dve_step, prior + MASKS)
                if due(i):
                    dve.wait_ge(deg_done, i)
                v.tensor_tensor(onehot[:, :, 0:J].rearrange("p n (g j) -> p n g j", g=NG),
                                group_hot[:].unsqueeze(3).to_broadcast([P, STEP, NG, GROUP]),
                                place_hot[:].unsqueeze(2).to_broadcast([P, STEP, NG, GROUP]), ALU.mult
                                ).then_inc(onehot_ready, 1)
                at = prior + MASKS

                def sum_inputs(e):
                    dve.wait_ge(q_done[1], 8 * i + e + 1)
                    if e == 0 and due(i):
                        dve.wait_ge(part_ready, i)
                    four = ps[:, 4 + e % 2, :].rearrange("p (s u w) -> p s w u", s=4, u=16)
                    v.tensor_reduce(sums[:, e, 0:MUL], four[:, 0], AX.X, ALU.add).then_inc(q_out[e % 2], 1)
                    v.tensor_reduce(sums[:, e, MUL:CH].rearrange("p (w s) -> p s w", s=3), four[:, 1:4], AX.X,
                                    ALU.add).then_inc(q_out[e % 2], 1)

                for q4 in range(4):
                    its = slice(QUART * q4, QUART * q4 + QUART)
                    dve.wait_ge(x_in[q4], 16 * QUART * (i + 1))
                    hs = xg[:, its, 0:MUL]
                    hv = xg[:, its, MUL:CH].rearrange("p n (u i) -> p n i u", i=3)
                    sh0 = meta[:, 5, its]
                    sh1 = meta[:, 6:9, its].rearrange("p i n -> p n i")
                    f_s = feat[:, its, :].rearrange("p n (s u) -> p n s u", s=4)
                    dot = dots.rearrange("p n (i u) -> p n i u", i=3)
                    v.tensor_tensor(f_s[:, :, 0, 0:MUL], hs, sh0.unsqueeze(2).to_broadcast([P, QUART, MUL]),
                                    ALU.mult).then_inc(dve_step, 1)
                    v.tensor_tensor(f_s[:, :, 1:4, MUL:2 * MUL], hv,
                                    sh0.unsqueeze(2).unsqueeze(3).to_broadcast([P, QUART, 3, MUL]),
                                    ALU.mult).then_inc(dve_step, 1)
                    v.tensor_tensor(f_s[:, :, 1:4, 0:MUL], hs.unsqueeze(2).to_broadcast([P, QUART, 3, MUL]),
                                    sh1.unsqueeze(3).to_broadcast([P, QUART, 3, MUL]), ALU.mult).then_inc(dve_step, 1)
                    v.tensor_tensor(dot, hv, sh1.unsqueeze(3).to_broadcast([P, QUART, 3, MUL]),
                                    ALU.mult).then_inc(dve_step, 1)
                    at = at + G0
                    dve.wait_ge(dve_step, at)
                    v.tensor_reduce(f_s[:, :, 0, MUL:2 * MUL], dot.rearrange("p n i u -> p n u i"), AX.X,
                                    ALU.add).then_inc(feat_ready[q4], 1)
                    dve.wait_ge(feat_ready[q4], i + 1)
                    if q4 == 3:
                        v.nop().then_inc(meta_used, 1)
                    for q in range(4 * q4, 4 * q4 + 4):
                        par = q % 2
                        dve.wait_ge(tpw_ready[par], 8 * i + q // 2 + 1)
                        if due(8 * i + q // 2):
                            dve.wait_ge(q_done[par], 8 * i + q // 2)
                        for h in range(2):
                            n = 2 * q + h
                            tpw = ps[:, 2 + par, 256 * h:256 * h + 256].rearrange("p (s u w) -> p s u w", s=2, u=16)
                            fn = feat[:, n, :].rearrange("p (s u) -> p s u", s=4)
                            pr = prod[:, par, h, :].rearrange("p (s u w) -> p s u w", s=4, u=16)
                            v.tensor_tensor(pr[:, 0], tpw[:, 0], fn[:, 0].unsqueeze(2).to_broadcast([P, 16, MUL]),
                                            ALU.mult).then_inc(prod_ready[par], 1)
                            v.tensor_tensor(pr[:, 1:4], tpw[:, 1].unsqueeze(1).to_broadcast([P, 3, 16, MUL]),
                                            fn[:, 1:4].unsqueeze(3).to_broadcast([P, 3, 16, MUL]),
                                            ALU.mult).then_inc(prod_ready[par], 1)
                        if q >= 3 and q % 2:
                            sum_inputs(q // 2 - 1)
                    if q4 == 1 and with_scan:
                        scan(i - 1, 2)
                        dve.wait_ge(dve_step, at + 2 * NG)
                        keep_last(2).then_inc(dve_step, 1)
                        at = at + SCAN0
                        dve.wait_ge(dve_step, at)
                        v.nop().then_inc(R_ready, 1)
                sum_inputs(7)

            l0_step(0, base0, False)
            l0_step(1, base0 + MASKS + 4 * G0, True)
            per0 = MASKS + 4 * G0 + SCAN0
            with dve.Fori(2, STEPS) as i:
                l0_step(i, i * per0 + (base0 - SCAN0), True)
            steps[0] = base0 - SCAN0 + STEPS * per0
            scan(STEPS - 1, 2)
            steps[0] += 2 * NG
            dve.wait_ge(dve_step, steps[0])
            link(keep_last(2))
            v.nop().then_inc(R_ready, 1)

            nodes_of = lambda ap: ap.rearrange("p b (j c) -> p (b j) c", c=CH)
            rooted = [0]

            def square_root(last_ins):
                last_ins.then_inc(root_in, 1)
                rooted[0] += 1
                dve.wait_ge(root_out, rooted[0])

            def per_node(col):
                return col.unsqueeze(2).to_broadcast([P, SLOTS_W, CH])

            def per_channel(row):
                return row.unsqueeze(1).to_broadcast([P, SLOTS_W, CH])

            def layer_norm(to):
                yn, qn = nodes_of(y), nodes_of(sq)
                link(v.tensor_reduce(stat[:, 0, :], yn, AX.X, ALU.add))
                link(v.tensor_scalar(stat[:, 0, :], stat[:, 0, :], 1.0 / CH, None, ALU.mult))
                link(v.tensor_tensor(yn, yn, per_node(stat[:, 0, :]), ALU.subtract))
                link(v.tensor_tensor(qn, yn, yn, ALU.mult))
                link(v.tensor_reduce(stat[:, 1, :], qn, AX.X, ALU.add))
                square_root(v.tensor_scalar(stat[:, 1, :], stat[:, 1, :], 1.0 / CH, EPS, ALU.mult, ALU.add))
                link(v.reciprocal(stat[:, 2, :], stat[:, 1, :]))
                return v.tensor_tensor(nodes_of(to), yn, per_node(stat[:, 2, :]), ALU.mult)

            dve.wait_ge(agg_in, 16 * WB)
            dve.wait_ge(cnt_in, 16 * WB)
            cnt = nodes_of(sq)[:, :, 0]
            link(v.tensor_scalar(rcnt[:], cnt, 1.0, None, ALU.max))
            link(v.reciprocal(rcnt[:], rcnt[:]))
            for b in range(WB):
                par = b % 2
                dve.wait_ge(nx_ready[par], uses(par, 0) + b // 2 + 1)
                v.scalar_tensor_tensor(y[:, b, :], ps[:, 2 + par, :], MUL ** -0.5, xw[:, b, :], ALU.mult,
                                       ALU.add).then_inc(nx_used[par], 1)
                dve.wait_ge(nx_used[par], uses(par, 0) + b // 2 + 1)
                link(v.tensor_tensor(y[:, b, :], y[:, b, :], agg[:, b, :], ALU.add))
            link(layer_norm(x1))
            link(v.tensor_copy(xw[:], x1[:]))
            v.nop().then_inc(x_ready, 1)

            LINKS1 = 7
            SCAN1 = NG + 1

            def l1_step(l, i, prior, with_scan):
                n = (l + 1) * STEPS + i
                n1 = l * STEPS + i
                dve.wait_ge(meta_loaded, 16 * (n + 1))
                if due(n1):
                    for ch in range(8):
                        dve.wait_ge(bm_ready[ch], n1)
                        dve.wait_ge(xm_ready[ch], n1)
                slot_masks()
                coords = meta[:, 0:3, :].rearrange("p d n -> p n d")
                v.tensor_tensor(hat[:], coords.unsqueeze(3).to_broadcast([P, STEP, 3, 4]),
                                tap_ids[:].unsqueeze(1).unsqueeze(1).to_broadcast([P, STEP, 3, 4]),
                                ALU.subtract).then_inc(meta_used, 1)
                dve.wait_ge(meta_used, n + 1)
                v.scalar_tensor_tensor(hat2[:], hat[:], -1.0, hat[:], ALU.mult, ALU.max).then_inc(dve_step, 1)
                dve.wait_ge(dve_step, prior + 3)
                v.tensor_scalar(hat2[:], hat2[:], -1.0, 1.0, ALU.mult, ALU.add).then_inc(dve_step, 1)
                dve.wait_ge(dve_step, prior + 4)
                v.tensor_scalar(hat[:], hat2[:], 0.0, None, ALU.max).then_inc(dve_step, 1)
                dve.wait_ge(dve_step, prior + 5)
                v.tensor_tensor(b01[:].rearrange("p n (b a) -> p n b a", a=4),
                                hat[:, :, 1, :].unsqueeze(3).to_broadcast([P, STEP, 4, 4]),
                                hat[:, :, 0, :].unsqueeze(2).to_broadcast([P, STEP, 4, 4]),
                                ALU.mult).then_inc(dve_step, 1)
                dve.wait_ge(dve_step, prior + 6)
                v.tensor_tensor(b01_group[:], b01[:].unsqueeze(2).to_broadcast([P, STEP, NG, 16]),
                                group_hot[:].unsqueeze(3).to_broadcast([P, STEP, NG, 16]), ALU.mult
                                ).then_inc(dve_step, 1)
                dve.wait_ge(dve_step, prior + LINKS1)
                for ch in range(8):
                    its = slice(4 * ch, 4 * ch + 4)
                    ring = slice(4 * (ch % 4), 4 * (ch % 4) + 4)
                    if due(4 * n1 + 2 * (ch // 2) - 2):
                        dve.wait_ge(s_done[2 * (ch % 2) + 1], 4 * n1 + (ch - 4) // 2 + 1)
                    v.tensor_tensor(bm[:, ring].rearrange("p n c g a -> p n c (g a)"),
                                    b01_group[:, its].rearrange("p n g a -> p n (g a)").unsqueeze(2)
                                    .to_broadcast([P, 4, 4, NG * 16]),
                                    hat[:, its, 2, :].unsqueeze(3).to_broadcast([P, 4, 4, NG * 16]), ALU.mult
                                    ).then_inc(bm_ready[ch], 1)
                    dve.wait_ge(x_in[ch // 2], 16 * QUART * (n + 1))
                    v.tensor_tensor(xm[:, ring], xg[:, its, :].unsqueeze(2).to_broadcast([P, 4, GROUP, CH]),
                                    place_hot[:, its, :].unsqueeze(3).to_broadcast([P, 4, GROUP, CH]),
                                    ALU.mult).then_inc(xm_ready[ch], 1)
                    if ch == 4 and with_scan:
                        scan(n - 2, 1)
                        dve.wait_ge(dve_step, prior + LINKS1 + NG)
                        keep_last(1).then_inc(dve_step, 1)
                        dve.wait_ge(dve_step, prior + LINKS1 + SCAN1)
                        v.nop().then_inc(R_ready, 1)

            for l in range(LAYERS):
                base1 = steps[0]
                per1 = LINKS1 + SCAN1
                l1_step(l, 0, base1, False)
                l1_step(l, 1, base1 + LINKS1, False)
                with dve.Fori(2, STEPS) as i:
                    l1_step(l, i, i * per1 + (base1 - 2 * SCAN1), True)
                steps[0] = base1 + STEPS * per1 - 2 * SCAN1
                for n in ((l + 2) * STEPS - 2, (l + 2) * STEPS - 1):
                    scan(n, 1)
                    steps[0] += NG
                    dve.wait_ge(dve_step, steps[0])
                    link(keep_last(1))
                    v.nop().then_inc(R_ready, 1)

                dve.wait_ge(agg_in, 16 * WB * (l + 2))
                for b in range(WB):
                    par = b % 2
                    done = uses(par, l + 1) + b // 2
                    yb = y[:, b, :].rearrange("p (j c) -> p j c", c=CH)
                    link(v.tensor_tensor(yb, agg[:, b, :].rearrange("p (j c) -> p j c", c=CH),
                                         rcnt[:, J * b:J * b + J].unsqueeze(2).to_broadcast([P, J, CH]), ALU.mult))
                    dve.wait_ge(nx_ready[par], done + 1)
                    v.tensor_tensor(y[:, b, :], ps[:, 2 + par, :], y[:, b, :], ALU.add).then_inc(nx_used[par], 1)
                    dve.wait_ge(nx_used[par], done + 1)
                    link(v.tensor_tensor(yb, yb, chan[:, l, 0, :].unsqueeze(1).to_broadcast([P, J, CH]), ALU.add))
                    if l < LAYERS - 1:
                        link(v.scalar_tensor_tensor(y[:, b, :], y[:, b, :], NEG, y[:, b, :], ALU.mult, ALU.max))
                    link(v.tensor_tensor(y[:, b, :], y[:, b, :], xw[:, b, :], ALU.add))
                    if b == WB - 1:
                        link(v.tensor_tensor(yb, yb, node_mask[:].unsqueeze(2).to_broadcast([P, J, CH]), ALU.mult))

                yn, qn = nodes_of(y), nodes_of(sq)
                v.tensor_reduce(bn[:, 0, :], yn.rearrange("p n c -> p c n"), AX.X, ALU.add).then_inc(sum_ready, 1)
                dve.wait_ge(sum_done, 2 * l + 1)
                link(v.tensor_scalar(bn[:, 1, :], ps[:, 4, 0:CH], 1.0 / nodes, None, ALU.mult))
                link(v.tensor_tensor(yn, yn, per_channel(bn[:, 1, :]), ALU.subtract))
                yb = y[:, WB - 1, :].rearrange("p (j c) -> p j c", c=CH)
                link(v.tensor_tensor(yb, yb, node_mask[:].unsqueeze(2).to_broadcast([P, J, CH]), ALU.mult))
                link(v.tensor_tensor(qn, yn, yn, ALU.mult))
                v.tensor_reduce(bn[:, 0, :], qn.rearrange("p n c -> p c n"), AX.X, ALU.add).then_inc(sum_ready, 1)
                dve.wait_ge(sum_done, 2 * l + 2)
                square_root(v.tensor_scalar(bn[:, 2, :], ps[:, 4, 0:CH], 1.0 / nodes, EPS, ALU.mult, ALU.add))
                link(v.reciprocal(bn[:, 3, :], bn[:, 2, :]))
                link(v.tensor_tensor(bn[:, 4, :], bn[:, 3, :], chan[:, l, 1, :], ALU.mult))
                link(v.tensor_tensor(yn, yn, per_channel(bn[:, 4, :]), ALU.mult))
                if l < LAYERS - 1:
                    v.tensor_tensor(nodes_of(xw), yn, per_channel(chan[:, l, 2, :]), ALU.add).then_inc(x_ready, 1)
                    dve.wait_ge(x_ready, l + 2)
            link(v.tensor_tensor(nodes_of(y), nodes_of(y), per_channel(chan[:, LAYERS - 1, 2, :]), ALU.add))
            link(v.tensor_tensor(y, y, x1[:], ALU.add))
            layer_norm(xw).then_inc(out_ready, 1)

        @block.tensor
        def _(pe):
            pe.wait_ge(loaded, LOADS)
            def transpose_block(b):
                pe.wait_ge(rows_ready, 3 * (b + 1))
                if due(b):
                    pe.wait_ge(item_out, 4 * b)
                for c in range(5):
                    nc.tensor.transpose(ps[:, c // 4, (c % 4) * P:(c % 4) * P + P], table_f[:, c * P:c * P + P],
                                        ident[:])
                for c in range(5, META):
                    nc.tensor.transpose(ps[:, c // 4, (c % 4) * P:(c % 4) * P + P],
                                        attr_r[:, (c - 2) * P:(c - 1) * P], ident[:])
                nc.tensor.transpose(ps[:, 2, P:2 * P], src_f, ident[:]).then_inc(item_tr, 1)

            transpose_block(0)
            with pe.Fori(1, NB) as b:
                transpose_block(b)

            def transpose_totals(n, kinds, bank, col):
                pe.wait_ge(R_ready, n + 1)
                if due(n):
                    pe.wait_ge(rt_out, n)
                for kind in range(kinds):
                    tr = nc.tensor.transpose(ps[:, bank, col + kind * P:col + kind * P + P], R[:, kind, :], ident[:])
                tr.then_inc(rt_ready, 1)

            def l0_spread(n):
                for f in range(2):
                    pe.wait_ge(q_out[f], 8 * (n + 1))
                for e in range(STEP // 4):
                    for jj in range(GROUP):
                        tr = nc.tensor.matmul(ps[CH * jj:CH * jj + CH, 7, J * e:J * e + J], sums[:, e, :],
                                              spread[:, jj, :], start=True, stop=True, tile_position=(0, CH * jj))
                tr.then_inc(part_ready, 1)

            def l0_degrees(i):
                for jj in range(GROUP):
                    tr = nc.tensor.matmul(ps[CH * jj:CH * jj + CH, 7, P:2 * P], ones[:, 0:CH],
                                          onehot[:, :, jj:jj + GROUP * (NG - 1) + 1:GROUP],
                                          start=True, stop=True, tile_position=(0, CH * jj))
                tr.then_inc(deg_done, 1)

            def l0_step(i, with_totals):
                def first_layer(f):
                    if due(4 * i + f):
                        pe.wait_ge(h1_act, 4 * i + f)
                    for p in range(4):
                        q = 4 * f + p
                        tr = nc.tensor.matmul(ps[:, 0, p * P:p * P + P], w1[:, q % 8, :], rad[:, q // 8, :],
                                              start=True, stop=True)
                    tr.then_inc(h1_ready, 1)

                def second_layer(f):
                    pe.wait_ge(h1_act, 4 * i + f + 1)
                    for h in range(2):
                        if due(8 * i + 2 * f + h - 1):
                            pe.wait_ge(h2_act, 8 * i + 2 * f + h - 1)
                        nc.tensor.matmul(ps[0:HID, (1, 6)[h], :], w2[:, h, :], h1_s, start=True, stop=True
                                         ).then_inc(h2_ready, 1)

                def third_layer(q):
                    par, f, p = q % 2, q // 4, q % 4
                    pe.wait_ge(h2_act, 8 * i + 2 * f + 2)
                    if due(8 * i + q // 2):
                        pe.wait_ge(prod_ready[par], 4 * (8 * i + q // 2))
                    for h in range(2):
                        tr = nc.tensor.matmul(ps[:, 2 + par, 256 * h:256 * h + 256],
                                              h2_s[0:HID + 1, f % 2, h, p * P:p * P + P], w3[:],
                                              start=True, stop=True)
                    tr.then_inc(tpw_ready[par], 1)

                def item_sums(q):
                    par, e = q % 2, q // 2
                    if q == 0:
                        pe.wait_ge(onehot_ready, i + 1)
                    if par == 0 and due(4 * i + e // 2):
                        pe.wait_ge(q_out[e % 2], 2 * (4 * i + e // 2))
                    pe.wait_ge(prod_ready[par], 4 * (8 * i + q // 2 + 1))
                    for h in range(2):
                        m = 2 * par + h
                        tr = nc.tensor.matmul(ps[CH * m:CH * m + CH, 4 + e % 2, :], onehot[:, 2 * q + h, :],
                                              prod[:, par, h, :], start=True, stop=True, tile_position=(0, CH * m))
                    tr.then_inc(q_done[par], 1)

                pe.wait_ge(rad_loaded, 16 * (i + 1))
                first_layer(0)
                if due(i):
                    if due(i - 1):
                        pe.wait_ge(rt_out, i - 1)
                    l0_spread(i - 1)
                second_layer(0)
                first_layer(1)
                for q in range(16):
                    f = q // 4
                    third_layer(q)
                    if q:
                        item_sums(q - 1)
                    if q % 4 == 1 and f + 1 < 4:
                        second_layer(f + 1)
                    if q % 4 == 2 and f + 2 < 4:
                        first_layer(f + 2)
                item_sums(15)
                if due(i):
                    pe.wait_ge(R_ready, i)
                l0_degrees(i)
                if with_totals:
                    transpose_totals(i - 1, 2, 7, 256)

            pe.wait_ge(w3_ready, 2)
            l0_step(0, False)
            l0_step(1, True)
            with pe.Fori(2, STEPS) as i:
                l0_step(i, True)
            pe.wait_ge(rt_out, STEPS - 1)
            l0_spread(STEPS - 1)
            transpose_totals(STEPS - 1, 2, 7, 256)

            def node_products(phase, weights):
                for b in range(WB):
                    par = b % 2
                    done = uses(par, phase) + b // 2
                    if due(done):
                        pe.wait_ge(nt_out[par], done)
                    for g in range(NG):
                        tr = nc.tensor.transpose(ps[:, par, g * P:g * P + P], xw[:, b, g * P:g * P + P], ident[:])
                    tr.then_inc(nt_ready[par], 1)
                    pe.wait_ge(nt_out[par], done + 1)
                    if due(done):
                        pe.wait_ge(nx_used[par], done)
                    for g in range(NG):
                        tr = nc.tensor.matmul(ps[:, 2 + par, g * P:g * P + P], xt[:, par, g * P:g * P + P], weights,
                                              start=True, stop=True)
                    tr.then_inc(nx_ready[par], 1)

            pe.wait_ge(x0_loaded, 16)
            node_products(0, w_self[:])

            def item_sums(l, i, ch):
                n1 = l * STEPS + i
                pe.wait_ge(bm_ready[ch], n1 + 1)
                pe.wait_ge(xm_ready[ch], n1 + 1)
                for pair in range(2):
                    e = 2 * ch + pair
                    bank = e % 4
                    if due(4 * n1 + e // 4):
                        pe.wait_ge(s_out[bank], 4 * n1 + e // 4)
                    for h in range(2):
                        r = (2 * e + h) % 16
                        tr = nc.tensor.matmul(ps[:, bank, 256 * h:256 * h + 256], xm[:, r].rearrange("p j c -> p (j c)"),
                                              bm[:, r].rearrange("p c g a -> p (c g a)"), start=True, stop=True)
                    tr.then_inc(s_done[bank], 1)

            def tap_products(l, i, par, part8):
                if part8 == 0:
                    for bank in range(4):
                        pe.wait_ge(s_out[bank], 4 * (l * STEPS + i + 1))
                    pe.wait_ge(R_ready, (l + 1) * STEPS + i)
                for k in range(8 * part8, 8 * part8 + 8):
                    tr = nc.tensor.matmul(ps[:, 7, 0:P], w_taps[:, k, :], S[:, par, :, k // 16, :, k % 16],
                                          start=(k == 0), stop=(k == TAPS - 1), skip_group_check=True)
                if part8 == 7:
                    tr.then_inc(part_ready, 1)

            def l1_step(l, i, par, with_taps, with_totals):
                for ch in range(8):
                    item_sums(l, i, ch)
                    if with_taps:
                        tap_products(l, i - 1, 1 - par, ch)
                if with_totals:
                    transpose_totals((l + 1) * STEPS + i - 2, 1, 6, 0)

            for l in range(LAYERS):
                pe.wait_ge(w_loaded, 16 * (l + 1))
                l1_step(l, 0, 0, False, False)
                l1_step(l, 1, 1, True, False)
                with pe.Fori(2, PAIRS_END, 2) as i:
                    for par in range(2):
                        l1_step(l, i + par, par, True, True)
                for i in range(PAIRS_END, STEPS):
                    l1_step(l, i, i % 2, True, True)
                transpose_totals((l + 2) * STEPS - 2, 1, 6, 0)
                for part8 in range(8):
                    tap_products(l, STEPS - 1, (STEPS - 1) % 2, part8)
                transpose_totals((l + 2) * STEPS - 1, 1, 6, 0)
                pe.wait_ge(x_ready, l + 1)
                node_products(l + 1, w_root[:, l, :])
                for half in range(2):
                    pe.wait_ge(sum_ready, 2 * l + half + 1)
                    nc.tensor.matmul(ps[:, 4, 0:CH], ones[:], bn[:, 0, :], start=True, stop=True).then_inc(sum_done, 1)


def prepare(inputs):
    f = np.float32
    x, src, dst = (np.asarray(inputs[k]) for k in ("x", "src", "dst"))
    nodes, edges = x.shape[0], src.shape[0]
    tiles, windows, items, steps, nb, wb = sizes(nodes, edges)
    d = {}
    d["x"] = np.zeros((wb * P * J, CH), f)
    d["x"][:nodes] = x
    d["src"] = src.reshape(tiles, P)
    d["dst"] = dst.reshape(tiles, P)
    d["last_dst"] = dst[P - 1::P].reshape(1, tiles)
    attr = np.concatenate([np.asarray(inputs[f"edge_attr_{k}"]) for k in (3, 4, 8)], axis=1)
    d["attr"] = np.ascontiguousarray(attr.reshape(tiles, P, 15).transpose(0, 2, 1)).reshape(tiles, 15 * P)
    g = lambda name: np.asarray(inputs[name])
    W1, W2, W3 = g("L0_gnn_W1"), g("L0_gnn_W2"), g("L0_gnn_W3")
    d["w1"] = np.zeros((P, 8, P), f)
    for q in range(8):
        for h in range(2):
            d["w1"][16 * q + 8 * h:16 * q + 8 * h + 8, q, HID * h:HID * h + HID] = W1
    d["w2"] = np.zeros((P, 2, HID), f)
    for h in range(2):
        d["w2"][HID * h:HID * h + HID, h] = W2
    d["w3"] = np.concatenate([W3, g("L0_gnn_b3")[None]], axis=0)
    d["b1"] = np.concatenate([g("L0_gnn_b1")] * 2).reshape(P, 1)
    d["b2"] = g("L0_gnn_b2").reshape(HID, 1)
    mean = 1.0 / np.sqrt(2.0 * MUL) / np.sqrt(16.0)
    d["w3_scale"] = np.full((HID + 1, 256), mean, f)
    d["w3_scale"][:, MUL * MUL:2 * MUL * MUL] = mean / np.sqrt(3.0)
    d["spread"] = np.zeros((P, GROUP, J), f)
    for q in range(4):
        for j in range(J):
            d["spread"][CH * q + j, j % GROUP, NG * q + j // GROUP] = 1.0
    one = np.zeros((CH, CH), f)
    one[:MUL, :MUL] = g("L0_gnn_Ws")
    for i in range(3):
        one[MUL + i::3, MUL + i::3] = g("L0_gnn_Wv")
    d["w_self"] = np.zeros((P, P), f)
    d["w_root"] = np.zeros((P, 3, P), f)
    for j in range(GROUP):
        own = slice(CH * j, CH * j + CH)
        d["w_self"][own, own] = one
        for l in range(3):
            d["w_root"][own, l, own] = g(f"L1_gnn_R{l + 1}")
    for l in range(3):
        taps = np.zeros((P, TAPS, P), f)
        for j in range(GROUP):
            taps[CH * j:CH * j + CH, :, CH * j:CH * j + CH] = g(f"L1_gnn_W{l + 1}").transpose(1, 0, 2)
        d[f"w_taps{l}"] = taps
    d["chan"] = np.stack([np.stack([g(f"L1_gnn_{k}{l + 1}") for k in ("b", "g", "be")]) for l in range(3)])[None]
    rows = np.ones((P, 1), f)
    d["ident"] = np.eye(P, dtype=f)
    d["ones"] = np.ones((P, P), f)
    d["tap_ids"] = rows * np.arange(4, dtype=f)
    d["item_ids"] = np.arange(nb * P, dtype=f).reshape(nb, P).T
    d["window_ids"] = np.arange(wb * P, dtype=f).reshape(wb, P).T
    d["tile_ids"] = np.arange(tiles, dtype=f).reshape(1, tiles)
    node = ((wb - 1) * P + np.arange(P)[:, None]) * J + np.arange(J)
    d["node_mask"] = (node < nodes).astype(f)
    return nodes, edges, {k: np.ascontiguousarray(v_) for k, v_ in d.items()}


def kernel(**inputs):
    import concourse.bacc as bacc
    from concourse.bass_utils import run_bass_kernel_spmd

    nodes, edges, data = prepare(inputs)
    nc = bacc.Bacc("TRN2", target_bir_lowering=False, num_devices=1)
    arrays, args = {}, {}
    for name, v_ in data.items():
        arrays[f"in_{name}"] = v_
        args[name] = nc.dram_tensor(f"in_{name}", v_.shape, mybir.dt.from_np(v_.dtype), kind="ExternalInput").ap()
    out = nc.dram_tensor("out_nodes", data["x"].shape, mybir.dt.float32, kind="ExternalOutput").ap()
    graph_kernel(nc, nodes, edges, args, out)
    got = run_bass_kernel_spmd(nc, [arrays], core_ids=[0])
    return got.results[0]["out_nodes"][:nodes]
```

```python
from collections import namedtuple
from contextlib import ExitStack

import concourse.bass as bass
import numpy as np
from concourse import mybir

P = 128
CH = 32
J = 16
HALF = J // 2
GROUP = 4
NG = J // GROUP
TAPS = 64
HID = 64
MUL = 8
ROW = J * CH
STEP = 32
QUART = 8
NEG = 0.01
EPS = 1e-5
BANK = 512


Path = namedtuple("Path", "narrow items steps blocks")


def sizes(nodes, edges):
    tiles = edges // P
    windows = -(-nodes // J)

    def path(narrow, items):
        steps = -(-items // STEP)
        return Path(narrow, items, steps, -(-steps * STEP // P))

    return tiles, windows, -(-windows // P), path(True, tiles + 1), path(False, tiles + windows)


def graph_kernel(nc, nodes, edges, a, out):
    F32, I32 = mybir.dt.float32, mybir.dt.int32
    ALU, ACT, AX = mybir.AluOpType, mybir.ActivationFunctionType, mybir.AxisListType
    TILES, WINDOWS, WB, NARROW, WIDE = sizes(nodes, edges)
    NB = max(NARROW.blocks, WIDE.blocks)
    NI = NARROW.steps * STEP
    SLOTS_W = WB * J
    NODE_F = WB * ROW
    ATTR = 15
    META = 9
    LAYERS = 3
    ds = bass.ds

    def dram(name, shape, dt):
        return nc.dram_tensor(name, shape, dt, kind="Internal").ap()

    src_items = dram("src_items", [P, NB * P], I32)
    meta_items = dram("meta_items", [P, NB * 4, META, STEP], F32)
    rad_items = dram("rad_items", [NB * P, MUL * P], F32)
    window_items = dram("window_items", [1 + NB * P], F32)
    carry_items = dram("carry_items", [NB * P], F32)
    agg_rows = dram("agg_rows", [NB * P, ROW], F32)
    cnt_rows = dram("cnt_rows", [NB * P, ROW], F32)
    run_counts = dram("run_counts", [2 + 2 * WB * P], F32)
    x_rows = dram("x_rows", [WB * P * J, CH], F32)

    ctx = ExitStack()
    with ctx:
        def sb(name, shape, dt=F32):
            return ctx.enter_context(nc.sbuf_tensor(name, shape, dt))

        def sem(name):
            return ctx.enter_context(nc.semaphore(name))

        def sems(name, n):
            return [sem(f"{name}{i}") for i in range(n)]

        ident = sb("ident", [P, P])
        ones = sb("ones", [P, P])
        tap_ids = sb("tap_ids", [P, 4])
        item_ids = sb("item_ids", [P, NB])
        window_ids = sb("window_ids", [P, WB])
        node_mask = sb("node_mask", [P, J])
        w1 = sb("w1", [P, 8, P])
        w2 = sb("w2", [P, 2, P])
        w3 = sb("w3", [HID + 1, 256])
        w3_scale = sb("w3_scale", [HID + 1, 256])
        b1 = sb("b1", [P, 1])
        b2 = sb("b2", [HID, 1])
        spread = sb("spread", [P, GROUP, J])
        w_self = sb("w_self", [P, P])
        w_root = sb("w_root", [P, LAYERS, P])
        chan = sb("chan", [P, LAYERS, 3, CH])
        w_taps = sb("w_taps", [P, TAPS, P])

        tile_of = sb("tile_of", [P, NB])
        window4 = sb("window4", [P, NB])
        tile_idx = sb("tile_idx", [P, NB], I32)
        last_f = sb("last_f", [P, WB])
        last_idx = sb("last_idx", [P, WB], I32)
        tile_col = sb("tile_col", [P, 1], I32)
        w4_col = sb("w4_col", [P, 1])
        win_now = sb("win_now", [NB, P])
        win_before = sb("win_before", [NB, P])
        goes_on = sb("goes_on", [NB, P])
        minus = sb("minus", [1, 1])
        zeros = sb("zeros", [1, 2])
        half_ids = sb("half_ids", [P, WB, 2])
        items_up_to = sb("items_up_to", [P, 3, WB, 2])
        run_last = sb("run_last", [P, 2, WB, 2])
        run_exists = sb("run_exists", [P, 2, WB, 2])
        run_idx = sb("run_idx", [P, 2, WB, 2], I32)
        span = sb("span", [P, 1])
        is_wide = sb("is_wide", [P, 1], I32)

        idx = sb("idx", [P, STEP], I32)
        meta = sb("meta", [P, META, STEP])
        carry = sb("carry", [P, STEP])
        xg = sb("xg", [P, STEP, CH])
        group_hot = sb("group_hot", [P, STEP, NG])
        place_hot = sb("place_hot", [P, STEP, GROUP])
        onehot = sb("onehot", [P, STEP, CH])
        hat = sb("hat", [P, STEP, 3, 4])
        hat2 = sb("hat2", [P, STEP, 3, 4])
        b01 = sb("b01", [P, STEP, 16])
        b01_group = sb("b01_group", [P, STEP, NG, 16])
        R = sb("R", [P, 2, STEP * NG])
        last = sb("last", [P, 2, NG])
        rts = sb("rts", [P, 2, P])

        xw = sb("xw", [P, WB, ROW])
        x1 = sb("x1", [P, WB, ROW])
        rcnt = sb("rcnt", [P, SLOTS_W])
        stat = sb("stat", [P, 4, SLOTS_W])
        bn = sb("bn", [P, 6, CH])
        xt = sb("xt", [P, 2, BANK])

        S_F = STEP * NG * TAPS
        XM_F = 16 * NG * TAPS
        BIG = max(7 * NI, 3 * TILES, 2 * S_F + XM_F + 16 * P, 3 * NODE_F, (ATTR + 9 + 2 * META) * P)
        big = sb("big", [P, BIG])
        last_dst = big[:, 0:TILES].bitcast(I32)
        first_dst = big[:, NI:2 * NI].bitcast(I32)
        base_i = big[:, 2 * NI:3 * NI].bitcast(I32)
        base_f = big[:, 3 * NI:4 * NI]
        reach = big[:, 4 * NI:4 * NI + TILES]
        dst_i = big[:, 0:NI].bitcast(I32)
        quarter_t = big[:, 2 * NI:3 * NI]
        place_t = big[:, 3 * NI:4 * NI]
        coord_t = big[:, 4 * NI:7 * NI]
        last_window = big[:, TILES:2 * TILES]
        tile_end = big[:, 2 * TILES:3 * TILES]
        src_r = big[:, 0:P].bitcast(I32)
        dst_r = big[:, P:2 * P].bitcast(I32)
        attr_r = big[:, 2 * P:(2 + ATTR) * P]
        at = 2 + ATTR
        src_f = big[:, at * P:(at + 1) * P]
        slot_i = big[:, (at + 1) * P:(at + 3) * P].bitcast(I32)
        table_f = big[:, (at + 3) * P:(at + 8) * P]
        src_t = big[:, (at + 8) * P:(at + 9) * P].bitcast(I32)
        meta_flat = big[:, (at + 9) * P:(at + 9 + META) * P]
        meta_t = meta_flat.rearrange("p (n c i) -> p n c i", n=4, c=META)
        def part(at, shape):
            n = int(np.prod(shape))
            flat = big[:, at:at + n]
            if len(shape) == 1:
                return flat, at + n
            names = "abcde"[:len(shape)]
            return flat.rearrange(f"p ({' '.join(names)}) -> p {' '.join(names)}", **dict(zip(names, shape))), at + n

        prod, at = part(0, (4, 2, ROW))
        feat, at = part(at, (STEP, 64))
        dots, at = part(at, (QUART, 24))
        h1_s, at = part(at, (BANK,))
        h2_s, at = part(at, (2, 2, BANK))
        rad, at = part(at, (2, P))
        sums, at = part(at, (STEP // 4, CH))
        S, at = part(0, (2, STEP, 4, NG, 16))
        bm, at = part(at, (16, 4, NG, 16))
        xm, at = part(at, (16, GROUP, CH))
        agg, at = part(0, (WB, ROW))
        y, at = part(at, (WB, ROW))
        sq, at = part(at, (WB, ROW))

        ps = ctx.enter_context(nc.psum_tensor("ps", [P, 8, BANK], F32))

        loaded, w_loaded, x0_loaded = sem("loaded"), sem("w_loaded"), sem("x0_loaded")
        dve_step = sem("dve_step")
        gathers_go, loads_go = sem("gathers_go"), sem("loads_go")
        count_ready, span_ready = sem("count_ready"), sem("span_ready")
        tables_in, tables_ready = sem("tables_in"), sem("tables_ready")
        tile_end_in, runs_ready, runs_stored = sem("tile_end_in"), sem("runs_ready"), sem("runs_stored")
        runs_in, run_idx_ready = sem("runs_in"), sem("run_idx_ready")
        sh_loaded = sem("sh_loaded")
        win_stored, win_loaded, goes_ready, goes_stored = (sem("win_stored"), sem("win_loaded"),
                                                           sem("goes_ready"), sem("goes_stored"))
        minus_ready = sem("minus_ready")
        col_ready, src_in, dst_in, attr_in = sem("col_ready"), sem("src_in"), sem("dst_in"), sem("attr_in")
        rad_in = sem("rad_in")
        rows_ready, item_tr, item_out = sem("rows_ready"), sem("item_tr"), sem("item_out")
        meta_stored, src_stored, rad_stored = sem("meta_stored"), sem("src_stored"), sem("rad_stored")
        idx_loaded, x_in = sems("idx_loaded", 2), sems("x_in", 4)
        meta_loaded, carry_loaded, rad_loaded = sem("meta_loaded"), sem("carry_loaded"), sems("rad_loaded", 2)
        meta_used = sem("meta_used")
        onehot_ready, feat_ready = sem("onehot_ready"), sems("feat_ready", 4)
        h1_ready, h1_act, h2_ready, h2_act = sem("h1_ready"), sem("h1_act"), sem("h2_ready"), sem("h2_act")
        tpw_ready, prod_ready, q_done, q_out = (sems("tpw_ready", 2), sems("prod_ready", 4),
                                                sems("q_done", 4), sems("q_out", 2))
        deg_done, w3_ready = sem("deg_done"), sem("w3_ready")
        bm_ready, xm_ready, s_done, s_out = (sems("bm_ready", 8), sems("xm_ready", 8),
                                             sems("s_done", 4), sems("s_out", 4))
        part_ready, R_ready, rt_ready, rt_out = sem("part_ready"), sem("R_ready"), sem("rt_ready"), sem("rt_out")
        rows_stored = sem("rows_stored")
        agg_in, cnt_in = sem("agg_in"), sem("cnt_in")
        nt_ready, nt_out = sems("nt_ready", 2), sems("nt_out", 2)
        nx_ready, nx_used = sems("nx_ready", 2), sems("nx_used", 2)
        sum_ready, sum_done, root_in, root_out = sem("sum_ready"), sem("sum_done"), sem("root_in"), sem("root_out")
        x_ready, x_stored, out_ready, out_stored = (sem("x_ready"), sem("x_stored"), sem("out_ready"),
                                                    sem("out_stored"))

        consts = [(ident, "ident"), (ones, "ones"), (tap_ids, "tap_ids"), (item_ids, "item_ids"),
                  (window_ids, "window_ids"), (node_mask, "node_mask"), (w1, "w1"), (w2, "w2"), (w3, "w3"),
                  (w3_scale, "w3_scale"), (b1, "b1"), (b2, "b2"), (spread, "spread"), (w_self, "w_self"),
                  (w_root, "w_root"), (half_ids, "half_ids")]
        LOADS = 16 * (len(consts) + 3)

        def rows0(path):
            return 2 * 16 * path.steps

        def pairs_end(path):
            return 2 + 2 * ((path.steps - 2) // 2)

        def uses(parity, phase):
            return phase * ((WB + 1) // 2 if parity == 0 else WB // 2)

        def due(value):
            return not isinstance(value, int) or value > 0

        block = ctx.enter_context(nc.Block())

        def sync_program(sp, path):
            STEPS = path.steps
            if path.narrow:
                sp.dma_start(dst_i, a["dst_t"]).then_inc(tables_in, 16)
                sp.dma_start(coord_t, a["coord_t"]).then_inc(tables_in, 16)
                sp.dma_start(win_now[0:path.blocks].bitcast(I32), a["first_now"]).then_inc(tables_in, 16)
                sp.dma_start(win_before[0:path.blocks].bitcast(I32), a["first_before"]).then_inc(tables_in, 16)
                sp.wait_ge(tables_ready, 1)
                by_step = meta_items[:, 0:STEPS]
                with nc.allow_non_contiguous_dma(reason="the channels of an iteration lie together"):
                    sp.dma_start(by_step[:, :, 0:3, :], coord_t.rearrange("p (n c i) -> p n c i", c=3, i=STEP)
                                 ).then_inc(meta_stored, 16)
                    sp.dma_start(by_step[:, :, 3, :], quarter_t.rearrange("p (n i) -> p n i", i=STEP)
                                 ).then_inc(meta_stored, 16)
                    sp.dma_start(by_step[:, :, 4, :], place_t.rearrange("p (n i) -> p n i", i=STEP)
                                 ).then_inc(meta_stored, 16)
                sp.dma_start(carry_items[0:path.blocks * P].rearrange("(b p) -> b p", p=P),
                             goes_on[0:path.blocks]).then_inc(goes_stored, 16)
                sp.wait_ge(runs_ready, 2)
                sp.dma_start(run_counts[0:2].rearrange("(a b) -> a b", a=1), zeros[:]).then_inc(runs_stored, 16)
                sp.dma_start(run_counts[2:2 + 2 * WB * P].rearrange("(b p h) -> p b h", p=P, h=2),
                             items_up_to[:, 0]).then_inc(runs_stored, 16)
                sp.wait_ge(runs_stored, 32)
                for before in (1, 2):
                    sp.dma_start(items_up_to[:, before], run_counts[2 - before:2 - before + 2 * WB * P]
                                 .rearrange("(b p h) -> p b h", p=P, h=2)).then_inc(runs_in, 16)
                sp.wait_ge(meta_stored, 48)
                sp.wait_ge(goes_stored, 16)
            else:
                sp.dma_start(tile_end, a["tile_ids"].to_broadcast([P, TILES])).then_inc(tile_end_in, 16)
                sp.wait_ge(minus_ready, 1)
                sp.dma_start(window_items[0:1].rearrange("(a b) -> a b", a=1), minus[:]).then_inc(win_stored, 16)
                sp.wait_ge(count_ready, 1)
                with nc.allow_non_contiguous_dma(reason="one column per block of items"):
                    sp.dma_start(window_items[1:1 + WIDE.blocks * P].rearrange("(b p) -> p b", p=P),
                                 tile_of[:, 0:WIDE.blocks]).then_inc(win_stored, 16)
                sp.wait_ge(win_stored, 32)
                sp.dma_start(win_before[0:WIDE.blocks], window_items[0:WIDE.blocks * P].rearrange("(b p) -> b p", p=P)).then_inc(win_loaded, 16)
                sp.dma_start(win_now[0:WIDE.blocks], window_items[1:1 + WIDE.blocks * P].rearrange("(b p) -> b p", p=P)).then_inc(win_loaded, 16)
                sp.wait_ge(goes_ready, 1)
                sp.dma_start(carry_items[0:WIDE.blocks * P].rearrange("(b p) -> b p", p=P), goes_on[0:WIDE.blocks]).then_inc(goes_stored, 16)

                def store_block(b):
                    sp.wait_ge(rad_in, 16 * (b + 1))
                    sp.dma_start(rad_items[ds(b * P, P), :], attr_r[:, 7 * P:15 * P]).then_inc(rad_stored, 16)
                    sp.wait_ge(item_out, 4 * (b + 1))
                    sp.dma_start(meta_items[:, ds(b * 4, 4), :, :].rearrange("p n c i -> p (n c i)"),
                                 meta_flat).then_inc(meta_stored, 16)
                    sp.dma_start(src_items[:, ds(b * P, P)], src_t).then_inc(src_stored, 16)

                store_block(0)
                with sp.Fori(1, WIDE.blocks) as b:
                    store_block(b)
                sp.wait_ge(rad_stored, 16 * WIDE.blocks)
                sp.wait_ge(meta_stored, 16 * WIDE.blocks)
                sp.wait_ge(src_stored, 16 * WIDE.blocks)
                sp.wait_ge(goes_stored, 16)
            src_table = a["src_t"] if path.narrow else src_items
            sh_table = a["sh_t"] if path.narrow else meta_items[:, :, 5:META, :]
            rad_table = a["rad"] if path.narrow else rad_items

            def load_indices(n, i):
                for half in range(2):
                    for q in (2 * half, 2 * half + 1):
                        if due(n):
                            sp.wait_ge(x_in[q], 16 * QUART * n)
                    sp.sem_inc(loads_go, 1)
                    sp.dma_start(idx[:, 16 * half:16 * half + 16],
                                 src_table[:, ds(i * STEP + 16 * half, 16)]).then_inc(idx_loaded[half], 16)

            def load_meta(n, i, first, end):
                if due(n):
                    sp.wait_ge(meta_used, n)
                sp.sem_inc(loads_go, 1)
                sp.dma_start(meta[:, first:end, :], meta_items[:, ds(i, 1), first:end, :]
                             .rearrange("p n c i -> p (n c) i")).then_inc(meta_loaded, 16)

            def load_carry(n, i):
                if due(n):
                    sp.wait_ge(R_ready, n)
                sp.sem_inc(loads_go, 1)
                sp.dma_start(carry[:], carry_items[ds(i * STEP, STEP)].rearrange("(o i) -> o i", o=1)
                             .to_broadcast([P, STEP])).then_inc(carry_loaded, 16)

            def load_radials(i, half):
                if due(i):
                    sp.wait_ge(h1_ready, 4 * i - 2 + 2 * half)
                sp.sem_inc(loads_go, 1)
                sp.dma_start(rad[:, half], rad_table[ds(i * STEP + 16 * half, 16), :]
                             .rearrange("n (k f) -> (n k) f", k=MUL)).then_inc(rad_loaded[half], 16)

            def l0_loads(i):
                load_radials(i, 0)
                load_indices(i, i)
                load_radials(i, 1)
                load_meta(i, i, 3, 5)
                sp.dma_start(meta[:, 5:META, :], sh_table[:, ds(i, 1), :, :].rearrange("p n c i -> p (n c) i")
                             ).then_inc(sh_loaded, 16)

            l0_loads(0)
            with sp.Fori(1, STEPS) as i:
                l0_loads(i)
                load_carry(i - 1, i - 1)
            load_carry(STEPS - 1, STEPS - 1)
            sp.wait_ge(x_ready, 1)
            sp.dma_start(x_rows.rearrange("(b p j) c -> p b (j c)", p=P, j=J), xw[:]).then_inc(x_stored, 16)
            for l in range(LAYERS):
                base = (l + 1) * STEPS
                if l:
                    sp.wait_ge(part_ready, base)
                    sp.dma_start(w_taps[:], a[f"w_taps{l}"]).then_inc(w_loaded, 16)
                    sp.wait_ge(x_ready, l + 1)
                    sp.dma_start(x_rows.rearrange("(b p j) c -> p b (j c)", p=P, j=J), xw[:]).then_inc(x_stored, 16)
                for i in range(2):
                    load_meta(base + i, i, 0, 5)
                    load_indices(base + i, i)
                with sp.Fori(2, STEPS) as i:
                    load_meta(base + i, i, 0, 5)
                    load_indices(base + i, i)
                    load_carry(base + i - 2, i - 2)
                for i in (STEPS - 2, STEPS - 1):
                    load_carry(base + i, i)
            sp.wait_ge(out_ready, 1)
            sp.dma_start(out.rearrange("(b p j) c -> p b (j c)", p=P, j=J), xw[:]).then_inc(out_stored, 16)
            sp.wait_ge(out_stored, 16)

        @block.sync
        def _(sp):
            for tile_, name in consts:
                sp.dma_start(tile_[:], a[name]).then_inc(loaded, 16)
            sp.dma_start(chan[:], a["chan"].to_broadcast([P, LAYERS, 3, CH])).then_inc(loaded, 16)
            sp.dma_start(last_dst, a["last_dst"].to_broadcast([P, TILES])).then_inc(loaded, 16)
            sp.dma_start(first_dst, a["first_dst"].to_broadcast([P, NI])).then_inc(loaded, 16)
            x_by_window = a["x"].rearrange("(b p j) c -> p b (j c)", p=P, j=J)
            sp.dma_start(xw[:], x_by_window).then_inc(x0_loaded, 16)
            sp.dma_start(w_taps[:], a["w_taps0"]).then_inc(w_loaded, 16)

            sp.wait_ge(span_ready, 1)
            wide = sp.value_load(is_wide[0:1, 0:1], min_val=0, max_val=1)
            with sp.If(wide):
                sync_program(sp, WIDE)
            with sp.Else():
                sync_program(sp, NARROW)

        def pool_program(pool, path):
            STEPS = path.steps
            def gather(dst_tile, table, index):
                return nc.gpsimd.indirect_dma_start(
                    out=dst_tile, out_offset=None, in_=table,
                    in_offset=bass.IndirectOffsetOnAxis(ap=index, axis=0))

            def gather_block(b):
                pool.wait_ge(col_ready, b + 1)
                if due(b):
                    pool.wait_ge(item_tr, b)
                    pool.wait_ge(rad_stored, 16 * b)
                pool.sem_inc(gathers_go, 1)
                gather(src_r, a["src"], tile_col[:]).then_inc(src_in, 16)
                gather(dst_r, a["dst"], tile_col[:]).then_inc(dst_in, 16)
                gather(attr_r[:, 0:7 * P], a["attr"], tile_col[:]).then_inc(attr_in, 16)
                gather(attr_r[:, 7 * P:15 * P], a["rad"], tile_col[:]).then_inc(rad_in, 16)

            if not path.narrow:
                gather_block(0)
                with pool.Fori(1, path.blocks) as b:
                    gather_block(b)

            def gather_sources(table, n, group_free):
                for q in range(4):
                    if q % 2 == 0:
                        pool.wait_ge(idx_loaded[q // 2], 16 * (n + 1))
                    group_free(q)
                    pool.sem_inc(gathers_go, 1)
                    for r in range(QUART):
                        s = QUART * q + r
                        gather(xg[:, s, :], table, idx[:, s:s + 1]).then_inc(x_in[q], 16)

            def window_totals(table, into, beside, done):
                if path.narrow:
                    by_half = table[0:NI, :].rearrange("i (h f) -> (i h) f", h=2)
                    for run, to in enumerate((into, beside)):
                        for b in range(WB):
                            for h in range(2):
                                gather(to[:, b, ROW // 2 * h:ROW // 2 * (h + 1)], by_half,
                                       run_idx[:, run, b, h:h + 1]).then_inc(done, 16)
                else:
                    for b in range(WB):
                        gather(into[:, b, :], table[0:STEPS * STEP, :], last_idx[:, b:b + 1]).then_inc(done, 16)

            gather_sources(a["x"], 0, lambda q: None)
            with pool.Fori(1, STEPS) as i:
                gather_sources(a["x"], i, lambda q: pool.wait_ge(feat_ready[q], i))
            pool.wait_ge(rows_stored, rows0(path))
            pool.wait_ge(part_ready, STEPS)
            if path.narrow:
                pool.wait_ge(run_idx_ready, 1)
            pool.sem_inc(gathers_go, 1)
            window_totals(agg_rows, agg, y, agg_in)
            window_totals(cnt_rows, sq, x1, cnt_in)
            for l in range(LAYERS):
                pool.wait_ge(x_stored, 16 * (l + 1))
                gather_sources(x_rows, (l + 1) * STEPS, lambda q: pool.wait_ge(xm_ready[2 * q + 1], l * STEPS) if l else None)
                with pool.Fori(1, STEPS) as i:
                    gather_sources(x_rows, (l + 1) * STEPS + i,
                                   lambda q: pool.wait_ge(xm_ready[2 * q + 1], l * STEPS + i))
                pool.wait_ge(rows_stored, rows0(path) + 16 * STEPS * (l + 1))
                pool.wait_ge(part_ready, (l + 2) * STEPS)
                window_totals(agg_rows, agg, y, agg_in)

        @block.gpsimd
        def _(pool):
            pool.wait_ge(span_ready, 1)
            wide = pool.value_load(is_wide[0:1, 0:1], min_val=0, max_val=1)
            with pool.If(wide):
                pool_program(pool, WIDE)
            with pool.Else():
                pool_program(pool, NARROW)

        def scalar_program(act, path):
            STEPS = path.steps
            act.wait_ge(loaded, LOADS)
            def copy_block(b):
                act.wait_ge(item_tr, b + 1)
                if due(b):
                    act.wait_ge(meta_stored, 16 * b)
                    act.wait_ge(src_stored, 16 * b)
                nc.scalar.copy(meta_t[:, :, 0:4, :].rearrange("p n c i -> p c n i"),
                               ps[:, 0, :].rearrange("p (c n i) -> p c n i", c=4, n=4)).then_inc(item_out, 1)
                nc.scalar.copy(meta_t[:, :, 4:8, :].rearrange("p n c i -> p c n i"),
                               ps[:, 1, :].rearrange("p (c n i) -> p c n i", c=4, n=4)).then_inc(item_out, 1)
                nc.scalar.copy(meta_t[:, :, 8, :], ps[:, 2, 0:P].rearrange("p (n i) -> p n i", n=4)
                               ).then_inc(item_out, 1)
                nc.scalar.copy(src_t, ps[:, 2, P:2 * P]).then_inc(item_out, 1)

            if not path.narrow:
                copy_block(0)
                with act.Fori(1, path.blocks) as b:
                    copy_block(b)

            def store_rows(n, kinds, bank, col, stored):
                act.wait_ge(rt_ready, n + 1)
                if due(stored):
                    act.wait_ge(rows_stored, stored)
                nc.scalar.copy(rts[:, 0:kinds, :], ps[:, bank, col:col + kinds * P].rearrange("p (k f) -> p k f", k=kinds)
                               ).then_inc(rt_out, 1)
                act.wait_ge(rt_out, n + 1)

            def rows_at(table, i):
                return table[ds(i * STEP, STEP), :].rearrange("i (g f) -> (i g) f", g=NG)

            def first_layer(i, f):
                act.wait_ge(h1_ready, 4 * i + f + 1)
                if due(8 * i + 2 * f):
                    act.wait_ge(h2_ready, 8 * i + 2 * f)
                nc.scalar.activation(h1_s, ps[:, 0, :], ACT.Silu, bias=b1[:, 0:1]).then_inc(h1_act, 1)

            def second_layer(i, f):
                for h in range(2):
                    act.wait_ge(h2_ready, 8 * i + 2 * f + h + 1)
                    if due(8 * i + 2 * f - 2):
                        act.wait_ge(tpw_ready[1], 8 * i + 2 * f - 2)
                    nc.scalar.activation(h2_s[0:HID, f % 2, h, :], ps[0:HID, (1, 6)[h], :], ACT.Silu,
                                         bias=b2[:, 0:1]).then_inc(h2_act, 1)

            def l0_step(i, groups):
                for f in range(4):
                    if f + 1 < groups:
                        second_layer(i, f + 1)
                    if f + 2 < groups:
                        first_layer(i, f + 2)

            def l0_rows(i):
                store_rows(i, 2, 7, 256, 32 * i)
                act.dma_start(rows_at(agg_rows, i), rts[:, 0, :]).then_inc(rows_stored, 16)
                act.dma_start(rows_at(cnt_rows, i), rts[:, 1, :]).then_inc(rows_stored, 16)

            first_layer(0, 0)
            second_layer(0, 0)
            first_layer(0, 1)
            l0_step(0, 6)
            l0_step(1, 6)
            l0_rows(0)
            with act.Fori(2, STEPS - 1) as i:
                l0_step(i, 6)
                l0_rows(i - 1)
            l0_step(STEPS - 1, 4)
            l0_rows(STEPS - 2)
            l0_rows(STEPS - 1)

            roots = [0]

            def square_root(col):
                roots[0] += 1
                act.wait_ge(root_in, roots[0])
                nc.scalar.activation(col, col, ACT.Sqrt).then_inc(root_out, 1)

            def node_copies(phase):
                for b in range(WB):
                    par = b % 2
                    done = uses(par, phase) + b // 2
                    act.wait_ge(nt_ready[par], done + 1)
                    if due(done):
                        act.wait_ge(nx_ready[par], done)
                    nc.scalar.copy(xt[:, par, :], ps[:, par, :]).then_inc(nt_out[par], 1)

            node_copies(0)
            square_root(stat[:, 1, :])

            def l1_step(l, i, par):
                for e in range(16):
                    bank = e % 4
                    if e == 0:
                        act.wait_ge(part_ready, (l + 1) * STEPS + i - 1)
                    act.wait_ge(s_done[bank], 4 * (l * STEPS + i) + e // 4 + 1)
                    nc.scalar.copy(S[:, par, 2 * e:2 * e + 2].rearrange("p n c g a -> p (n c g a)"), ps[:, bank, :]
                                   ).then_inc(s_out[bank], 1)

            def l1_rows(l, i):
                n = (l + 1) * STEPS + i
                store_rows(n, 1, 6, 0, rows0(path) + 16 * (n - STEPS))
                act.dma_start(rows_at(agg_rows, i), rts[:, 0, :]).then_inc(rows_stored, 16)

            for l in range(LAYERS):
                l1_step(l, 0, 0)
                l1_step(l, 1, 1)
                with act.Fori(2, pairs_end(path), 2) as i:
                    for par in range(2):
                        l1_step(l, i + par, par)
                        l1_rows(l, i + par - 2)
                for i in range(pairs_end(path), STEPS):
                    l1_step(l, i, i % 2)
                    l1_rows(l, i - 2)
                for i in (STEPS - 2, STEPS - 1):
                    l1_rows(l, i)
                node_copies(l + 1)
                square_root(bn[:, 2, :])
            square_root(stat[:, 1, :])

        @block.scalar
        def _(act):
            act.wait_ge(span_ready, 1)
            wide = act.value_load(is_wide[0:1, 0:1], min_val=0, max_val=1)
            with act.If(wide):
                scalar_program(act, WIDE)
            with act.Else():
                scalar_program(act, NARROW)

        def vector_program(dve, path, steps_before):
            STEPS = path.steps
            v = nc.vector
            steps = [steps_before]

            def link(ins):
                steps[0] += 1
                ins.then_inc(dve_step, 1)
                dve.wait_ge(dve_step, steps[0])

            def narrow_tables():
                for b in range(WB):
                    for h in range(2):
                        link(v.tensor_scalar(out=base_i.bitcast(F32), in0=base_f, scalar1=half_ids[:, b, h:h + 1],
                                             scalar2=0.0, op0=ALU.is_le, op1=ALU.add,
                                             accum_out=items_up_to[:, 0, b, h:h + 1]))
                v.nop().then_inc(runs_ready, 1)
                dve.wait_ge(tables_in, 64)
                link(v.tensor_scalar(first_dst, first_dst, HALF.bit_length() - 1, (HALF // GROUP).bit_length() - 1,
                                     ALU.arith_shift_right, ALU.arith_shift_left))
                link(v.tensor_scalar(quarter_t.bitcast(I32), dst_i, NG.bit_length() - 1, None, ALU.arith_shift_right))
                link(v.tensor_tensor(quarter_t, quarter_t.bitcast(I32), first_dst, ALU.subtract))
                link(v.tensor_scalar(place_t.bitcast(I32), dst_i, NG - 1, None, ALU.bitwise_and))
                link(v.tensor_copy(place_t, place_t.bitcast(I32)))
                link(v.tensor_scalar(coord_t, coord_t, 3.0, 0.0, ALU.mult, ALU.max))
                link(v.tensor_scalar(coord_t, coord_t, 3.0, None, ALU.min))
                now, before = win_now[0:path.blocks].bitcast(I32), win_before[0:path.blocks].bitcast(I32)
                link(v.tensor_scalar(now, now, HALF.bit_length() - 1, None, ALU.arith_shift_right))
                link(v.tensor_scalar(before, before, HALF.bit_length() - 1, None, ALU.arith_shift_right))
                link(v.tensor_tensor(goes_on[0:path.blocks], now, before, ALU.is_equal))
                v.nop().then_inc(tables_ready, 1)

            def run_ends():
                dve.wait_ge(runs_in, 32)
                nothing = float(2 * (NI - 1))
                link(v.tensor_tensor(run_exists[:], items_up_to[:, 0:2], items_up_to[:, 1:3], ALU.is_gt))
                for run in range(2):
                    link(v.tensor_scalar(run_last[:, run], items_up_to[:, run], 2.0, float(run - 2) - nothing,
                                         ALU.mult, ALU.add))
                link(v.tensor_tensor(run_last[:], run_last[:], run_exists[:], ALU.mult))
                link(v.tensor_scalar(run_last[:], run_last[:], nothing, None, ALU.add))
                link(v.tensor_copy(run_idx[:], run_last[:]))
                v.nop().then_inc(run_idx_ready, 1)

            if path.narrow:
                narrow_tables()
            else:
                dve.wait_ge(tile_end_in, 16)
                last_win_i = last_window.bitcast(I32)
                link(v.tensor_scalar(last_win_i, last_dst, J.bit_length() - 1, None, ALU.arith_shift_right))
                link(v.tensor_copy(last_dst.bitcast(F32), last_win_i))
                link(v.tensor_tensor(tile_end, tile_end, last_dst.bitcast(F32), ALU.add))
                ended = last_dst.bitcast(F32)
                for b in range(path.blocks):
                    v.tensor_scalar(out=last_window, in0=tile_end, scalar1=item_ids[:, b:b + 1], scalar2=0.0,
                                    op0=ALU.is_lt, op1=ALU.add, accum_out=tile_of[:, b:b + 1]).then_inc(dve_step, 1)
                    steps[0] += 1
                    dve.wait_ge(dve_step, steps[0])
                for b in range(WB):
                    link(v.tensor_scalar(out=last_window, in0=ended, scalar1=window_ids[:, b:b + 1], scalar2=0.0,
                                         op0=ALU.is_le, op1=ALU.add, accum_out=last_f[:, b:b + 1]))
                link(v.tensor_tensor(last_f[:], last_f[:], window_ids[:], ALU.add))
                link(v.tensor_scalar(last_idx[:], last_f[:], float(path.items - 1), None, ALU.min))
                link(v.tensor_scalar(tile_idx[:, 0:path.blocks], tile_of[:, 0:path.blocks], float(TILES - 1), None, ALU.min))
                link(v.tensor_scalar(window4[:, 0:path.blocks], tile_of[:, 0:path.blocks], float(TILES), float(1 << 20), ALU.is_ge, ALU.mult))
                link(v.tensor_tensor(tile_of[:, 0:path.blocks], item_ids[:, 0:path.blocks], tile_of[:, 0:path.blocks], ALU.subtract))
                v.scalar_tensor_tensor(window4[:, 0:path.blocks], tile_of[:, 0:path.blocks], float(NG), window4[:, 0:path.blocks], ALU.mult,
                                       ALU.add).then_inc(count_ready, 1)
                dve.wait_ge(win_loaded, 32)
                v.tensor_tensor(goes_on[0:path.blocks], win_now[0:path.blocks], win_before[0:path.blocks], ALU.is_equal).then_inc(goes_ready, 1)
                dve.wait_ge(count_ready, 1)

                base = steps[0]
                LINKS = 6

                def table_block(b):
                    if due(b):
                        dve.wait_ge(attr_in, 16 * b)
                        dve.wait_ge(rad_in, 16 * b)
                    v.tensor_copy(w4_col[:], window4[:, ds(b, 1)]).then_inc(dve_step, 1)
                    v.tensor_copy(tile_col[:], tile_idx[:, ds(b, 1)]).then_inc(col_ready, 1)
                    dve.wait_ge(src_in, 16 * (b + 1))
                    dve.wait_ge(dst_in, 16 * (b + 1))
                    dve.wait_ge(attr_in, 16 * (b + 1))
                    if due(b):
                        dve.wait_ge(item_tr, b)
                    v.tensor_copy(src_f, src_r).then_inc(dve_step, 1)
                    v.tensor_scalar(slot_i[:, 0:P], dst_r, NG.bit_length() - 1, None, ALU.arith_shift_right
                                    ).then_inc(dve_step, 1)
                    v.tensor_scalar(slot_i[:, P:2 * P], dst_r, NG - 1, None, ALU.bitwise_and).then_inc(dve_step, 1)
                    v.tensor_scalar(table_f[:, 0:3 * P], attr_r[:, 0:3 * P], 3.0, 0.0, ALU.mult, ALU.max
                                    ).then_inc(dve_step, 1)
                    dve.wait_ge(dve_step, base + b * LINKS + 5)
                    v.tensor_scalar(table_f[:, 3 * P:4 * P], slot_i[:, 0:P], w4_col[:, 0:1], None, ALU.subtract
                                    ).then_inc(rows_ready, 1)
                    v.tensor_copy(table_f[:, 4 * P:5 * P], slot_i[:, P:2 * P]).then_inc(rows_ready, 1)
                    v.tensor_scalar(table_f[:, 0:3 * P], table_f[:, 0:3 * P], 3.0, None, ALU.min).then_inc(dve_step, 1)
                    dve.wait_ge(dve_step, base + b * LINKS + 6)
                    v.nop().then_inc(rows_ready, 1)

                table_block(0)
                with dve.Fori(1, path.blocks) as b:
                    table_block(b)
                steps[0] += LINKS * path.blocks

            def scan(n, kinds):
                dve.wait_ge(part_ready, n + 1)
                dve.wait_ge(carry_loaded, 16 * (n + 1))
                if due(n):
                    dve.wait_ge(rt_ready, n)
                for kind in range(kinds):
                    part = ps[:, 7, kind * P:kind * P + P].rearrange("p (i g) -> p g i", g=NG)
                    to = R[:, kind, :].rearrange("p (i g) -> p g i", g=NG)
                    for g in range(NG):
                        v.tensor_tensor_scan(to[:, g, :], carry[:], part[:, g, :], last[:, kind, g:g + 1],
                                             ALU.mult, ALU.add).then_inc(dve_step, 1)

            def keep_last(kinds):
                return v.tensor_copy(last[:, 0:kinds, :], R[:, 0:kinds, (STEP - 1) * NG:STEP * NG])

            def slot_masks():
                v.tensor_tensor(group_hot[:], meta[:, 3, :].unsqueeze(2).to_broadcast([P, STEP, NG]),
                                tap_ids[:].unsqueeze(1).to_broadcast([P, STEP, NG]), ALU.is_equal).then_inc(dve_step, 1)
                v.tensor_tensor(place_hot[:], meta[:, 4, :].unsqueeze(2).to_broadcast([P, STEP, GROUP]),
                                tap_ids[:].unsqueeze(1).to_broadcast([P, STEP, GROUP]), ALU.is_equal
                                ).then_inc(dve_step, 1)

            dve.wait_ge(meta_loaded, 16)
            v.memset(h2_s[HID:HID + 1], 1.0).then_inc(w3_ready, 1)
            base0 = steps[0]
            MASKS = 2
            G0 = 4
            SCAN0 = 2 * NG + 1

            def sum_inputs(i, e):
                dve.wait_ge(q_done[(2 * e + 1) % 4], 4 * i + e // 2 + 1)
                if e == 0 and due(i):
                    dve.wait_ge(part_ready, i)
                four = ps[:, 4 + e % 2, :].rearrange("p (s u w) -> p s w u", s=4, u=16)
                v.tensor_reduce(sums[:, e, 0:MUL], four[:, 0], AX.X, ALU.add).then_inc(q_out[e % 2], 1)
                v.tensor_reduce(sums[:, e, MUL:CH].rearrange("p (w s) -> p s w", s=3), four[:, 1:4], AX.X,
                                ALU.add).then_inc(q_out[e % 2], 1)

            def l0_step(i, prior, with_scan):
                dve.wait_ge(meta_loaded, 16 * (i + 1))
                dve.wait_ge(sh_loaded, 16 * (i + 1))
                slot_masks()
                at = prior + MASKS

                for q4 in range(4):
                    its = slice(QUART * q4, QUART * q4 + QUART)
                    dve.wait_ge(x_in[q4], 16 * QUART * (i + 1))
                    hs = xg[:, its, 0:MUL]
                    hv = xg[:, its, MUL:CH].rearrange("p n (u i) -> p n i u", i=3)
                    sh0 = meta[:, 5, its]
                    sh1 = meta[:, 6:9, its].rearrange("p i n -> p n i")
                    f_s = feat[:, its, :].rearrange("p n (s u) -> p n s u", s=4)
                    dot = dots.rearrange("p n (i u) -> p n i u", i=3)
                    v.tensor_tensor(f_s[:, :, 0, 0:MUL], hs, sh0.unsqueeze(2).to_broadcast([P, QUART, MUL]),
                                    ALU.mult).then_inc(dve_step, 1)
                    v.tensor_tensor(f_s[:, :, 1:4, MUL:2 * MUL], hv,
                                    sh0.unsqueeze(2).unsqueeze(3).to_broadcast([P, QUART, 3, MUL]),
                                    ALU.mult).then_inc(dve_step, 1)
                    v.tensor_tensor(f_s[:, :, 1:4, 0:MUL], hs.unsqueeze(2).to_broadcast([P, QUART, 3, MUL]),
                                    sh1.unsqueeze(3).to_broadcast([P, QUART, 3, MUL]), ALU.mult).then_inc(dve_step, 1)
                    v.tensor_tensor(dot, hv, sh1.unsqueeze(3).to_broadcast([P, QUART, 3, MUL]),
                                    ALU.mult).then_inc(dve_step, 1)
                    at = at + G0
                    dve.wait_ge(dve_step, at)
                    v.tensor_reduce(f_s[:, :, 0, MUL:2 * MUL], dot.rearrange("p n i u -> p n u i"), AX.X,
                                    ALU.add).then_inc(feat_ready[q4], 1)
                    dve.wait_ge(feat_ready[q4], i + 1)
                    if q4 == 3:
                        v.nop().then_inc(meta_used, 1)
                    if q4 == 0:
                        if due(i):
                            sum_inputs(i - 1, 7)
                        dve.wait_ge(dve_step, prior + MASKS)
                        if due(i):
                            dve.wait_ge(deg_done, i)
                        v.tensor_tensor(onehot[:, :, 0:J].rearrange("p n (g j) -> p n g j", g=NG),
                                        group_hot[:].unsqueeze(3).to_broadcast([P, STEP, NG, GROUP]),
                                        place_hot[:].unsqueeze(2).to_broadcast([P, STEP, NG, GROUP]), ALU.mult
                                        ).then_inc(onehot_ready, 1)
                    for q in range(4 * q4, 4 * q4 + 4):
                        par = q % 2
                        dve.wait_ge(tpw_ready[par], 8 * i + q // 2 + 1)
                        if due(4 * i + q4):
                            dve.wait_ge(q_done[q % 4], 4 * i + q4)
                        for h in range(2):
                            n = 2 * q + h
                            tpw = ps[:, 2 + par, 256 * h:256 * h + 256].rearrange("p (s u w) -> p s u w", s=2, u=16)
                            fn = feat[:, n, :].rearrange("p (s u) -> p s u", s=4)
                            pr = prod[:, q % 4, h, :].rearrange("p (s u w) -> p s u w", s=4, u=16)
                            v.tensor_tensor(pr[:, 0], tpw[:, 0], fn[:, 0].unsqueeze(2).to_broadcast([P, 16, MUL]),
                                            ALU.mult).then_inc(prod_ready[q % 4], 1)
                            v.tensor_tensor(pr[:, 1:4], tpw[:, 1].unsqueeze(1).to_broadcast([P, 3, 16, MUL]),
                                            fn[:, 1:4].unsqueeze(3).to_broadcast([P, 3, 16, MUL]),
                                            ALU.mult).then_inc(prod_ready[q % 4], 1)
                        if q >= 3 and q % 2:
                            sum_inputs(i, q // 2 - 1)
                    if q4 == 1 and with_scan:
                        scan(i - 1, 2)
                        dve.wait_ge(dve_step, at + 2 * NG)
                        keep_last(2).then_inc(dve_step, 1)
                        at = at + SCAN0
                        dve.wait_ge(dve_step, at)
                        v.nop().then_inc(R_ready, 1)

            l0_step(0, base0, False)
            l0_step(1, base0 + MASKS + 4 * G0, True)
            per0 = MASKS + 4 * G0 + SCAN0
            with dve.Fori(2, STEPS) as i:
                l0_step(i, i * per0 + (base0 - SCAN0), True)
            steps[0] = base0 - SCAN0 + STEPS * per0
            sum_inputs(STEPS - 1, 7)
            if path.narrow:
                run_ends()
            scan(STEPS - 1, 2)
            steps[0] += 2 * NG
            dve.wait_ge(dve_step, steps[0])
            link(keep_last(2))
            v.nop().then_inc(R_ready, 1)

            GATHERS = 4 * WB if path.narrow else WB
            nodes_of = lambda ap: ap.rearrange("p b (j c) -> p (b j) c", c=CH)
            rooted = [0]

            def square_root(last_ins):
                last_ins.then_inc(root_in, 1)
                rooted[0] += 1
                dve.wait_ge(root_out, rooted[0])

            def per_node(col):
                return col.unsqueeze(2).to_broadcast([P, SLOTS_W, CH])

            def per_channel(row):
                return row.unsqueeze(1).to_broadcast([P, SLOTS_W, CH])

            def layer_norm(to):
                yn, qn = nodes_of(y), nodes_of(sq)
                link(v.tensor_reduce(stat[:, 0, :], yn, AX.X, ALU.add))
                link(v.tensor_scalar(stat[:, 0, :], stat[:, 0, :], 1.0 / CH, None, ALU.mult))
                link(v.tensor_tensor(yn, yn, per_node(stat[:, 0, :]), ALU.subtract))
                link(v.tensor_tensor(qn, yn, yn, ALU.mult))
                link(v.tensor_reduce(stat[:, 1, :], qn, AX.X, ALU.add))
                square_root(v.tensor_scalar(stat[:, 1, :], stat[:, 1, :], 1.0 / CH, EPS, ALU.mult, ALU.add))
                link(v.reciprocal(stat[:, 2, :], stat[:, 1, :]))
                return v.tensor_tensor(nodes_of(to), yn, per_node(stat[:, 2, :]), ALU.mult)

            dve.wait_ge(agg_in, 16 * GATHERS)
            dve.wait_ge(cnt_in, 16 * GATHERS)
            if path.narrow:
                link(v.tensor_tensor(agg, agg, y, ALU.add))
                link(v.tensor_tensor(sq, sq, x1[:], ALU.add))
            cnt = nodes_of(sq)[:, :, 0]
            link(v.tensor_scalar(rcnt[:], cnt, 1.0, None, ALU.max))
            link(v.reciprocal(rcnt[:], rcnt[:]))
            for b in range(WB):
                par = b % 2
                dve.wait_ge(nx_ready[par], uses(par, 0) + b // 2 + 1)
                v.scalar_tensor_tensor(y[:, b, :], ps[:, 2 + par, :], MUL ** -0.5, xw[:, b, :], ALU.mult,
                                       ALU.add).then_inc(nx_used[par], 1)
                dve.wait_ge(nx_used[par], uses(par, 0) + b // 2 + 1)
                link(v.tensor_tensor(y[:, b, :], y[:, b, :], agg[:, b, :], ALU.add))
            link(layer_norm(x1))
            link(v.tensor_copy(xw[:], x1[:]))
            v.nop().then_inc(x_ready, 1)

            LINKS1 = 7
            SCAN1 = NG + 1

            def l1_step(l, i, prior, with_scan):
                n = (l + 1) * STEPS + i
                n1 = l * STEPS + i
                dve.wait_ge(meta_loaded, 16 * (n + 1))
                if due(n1):
                    for ch in range(8):
                        dve.wait_ge(bm_ready[ch], n1)
                        dve.wait_ge(xm_ready[ch], n1)
                slot_masks()
                coords = meta[:, 0:3, :].rearrange("p d n -> p n d")
                v.tensor_tensor(hat[:], coords.unsqueeze(3).to_broadcast([P, STEP, 3, 4]),
                                tap_ids[:].unsqueeze(1).unsqueeze(1).to_broadcast([P, STEP, 3, 4]),
                                ALU.subtract).then_inc(meta_used, 1)
                dve.wait_ge(meta_used, n + 1)
                v.scalar_tensor_tensor(hat2[:], hat[:], -1.0, hat[:], ALU.mult, ALU.max).then_inc(dve_step, 1)
                dve.wait_ge(dve_step, prior + 3)
                v.tensor_scalar(hat2[:], hat2[:], -1.0, 1.0, ALU.mult, ALU.add).then_inc(dve_step, 1)
                dve.wait_ge(dve_step, prior + 4)
                v.tensor_scalar(hat[:], hat2[:], 0.0, None, ALU.max).then_inc(dve_step, 1)
                dve.wait_ge(dve_step, prior + 5)
                v.tensor_tensor(b01[:].rearrange("p n (b a) -> p n b a", a=4),
                                hat[:, :, 1, :].unsqueeze(3).to_broadcast([P, STEP, 4, 4]),
                                hat[:, :, 0, :].unsqueeze(2).to_broadcast([P, STEP, 4, 4]),
                                ALU.mult).then_inc(dve_step, 1)
                dve.wait_ge(dve_step, prior + 6)
                v.tensor_tensor(b01_group[:], b01[:].unsqueeze(2).to_broadcast([P, STEP, NG, 16]),
                                group_hot[:].unsqueeze(3).to_broadcast([P, STEP, NG, 16]), ALU.mult
                                ).then_inc(dve_step, 1)
                dve.wait_ge(dve_step, prior + LINKS1)
                for ch in range(8):
                    its = slice(4 * ch, 4 * ch + 4)
                    ring = slice(4 * (ch % 4), 4 * (ch % 4) + 4)
                    if due(4 * n1 + 2 * (ch // 2) - 2):
                        dve.wait_ge(s_done[2 * (ch % 2) + 1], 4 * n1 + (ch - 4) // 2 + 1)
                    v.tensor_tensor(bm[:, ring].rearrange("p n c g a -> p n c (g a)"),
                                    b01_group[:, its].rearrange("p n g a -> p n (g a)").unsqueeze(2)
                                    .to_broadcast([P, 4, 4, NG * 16]),
                                    hat[:, its, 2, :].unsqueeze(3).to_broadcast([P, 4, 4, NG * 16]), ALU.mult
                                    ).then_inc(bm_ready[ch], 1)
                    dve.wait_ge(x_in[ch // 2], 16 * QUART * (n + 1))
                    v.tensor_tensor(xm[:, ring], xg[:, its, :].unsqueeze(2).to_broadcast([P, 4, GROUP, CH]),
                                    place_hot[:, its, :].unsqueeze(3).to_broadcast([P, 4, GROUP, CH]),
                                    ALU.mult).then_inc(xm_ready[ch], 1)
                    if ch == 4 and with_scan:
                        scan(n - 2, 1)
                        dve.wait_ge(dve_step, prior + LINKS1 + NG)
                        keep_last(1).then_inc(dve_step, 1)
                        dve.wait_ge(dve_step, prior + LINKS1 + SCAN1)
                        v.nop().then_inc(R_ready, 1)

            for l in range(LAYERS):
                base1 = steps[0]
                per1 = LINKS1 + SCAN1
                l1_step(l, 0, base1, False)
                l1_step(l, 1, base1 + LINKS1, False)
                with dve.Fori(2, STEPS) as i:
                    l1_step(l, i, i * per1 + (base1 - 2 * SCAN1), True)
                steps[0] = base1 + STEPS * per1 - 2 * SCAN1
                for n in ((l + 2) * STEPS - 2, (l + 2) * STEPS - 1):
                    scan(n, 1)
                    steps[0] += NG
                    dve.wait_ge(dve_step, steps[0])
                    link(keep_last(1))
                    v.nop().then_inc(R_ready, 1)

                dve.wait_ge(agg_in, 16 * GATHERS * (l + 2))
                if path.narrow:
                    link(v.tensor_tensor(agg, agg, y, ALU.add))
                for b in range(WB):
                    par = b % 2
                    done = uses(par, l + 1) + b // 2
                    yb = y[:, b, :].rearrange("p (j c) -> p j c", c=CH)
                    link(v.tensor_tensor(yb, agg[:, b, :].rearrange("p (j c) -> p j c", c=CH),
                                         rcnt[:, J * b:J * b + J].unsqueeze(2).to_broadcast([P, J, CH]), ALU.mult))
                    dve.wait_ge(nx_ready[par], done + 1)
                    v.tensor_tensor(y[:, b, :], ps[:, 2 + par, :], y[:, b, :], ALU.add).then_inc(nx_used[par], 1)
                    dve.wait_ge(nx_used[par], done + 1)
                    link(v.tensor_tensor(yb, yb, chan[:, l, 0, :].unsqueeze(1).to_broadcast([P, J, CH]), ALU.add))
                    if l < LAYERS - 1:
                        link(v.scalar_tensor_tensor(y[:, b, :], y[:, b, :], NEG, y[:, b, :], ALU.mult, ALU.max))
                    link(v.tensor_tensor(y[:, b, :], y[:, b, :], xw[:, b, :], ALU.add))
                    if b == WB - 1:
                        link(v.tensor_tensor(yb, yb, node_mask[:].unsqueeze(2).to_broadcast([P, J, CH]), ALU.mult))

                yn, qn = nodes_of(y), nodes_of(sq)
                v.tensor_reduce(bn[:, 0, :], yn.rearrange("p n c -> p c n"), AX.X, ALU.add).then_inc(sum_ready, 1)
                dve.wait_ge(sum_done, 2 * l + 1)
                link(v.tensor_scalar(bn[:, 1, :], ps[:, 4, 0:CH], 1.0 / nodes, None, ALU.mult))
                link(v.tensor_tensor(yn, yn, per_channel(bn[:, 1, :]), ALU.subtract))
                yb = y[:, WB - 1, :].rearrange("p (j c) -> p j c", c=CH)
                link(v.tensor_tensor(yb, yb, node_mask[:].unsqueeze(2).to_broadcast([P, J, CH]), ALU.mult))
                link(v.tensor_tensor(qn, yn, yn, ALU.mult))
                v.tensor_reduce(bn[:, 0, :], qn.rearrange("p n c -> p c n"), AX.X, ALU.add).then_inc(sum_ready, 1)
                dve.wait_ge(sum_done, 2 * l + 2)
                square_root(v.tensor_scalar(bn[:, 2, :], ps[:, 4, 0:CH], 1.0 / nodes, EPS, ALU.mult, ALU.add))
                link(v.reciprocal(bn[:, 3, :], bn[:, 2, :]))
                link(v.tensor_tensor(bn[:, 4, :], bn[:, 3, :], chan[:, l, 1, :], ALU.mult))
                link(v.tensor_tensor(yn, yn, per_channel(bn[:, 4, :]), ALU.mult))
                if l < LAYERS - 1:
                    v.tensor_tensor(nodes_of(xw), yn, per_channel(chan[:, l, 2, :]), ALU.add).then_inc(x_ready, 1)
                    dve.wait_ge(x_ready, l + 2)
            link(v.tensor_tensor(nodes_of(y), nodes_of(y), per_channel(chan[:, LAYERS - 1, 2, :]), ALU.add))
            link(v.tensor_tensor(y, y, x1[:], ALU.add))
            layer_norm(xw).then_inc(out_ready, 1)

        @block.vector
        def _(dve):
            v = nc.vector
            steps = [0]

            def link(ins):
                steps[0] += 1
                ins.then_inc(dve_step, 1)
                dve.wait_ge(dve_step, steps[0])

            dve.wait_ge(loaded, LOADS)
            v.memset(minus[:], -1.0).then_inc(minus_ready, 1)
            v.memset(zeros[:], 0.0).then_inc(runs_ready, 1)
            link(v.memset(last[:], 0.0))
            v.tensor_tensor(w3[:], w3[:], w3_scale[:], ALU.mult).then_inc(w3_ready, 1)
            link(v.memset(onehot[:], 0.0))
            link(v.tensor_scalar(base_i, first_dst, HALF.bit_length() - 1, None, ALU.arith_shift_right))
            link(v.tensor_copy(base_f, base_i))
            link(v.tensor_copy(reach, last_dst))
            link(v.scalar_tensor_tensor(reach, base_f[:, 0:TILES], -float(HALF), reach, ALU.mult, ALU.add))
            link(v.tensor_reduce(span[:], reach, AX.X, ALU.max))
            link(v.tensor_scalar(span[:], span[:], float(J), None, ALU.is_ge))
            v.tensor_copy(is_wide[:], span[:]).then_inc(span_ready, 1)
            dve.wait_ge(span_ready, 1)
            wide = dve.value_load(is_wide[0:1, 0:1], min_val=0, max_val=1)
            with dve.If(wide):
                vector_program(dve, WIDE, steps[0])
            with dve.Else():
                vector_program(dve, NARROW, steps[0])

        def tensor_program(pe, path):
            STEPS = path.steps
            pe.wait_ge(loaded, LOADS)
            def transpose_block(b):
                pe.wait_ge(rows_ready, 3 * (b + 1))
                if due(b):
                    pe.wait_ge(item_out, 4 * b)
                for c in range(5):
                    nc.tensor.transpose(ps[:, c // 4, (c % 4) * P:(c % 4) * P + P], table_f[:, c * P:c * P + P],
                                        ident[:])
                for c in range(5, META):
                    nc.tensor.transpose(ps[:, c // 4, (c % 4) * P:(c % 4) * P + P],
                                        attr_r[:, (c - 2) * P:(c - 1) * P], ident[:])
                nc.tensor.transpose(ps[:, 2, P:2 * P], src_f, ident[:]).then_inc(item_tr, 1)

            if not path.narrow:
                transpose_block(0)
                with pe.Fori(1, path.blocks) as b:
                    transpose_block(b)

            def transpose_totals(n, kinds, bank, col):
                pe.wait_ge(R_ready, n + 1)
                if due(n):
                    pe.wait_ge(rt_out, n)
                for kind in range(kinds):
                    tr = nc.tensor.transpose(ps[:, bank, col + kind * P:col + kind * P + P], R[:, kind, :], ident[:])
                tr.then_inc(rt_ready, 1)

            def l0_spread(n, half):
                if half == 0:
                    for f in range(2):
                        pe.wait_ge(q_out[f], 8 * (n + 1))
                    if due(n):
                        pe.wait_ge(rt_out, n)
                for e in range(STEP // 8 * half, STEP // 8 * (half + 1)):
                    for jj in range(GROUP):
                        tr = nc.tensor.matmul(ps[CH * jj:CH * jj + CH, 7, J * e:J * e + J], sums[:, e, :],
                                              spread[:, jj, :], start=True, stop=True, tile_position=(0, CH * jj))
                if half == 1:
                    tr.then_inc(part_ready, 1)

            def l0_degrees(i):
                for jj in range(GROUP):
                    tr = nc.tensor.matmul(ps[CH * jj:CH * jj + CH, 7, P:2 * P], ones[:, 0:CH],
                                          onehot[:, :, jj:jj + GROUP * (NG - 1) + 1:GROUP],
                                          start=True, stop=True, tile_position=(0, CH * jj))
                tr.then_inc(deg_done, 1)

            def first_layer(i, f, half):
                if half == 0:
                    pe.wait_ge(rad_loaded[f // 2 % 2], 16 * (i + f // 4 + 1))
                    if due(4 * i + f):
                        pe.wait_ge(h1_act, 4 * i + f)
                for p in (2 * half, 2 * half + 1):
                    q = 4 * (f % 4) + p
                    tr = nc.tensor.matmul(ps[:, 0, p * P:p * P + P], w1[:, q % 8, :], rad[:, q // 8, :],
                                          start=True, stop=True)
                if half == 1:
                    tr.then_inc(h1_ready, 1)

            def second_layer(i, f, h):
                pe.wait_ge(h1_act, 4 * i + f + 1)
                if due(8 * i + 2 * f + h - 1):
                    pe.wait_ge(h2_act, 8 * i + 2 * f + h - 1)
                nc.tensor.matmul(ps[:, (1, 6)[h], :], w2[:, h, :], h1_s, start=True, stop=True).then_inc(h2_ready, 1)

            def l0_step(i, groups, with_totals):
                def third_layer(q):
                    par, f, p = q % 2, q // 4, q % 4
                    pe.wait_ge(h2_act, 8 * i + 2 * f + 2)
                    if q >= 2:
                        pe.wait_ge(prod_ready[(q - 2) % 4], 4 * (4 * i + (q - 2) // 4 + 1))
                    elif due(i):
                        pe.wait_ge(prod_ready[q + 2], 16 * i)
                    for h in range(2):
                        tr = nc.tensor.matmul(ps[:, 2 + par, 256 * h:256 * h + 256],
                                              h2_s[0:HID + 1, f % 2, h, p * P:p * P + P], w3[:],
                                              start=True, stop=True)
                    tr.then_inc(tpw_ready[par], 1)

                def item_sums(q):
                    par, e = q % 2, q // 2
                    if q == 0:
                        pe.wait_ge(onehot_ready, i + 1)
                    if par == 0 and due(4 * i + e // 2):
                        pe.wait_ge(q_out[e % 2], 2 * (4 * i + e // 2))
                    pe.wait_ge(prod_ready[q % 4], 4 * (4 * i + q // 4 + 1))
                    for h in range(2):
                        m = 2 * par + h
                        tr = nc.tensor.matmul(ps[CH * m:CH * m + CH, 4 + e % 2, :], onehot[:, 2 * q + h, :],
                                              prod[:, q % 4, h, :], start=True, stop=True, tile_position=(0, CH * m))
                    tr.then_inc(q_done[q % 4], 1)

                for q in range(16):
                    f = q // 4
                    third_layer(q)
                    if q in (1, 2) and due(i):
                        l0_spread(i - 1, q - 1)
                    if q >= 2:
                        item_sums(q - 2)
                    if q % 4 < 2 and f + 1 < groups:
                        second_layer(i, f + 1, q % 4)
                    if q % 4 >= 2 and f + 2 < groups:
                        first_layer(i, f + 2, q % 4 - 2)
                item_sums(14)
                item_sums(15)
                if due(i):
                    pe.wait_ge(R_ready, i)
                l0_degrees(i)
                if with_totals:
                    transpose_totals(i - 1, 2, 7, 256)

            pe.wait_ge(w3_ready, 2)
            for half in range(2):
                first_layer(0, 0, half)
            for h in range(2):
                second_layer(0, 0, h)
            for half in range(2):
                first_layer(0, 1, half)
            l0_step(0, 6, False)
            l0_step(1, 6, True)
            with pe.Fori(2, STEPS - 1) as i:
                l0_step(i, 6, True)
            l0_step(STEPS - 1, 4, True)
            for half in range(2):
                l0_spread(STEPS - 1, half)
            transpose_totals(STEPS - 1, 2, 7, 256)

            def node_products(phase, weights):
                for b in range(WB):
                    par = b % 2
                    done = uses(par, phase) + b // 2
                    if due(done):
                        pe.wait_ge(nt_out[par], done)
                    for g in range(NG):
                        tr = nc.tensor.transpose(ps[:, par, g * P:g * P + P], xw[:, b, g * P:g * P + P], ident[:])
                    tr.then_inc(nt_ready[par], 1)
                    pe.wait_ge(nt_out[par], done + 1)
                    if due(done):
                        pe.wait_ge(nx_used[par], done)
                    for g in range(NG):
                        tr = nc.tensor.matmul(ps[:, 2 + par, g * P:g * P + P], xt[:, par, g * P:g * P + P], weights,
                                              start=True, stop=True)
                    tr.then_inc(nx_ready[par], 1)

            pe.wait_ge(x0_loaded, 16)
            node_products(0, w_self[:])

            def item_sums(l, i, ch):
                n1 = l * STEPS + i
                pe.wait_ge(bm_ready[ch], n1 + 1)
                pe.wait_ge(xm_ready[ch], n1 + 1)
                for pair in range(2):
                    e = 2 * ch + pair
                    bank = e % 4
                    if due(4 * n1 + e // 4):
                        pe.wait_ge(s_out[bank], 4 * n1 + e // 4)
                    for h in range(2):
                        r = (2 * e + h) % 16
                        tr = nc.tensor.matmul(ps[:, bank, 256 * h:256 * h + 256], xm[:, r].rearrange("p j c -> p (j c)"),
                                              bm[:, r].rearrange("p c g a -> p (c g a)"), start=True, stop=True)
                    tr.then_inc(s_done[bank], 1)

            def tap_products(l, i, par, part8):
                if part8 == 0:
                    for bank in range(4):
                        pe.wait_ge(s_out[bank], 4 * (l * STEPS + i + 1))
                    pe.wait_ge(R_ready, (l + 1) * STEPS + i)
                for k in range(8 * part8, 8 * part8 + 8):
                    tr = nc.tensor.matmul(ps[:, 7, 0:P], w_taps[:, k, :], S[:, par, :, k // 16, :, k % 16],
                                          start=(k == 0), stop=(k == TAPS - 1), skip_group_check=True)
                if part8 == 7:
                    tr.then_inc(part_ready, 1)

            def l1_step(l, i, par, with_taps, with_totals):
                for ch in range(8):
                    item_sums(l, i, ch)
                    if with_taps:
                        tap_products(l, i - 1, 1 - par, ch)
                if with_totals:
                    transpose_totals((l + 1) * STEPS + i - 2, 1, 6, 0)

            for l in range(LAYERS):
                pe.wait_ge(w_loaded, 16 * (l + 1))
                l1_step(l, 0, 0, False, False)
                l1_step(l, 1, 1, True, False)
                with pe.Fori(2, pairs_end(path), 2) as i:
                    for par in range(2):
                        l1_step(l, i + par, par, True, True)
                for i in range(pairs_end(path), STEPS):
                    l1_step(l, i, i % 2, True, True)
                transpose_totals((l + 2) * STEPS - 2, 1, 6, 0)
                for part8 in range(8):
                    tap_products(l, STEPS - 1, (STEPS - 1) % 2, part8)
                transpose_totals((l + 2) * STEPS - 1, 1, 6, 0)
                pe.wait_ge(x_ready, l + 1)
                node_products(l + 1, w_root[:, l, :])
                for half in range(2):
                    pe.wait_ge(sum_ready, 2 * l + half + 1)
                    nc.tensor.matmul(ps[:, 4, 0:CH], ones[:], bn[:, 0, :], start=True, stop=True).then_inc(sum_done, 1)

        @block.tensor
        def _(pe):
            pe.wait_ge(span_ready, 1)
            wide = pe.value_load(is_wide[0:1, 0:1], min_val=0, max_val=1)
            with pe.If(wide):
                tensor_program(pe, WIDE)
            with pe.Else():
                tensor_program(pe, NARROW)


def prepare(inputs):
    f = np.float32
    x, src, dst = (np.asarray(inputs[k]) for k in ("x", "src", "dst"))
    nodes, edges = x.shape[0], src.shape[0]
    tiles, windows, wb, narrow, wide = sizes(nodes, edges)
    nb, ni = max(narrow.blocks, wide.blocks), narrow.steps * STEP
    d = {}
    d["x"] = np.zeros((wb * P * J, CH), f)
    d["x"][:nodes] = x
    d["src"] = src.reshape(tiles, P)
    d["dst"] = dst.reshape(tiles, P)
    d["last_dst"] = dst[P - 1::P].reshape(1, tiles)
    attr = np.concatenate([np.asarray(inputs[f"edge_attr_{k}"]) for k in (3, 4, 8)], axis=1)
    attr = attr.reshape(tiles, P, 15).transpose(0, 2, 1)
    d["attr"] = attr[:, :7].reshape(tiles, 7 * P)
    d["rad"] = np.zeros((ni, MUL * P), f)
    d["rad"][:tiles] = attr[:, 7:].reshape(tiles, MUL * P)
    far = 1 << 22
    first = np.concatenate([dst[0::P], np.full(nb * P - tiles, far, dst.dtype)])
    d["first_dst"] = first[None, :ni]
    d["first_now"] = first[:narrow.blocks * P].reshape(narrow.blocks, P)
    d["first_before"] = np.concatenate([[-HALF], first])[:narrow.blocks * P].astype(dst.dtype).reshape(narrow.blocks, P)
    for name, rows in (("src_t", d["src"]), ("dst_t", d["dst"])):
        d[name] = np.zeros((P, ni), rows.dtype)
        d[name][:, :tiles] = rows.T
    for name, c0, c1 in (("coord_t", 0, 3), ("sh_t", 3, 7)):
        by_lane = np.zeros((ni, c1 - c0, P), f)
        by_lane[:tiles] = attr[:, c0:c1]
        d[name] = by_lane.reshape(narrow.steps, STEP, c1 - c0, P).transpose(3, 0, 2, 1)
    d["coord_t"] = d["coord_t"].reshape(P, 3 * ni)
    g = lambda name: np.asarray(inputs[name])
    W1, W2, W3 = g("L0_gnn_W1"), g("L0_gnn_W2"), g("L0_gnn_W3")
    d["w1"] = np.zeros((P, 8, P), f)
    for q in range(8):
        for h in range(2):
            d["w1"][16 * q + 8 * h:16 * q + 8 * h + 8, q, HID * h:HID * h + HID] = W1
    d["w2"] = np.zeros((P, 2, P), f)
    for h in range(2):
        d["w2"][HID * h:HID * h + HID, h, :HID] = W2
    d["w3"] = np.concatenate([W3, g("L0_gnn_b3")[None]], axis=0)
    d["b1"] = np.concatenate([g("L0_gnn_b1")] * 2).reshape(P, 1)
    d["b2"] = g("L0_gnn_b2").reshape(HID, 1)
    mean = 1.0 / np.sqrt(2.0 * MUL) / np.sqrt(16.0)
    d["w3_scale"] = np.full((HID + 1, 256), mean, f)
    d["w3_scale"][:, MUL * MUL:2 * MUL * MUL] = mean / np.sqrt(3.0)
    d["spread"] = np.zeros((P, GROUP, J), f)
    for q in range(4):
        for j in range(J):
            d["spread"][CH * q + j, j % GROUP, NG * q + j // GROUP] = 1.0
    one = np.zeros((CH, CH), f)
    one[:MUL, :MUL] = g("L0_gnn_Ws")
    for i in range(3):
        one[MUL + i::3, MUL + i::3] = g("L0_gnn_Wv")
    d["w_self"] = np.zeros((P, P), f)
    d["w_root"] = np.zeros((P, 3, P), f)
    for j in range(GROUP):
        own = slice(CH * j, CH * j + CH)
        d["w_self"][own, own] = one
        for l in range(3):
            d["w_root"][own, l, own] = g(f"L1_gnn_R{l + 1}")
    for l in range(3):
        taps = np.zeros((P, TAPS, P), f)
        for j in range(GROUP):
            taps[CH * j:CH * j + CH, :, CH * j:CH * j + CH] = g(f"L1_gnn_W{l + 1}").transpose(1, 0, 2)
        d[f"w_taps{l}"] = taps
    d["chan"] = np.stack([np.stack([g(f"L1_gnn_{k}{l + 1}") for k in ("b", "g", "be")]) for l in range(3)])[None]
    rows = np.ones((P, 1), f)
    d["ident"] = np.eye(P, dtype=f)
    d["ones"] = np.ones((P, P), f)
    d["tap_ids"] = rows * np.arange(4, dtype=f)
    d["item_ids"] = np.arange(nb * P, dtype=f).reshape(nb, P).T
    d["half_ids"] = (2 * np.arange(wb * P, dtype=f).reshape(wb, P).T[:, :, None] + np.arange(2, dtype=f))
    d["window_ids"] = np.arange(wb * P, dtype=f).reshape(wb, P).T
    d["tile_ids"] = np.arange(tiles, dtype=f).reshape(1, tiles)
    node = ((wb - 1) * P + np.arange(P)[:, None]) * J + np.arange(J)
    d["node_mask"] = (node < nodes).astype(f)
    return nodes, edges, {k: np.ascontiguousarray(v_) for k, v_ in d.items()}


def kernel(**inputs):
    import concourse.bacc as bacc
    from concourse.bass_utils import run_bass_kernel_spmd

    nodes, edges, data = prepare(inputs)
    nc = bacc.Bacc("TRN2", target_bir_lowering=False, num_devices=1)
    arrays, args = {}, {}
    for name, v_ in data.items():
        arrays[f"in_{name}"] = v_
        args[name] = nc.dram_tensor(f"in_{name}", v_.shape, mybir.dt.from_np(v_.dtype), kind="ExternalInput").ap()
    out = nc.dram_tensor("out_nodes", data["x"].shape, mybir.dt.float32, kind="ExternalOutput").ap()
    graph_kernel(nc, nodes, edges, args, out)
    got = run_bass_kernel_spmd(nc, [arrays], core_ids=[0])
    return got.results[0]["out_nodes"][:nodes]
```

```python
from collections import namedtuple
from contextlib import ExitStack

import concourse.bass as bass
import numpy as np
from concourse import mybir

P = 128
CH = 32
J = 16
HALF = J // 2
GROUP = 4
NG = J // GROUP
TAPS = 64
HID = 64
MUL = 8
ROW = J * CH
TPW = (2, 3, 5, 6)
SUMS = (1, 4)
STEP = 32
QUART = 8
NEG = 0.01
EPS = 1e-5
BANK = 512


Path = namedtuple("Path", "narrow items steps blocks")


def sizes(nodes, edges):
    tiles = edges // P
    windows = -(-nodes // J)

    def path(narrow, items):
        steps = -(-items // STEP)
        return Path(narrow, items, steps, -(-steps * STEP // P))

    return tiles, -(-windows // P), path(True, tiles + 1), path(False, tiles + windows)


def graph_kernel(nc, nodes, edges, a, out):
    F32, I32 = mybir.dt.float32, mybir.dt.int32
    ALU, ACT, AX = mybir.AluOpType, mybir.ActivationFunctionType, mybir.AxisListType
    TILES, WB, NARROW, WIDE = sizes(nodes, edges)
    NB = max(NARROW.blocks, WIDE.blocks)
    NI = NARROW.steps * STEP
    SLOTS_W = WB * J
    NODE_F = WB * ROW
    ATTR = 15
    META = 9
    LAYERS = 3
    ds = bass.ds

    def dram(name, shape, dt):
        return nc.dram_tensor(name, shape, dt, kind="Internal").ap()

    src_items = dram("src_items", [P, NB * P], I32)
    meta_items = dram("meta_items", [P, NB * 4, META, STEP], F32)
    rad_items = dram("rad_items", [NB * P, MUL * P], F32)
    window_items = dram("window_items", [1 + NB * P], F32)
    carry_items = dram("carry_items", [NB * P], F32)
    agg_rows = dram("agg_rows", [NB * P, ROW], F32)
    cnt_rows = dram("cnt_rows", [NB * P, ROW], F32)
    run_counts = dram("run_counts", [2 + 2 * WB * P], F32)
    x_rows = dram("x_rows", [WB * P * J, CH], F32)

    ctx = ExitStack()
    with ctx:
        def sb(name, shape, dt=F32):
            return ctx.enter_context(nc.sbuf_tensor(name, shape, dt))

        def sem(name):
            return ctx.enter_context(nc.semaphore(name))

        def sems(name, n):
            return [sem(f"{name}{i}") for i in range(n)]

        ident = sb("ident", [P, P])
        ones = sb("ones", [P, P])
        slot_ids = sb("slot_ids", [P, J])
        item_ids = sb("item_ids", [P, NB])
        window_ids = sb("window_ids", [P, WB])
        node_mask = sb("node_mask", [P, J])
        w1 = sb("w1", [P, 8, P])
        w2 = sb("w2", [P, P])
        w3 = sb("w3", [HID + 1, 256])
        w3_scale = sb("w3_scale", [HID + 1, 256])
        b1 = sb("b1", [P, 1])
        b2 = sb("b2", [P, 1])
        spread = sb("spread", [P, GROUP, J])
        w_self = sb("w_self", [P, P])
        w_root = sb("w_root", [P, LAYERS, P])
        chan = sb("chan", [P, LAYERS, 3, CH])
        w_taps = sb("w_taps", [P, TAPS, P])

        tile_of = sb("tile_of", [P, NB])
        window4 = sb("window4", [P, NB])
        tile_idx = sb("tile_idx", [P, NB], I32)
        last_f = sb("last_f", [P, WB])
        last_idx = sb("last_idx", [P, WB], I32)
        tile_col = sb("tile_col", [P, 1], I32)
        w4_col = sb("w4_col", [P, 1])
        win_now = sb("win_now", [NB, P])
        win_before = sb("win_before", [NB, P])
        goes_on = sb("goes_on", [NB, P])
        minus = sb("minus", [1, 1])
        zeros = sb("zeros", [1, 2])
        half_ids = sb("half_ids", [P, WB, 2])
        items_up_to = sb("items_up_to", [P, 3, WB, 2])
        run_last = sb("run_last", [P, 2, WB, 2])
        run_exists = sb("run_exists", [P, 2, WB, 2])
        run_idx = sb("run_idx", [P, 2, WB, 2], I32)
        span = sb("span", [P, 1])
        is_wide = sb("is_wide", [P, 1], I32)

        idx = sb("idx", [P, STEP], I32)
        meta = sb("meta", [P, META, STEP])
        carry = sb("carry", [P, STEP])
        xg = sb("xg", [P, STEP, CH])
        group_hot = sb("group_hot", [P, STEP, NG])
        place_hot = sb("place_hot", [P, STEP, GROUP])
        slot = sb("slot", [P, STEP])
        onehot = sb("onehot", [P, STEP, CH])
        hat = sb("hat", [P, STEP, 3, 4])
        hat2 = sb("hat2", [P, STEP, 3, 4])
        b01 = sb("b01", [P, STEP, 16])
        b01_group = sb("b01_group", [P, STEP, NG, 16])
        R = sb("R", [P, 2, STEP * NG])
        last = sb("last", [P, 2, NG])
        rts = sb("rts", [P, 2, P])

        xw = sb("xw", [P, WB, ROW])
        x1 = sb("x1", [P, WB, ROW])
        rcnt = sb("rcnt", [P, SLOTS_W])
        stat = sb("stat", [P, 4, SLOTS_W])
        bn = sb("bn", [P, 6, CH])
        xt = sb("xt", [P, 2, BANK])

        S_F = STEP * NG * TAPS
        XM_F = 16 * NG * TAPS
        L0_F = 16 * ROW + STEP * 64 + 2 * QUART * 24 + 5 * BANK + 2 * P + STEP // 4 * CH
        RUNS_AT = max(4 * NI + TILES, L0_F)
        BIG = max(RUNS_AT + 2 * NI, 3 * TILES, 2 * S_F + XM_F + 16 * P, 3 * NODE_F, (ATTR + 9 + 2 * META) * P)
        big = sb("big", [P, BIG])
        last_dst = big[:, 0:TILES].bitcast(I32)
        first_dst = big[:, NI:2 * NI].bitcast(I32)
        base_i = big[:, RUNS_AT:RUNS_AT + NI].bitcast(I32)
        base_f = big[:, RUNS_AT + NI:RUNS_AT + 2 * NI]
        reach = big[:, 4 * NI:4 * NI + TILES]
        dst_i = big[:, 0:NI].bitcast(I32)
        quarter_t = big[:, 2 * NI:3 * NI]
        place_t = big[:, 3 * NI:4 * NI]
        last_window = big[:, TILES:2 * TILES]
        tile_end = big[:, 2 * TILES:3 * TILES]
        src_r = big[:, 0:P].bitcast(I32)
        dst_r = big[:, P:2 * P].bitcast(I32)
        attr_r = big[:, 2 * P:(2 + ATTR) * P]
        at = 2 + ATTR
        src_f = big[:, at * P:(at + 1) * P]
        slot_i = big[:, (at + 1) * P:(at + 3) * P].bitcast(I32)
        table_f = big[:, (at + 3) * P:(at + 8) * P]
        src_t = big[:, (at + 8) * P:(at + 9) * P].bitcast(I32)
        meta_flat = big[:, (at + 9) * P:(at + 9 + META) * P]
        meta_t = meta_flat.rearrange("p (n c i) -> p n c i", n=4, c=META)
        def part(at, shape):
            n = int(np.prod(shape))
            flat = big[:, at:at + n]
            if len(shape) == 1:
                return flat, at + n
            names = "abcde"[:len(shape)]
            return flat.rearrange(f"p ({' '.join(names)}) -> p {' '.join(names)}", **dict(zip(names, shape))), at + n

        prod, at = part(0, (8, 2, ROW))
        feat, at = part(at, (STEP, 64))
        dots, at = part(at, (2 * QUART, 24))
        h1_s, at = part(at, (BANK,))
        h2_s, at = part(at, (2, 2, BANK))
        rad, at = part(at, (2, P))
        sums, at = part(at, (STEP // 4, CH))
        S, at = part(0, (2, STEP, 4, NG, 16))
        bm, at = part(at, (16, 4, NG, 16))
        xm, at = part(at, (16, GROUP, CH))
        agg, at = part(0, (WB, ROW))
        y, at = part(at, (WB, ROW))
        sq, at = part(at, (WB, ROW))

        ps = ctx.enter_context(nc.psum_tensor("ps", [P, 8, BANK], F32))

        loaded, w_loaded, x0_loaded = sem("loaded"), sem("w_loaded"), sem("x0_loaded")
        dve_step = sem("dve_step")
        gathers_go, loads_go = sem("gathers_go"), sem("loads_go")
        count_ready, span_ready = sem("count_ready"), sem("span_ready")
        tables_in, tables_ready = sem("tables_in"), sem("tables_ready")
        tile_end_in, runs_ready, runs_stored = sem("tile_end_in"), sem("runs_ready"), sem("runs_stored")
        runs_in, run_idx_ready = sem("runs_in"), sem("run_idx_ready")
        attr_loaded = sem("attr_loaded")
        win_stored, win_loaded, goes_ready, goes_stored = (sem("win_stored"), sem("win_loaded"),
                                                           sem("goes_ready"), sem("goes_stored"))
        minus_ready = sem("minus_ready")
        col_ready, src_in, dst_in, attr_in = sem("col_ready"), sem("src_in"), sem("dst_in"), sem("attr_in")
        rad_in = sem("rad_in")
        rows_ready, item_tr, item_out = sem("rows_ready"), sem("item_tr"), sem("item_out")
        meta_stored, src_stored, rad_stored = sem("meta_stored"), sem("src_stored"), sem("rad_stored")
        idx_loaded, x_in = sems("idx_loaded", 2), sems("x_in", 4)
        meta_loaded, carry_loaded, rad_loaded = sem("meta_loaded"), sem("carry_loaded"), sems("rad_loaded", 2)
        meta_used = sem("meta_used")
        onehot_ready, feat_ready = sem("onehot_ready"), sems("feat_ready", 2)
        h1_ready, h1_act, h2_ready, h2_act = sem("h1_ready"), sem("h1_act"), sem("h2_ready"), sem("h2_act")
        tpw_ready, prod_ready, q_done, q_out = (sems("tpw_ready", 4), sems("prod_ready", 8),
                                                sems("q_done", 8), sem("q_out"))
        deg_done, w3_ready = sem("deg_done"), sem("w3_ready")
        bm_ready, xm_ready, s_done, s_out = (sems("bm_ready", 8), sems("xm_ready", 8),
                                             sems("s_done", 4), sems("s_out", 4))
        part_ready, R_ready, rt_ready, rt_out = sem("part_ready"), sem("R_ready"), sem("rt_ready"), sem("rt_out")
        rows_stored = sem("rows_stored")
        agg_in, cnt_in = sems("agg_in", WB), sems("cnt_in", WB)
        nt_ready, nt_out = sems("nt_ready", 2), sems("nt_out", 2)
        nx_ready, nx_used = sems("nx_ready", 2), sems("nx_used", 2)
        sum_ready, sum_done, root_in, root_out = sem("sum_ready"), sem("sum_done"), sem("root_in"), sem("root_out")
        x_ready, x_stored, out_ready, out_stored = (sem("x_ready"), sem("x_stored"), sem("out_ready"),
                                                    sem("out_stored"))

        consts = [(ident, "ident"), (ones, "ones"), (slot_ids, "slot_ids"), (item_ids, "item_ids"),
                  (window_ids, "window_ids"), (node_mask, "node_mask"), (w1, "w1"), (w2, "w2"), (w3, "w3"),
                  (w3_scale, "w3_scale"), (b1, "b1"), (b2, "b2"), (spread, "spread"), (w_self, "w_self"),
                  (w_root, "w_root"), (half_ids, "half_ids")]
        LOADS = 16 * (len(consts) + 3)

        def rows0(path):
            return 2 * 16 * path.steps

        def pairs_end(path):
            return 2 + 2 * ((path.steps - 2) // 2)

        def uses(parity, phase):
            return phase * ((WB + 1) // 2 if parity == 0 else WB // 2)

        def due(value):
            return not isinstance(value, int) or value > 0

        block = ctx.enter_context(nc.Block())

        def sync_program(sp, path):
            STEPS = path.steps
            if path.narrow:
                sp.dma_start(dst_i, a["dst_t"]).then_inc(tables_in, 16)
                sp.dma_start(win_now[0:path.blocks].bitcast(I32), a["first_now"]).then_inc(tables_in, 16)
                sp.dma_start(win_before[0:path.blocks].bitcast(I32), a["first_before"]).then_inc(tables_in, 16)
            else:
                sp.dma_start(tile_end, a["tile_ids"].to_broadcast([P, TILES])).then_inc(tile_end_in, 16)
                sp.wait_ge(minus_ready, 1)
                sp.dma_start(window_items[0:1].rearrange("(a b) -> a b", a=1), minus[:]).then_inc(win_stored, 16)
                sp.wait_ge(count_ready, 1)
                with nc.allow_non_contiguous_dma(reason="one column per block of items"):
                    sp.dma_start(window_items[1:1 + WIDE.blocks * P].rearrange("(b p) -> p b", p=P),
                                 tile_of[:, 0:WIDE.blocks]).then_inc(win_stored, 16)
                sp.wait_ge(win_stored, 32)
                for shift, rows in enumerate((win_before, win_now)):
                    sp.dma_start(rows[0:WIDE.blocks], window_items[shift:shift + WIDE.blocks * P]
                                 .rearrange("(b p) -> b p", p=P)).then_inc(win_loaded, 16)
                sp.wait_ge(goes_ready, 1)
                sp.dma_start(carry_items[0:WIDE.blocks * P].rearrange("(b p) -> b p", p=P),
                             goes_on[0:WIDE.blocks]).then_inc(goes_stored, 16)

                def store_block(b):
                    sp.wait_ge(rad_in, 16 * (b + 1))
                    sp.dma_start(rad_items[ds(b * P, P), :], attr_r[:, 7 * P:15 * P]).then_inc(rad_stored, 16)
                    sp.wait_ge(item_out, 4 * (b + 1))
                    sp.dma_start(meta_items[:, ds(b * 4, 4), :, :].rearrange("p n c i -> p (n c i)"),
                                 meta_flat).then_inc(meta_stored, 16)
                    sp.dma_start(src_items[:, ds(b * P, P)], src_t).then_inc(src_stored, 16)

                store_block(0)
                with sp.Fori(1, WIDE.blocks) as b:
                    store_block(b)
                sp.wait_ge(rad_stored, 16 * WIDE.blocks)
                sp.wait_ge(meta_stored, 16 * WIDE.blocks)
                sp.wait_ge(src_stored, 16 * WIDE.blocks)
                sp.wait_ge(goes_stored, 16)
            src_table = a["src_t"] if path.narrow else src_items
            sh_table = a["sh_t"] if path.narrow else meta_items[:, :, 5:META, :]
            coord_table = a["coord_t"] if path.narrow else meta_items[:, :, 0:3, :]
            rad_table = a["rad"] if path.narrow else rad_items

            def load_indices(n, i):
                for half in range(2):
                    for q in (2 * half, 2 * half + 1):
                        if due(n):
                            sp.wait_ge(x_in[q], 16 * QUART * n)
                    sp.sem_inc(loads_go, 1)
                    sp.dma_start(idx[:, 16 * half:16 * half + 16],
                                 src_table[:, ds(i * STEP + 16 * half, 16)]).then_inc(idx_loaded[half], 16)

            def load_meta(n, i, table, first, end):
                if due(n):
                    sp.wait_ge(meta_used, n)
                sp.sem_inc(loads_go, 1)
                sp.dma_start(meta[:, 3:5, :], meta_items[:, ds(i, 1), 3:5, :].rearrange("p n c i -> p (n c) i")
                             ).then_inc(meta_loaded, 16)
                sp.dma_start(meta[:, first:end, :], table[:, ds(i, 1), :, :].rearrange("p n c i -> p (n c) i")
                             ).then_inc(attr_loaded, 16)

            def load_carry(n, i):
                if due(n):
                    sp.wait_ge(R_ready, n)
                sp.sem_inc(loads_go, 1)
                sp.dma_start(carry[:], carry_items[ds(i * STEP, STEP)].rearrange("(o i) -> o i", o=1)
                             .to_broadcast([P, STEP])).then_inc(carry_loaded, 16)

            def load_radials(i, half):
                if due(i):
                    sp.wait_ge(h1_ready, 4 * i - 2 + 2 * half)
                sp.sem_inc(loads_go, 1)
                sp.dma_start(rad[:, half], rad_table[ds(i * STEP + 16 * half, 16), :]
                             .rearrange("n (k f) -> (n k) f", k=MUL)).then_inc(rad_loaded[half], 16)

            def store_tables():
                sp.wait_ge(tables_ready, 1)
                by_step = meta_items[:, 0:STEPS]
                with nc.allow_non_contiguous_dma(reason="the channels of an iteration lie together"):
                    sp.dma_start(by_step[:, :, 3, :], quarter_t.rearrange("p (n i) -> p n i", i=STEP)
                                 ).then_inc(meta_stored, 16)
                    sp.dma_start(by_step[:, :, 4, :], place_t.rearrange("p (n i) -> p n i", i=STEP)
                                 ).then_inc(meta_stored, 16)
                sp.dma_start(carry_items[0:path.blocks * P].rearrange("(b p) -> b p", p=P),
                             goes_on[0:path.blocks]).then_inc(goes_stored, 16)
                sp.wait_ge(meta_stored, 32)
                sp.wait_ge(goes_stored, 16)

            def store_runs():
                sp.wait_ge(runs_ready, 2)
                sp.dma_start(run_counts[0:2].rearrange("(a b) -> a b", a=1), zeros[:]).then_inc(runs_stored, 16)
                sp.dma_start(run_counts[2:2 + 2 * WB * P].rearrange("(b p h) -> p b h", p=P, h=2),
                             items_up_to[:, 0]).then_inc(runs_stored, 16)
                sp.wait_ge(runs_stored, 32)
                for before in (1, 2):
                    sp.dma_start(items_up_to[:, before], run_counts[2 - before:2 - before + 2 * WB * P]
                                 .rearrange("(b p h) -> p b h", p=P, h=2)).then_inc(runs_in, 16)

            load_radials(0, 0)
            load_indices(0, 0)
            load_radials(0, 1)
            if path.narrow:
                store_tables()
            load_meta(0, 0, sh_table, 5, META)
            if path.narrow:
                store_runs()
            with sp.Fori(1, STEPS) as i:
                load_radials(i, 0)
                load_indices(i, i)
                load_radials(i, 1)
                load_meta(i, i, sh_table, 5, META)
                load_carry(i - 1, i - 1)
            load_carry(STEPS - 1, STEPS - 1)

            def store_nodes(table, ready, before, stored):
                for b in range(WB):
                    sp.wait_ge(ready, before + b + 1)
                    sp.dma_start(table[b * P * J:(b + 1) * P * J, :].rearrange("(p j) c -> p (j c)", j=J),
                                 xw[:, b, :]).then_inc(stored, 16)

            store_nodes(x_rows, x_ready, 0, x_stored)
            for l in range(LAYERS):
                base = (l + 1) * STEPS
                if l:
                    sp.wait_ge(part_ready, base)
                    sp.dma_start(w_taps[:], a[f"w_taps{l}"]).then_inc(w_loaded, 16)
                    store_nodes(x_rows, x_ready, WB * l, x_stored)
                for i in range(2):
                    load_meta(base + i, i, coord_table, 0, 3)
                    load_indices(base + i, i)
                with sp.Fori(2, STEPS) as i:
                    load_meta(base + i, i, coord_table, 0, 3)
                    load_indices(base + i, i)
                    load_carry(base + i - 2, i - 2)
                for i in (STEPS - 2, STEPS - 1):
                    load_carry(base + i, i)
            store_nodes(out, out_ready, 0, out_stored)
            sp.wait_ge(out_stored, 16 * WB)

        @block.sync
        def _(sp):
            for tile_, name in consts:
                sp.dma_start(tile_[:], a[name]).then_inc(loaded, 16)
            sp.dma_start(chan[:], a["chan"].to_broadcast([P, LAYERS, 3, CH])).then_inc(loaded, 16)
            sp.dma_start(last_dst, a["last_dst"].to_broadcast([P, TILES])).then_inc(loaded, 16)
            sp.dma_start(first_dst, a["first_dst"].to_broadcast([P, NI])).then_inc(loaded, 16)
            x_by_window = a["x"].rearrange("(b p j) c -> p b (j c)", p=P, j=J)
            sp.dma_start(xw[:], x_by_window).then_inc(x0_loaded, 16)
            sp.dma_start(w_taps[:], a["w_taps0"]).then_inc(w_loaded, 16)

            sp.wait_ge(span_ready, 1)
            wide = sp.value_load(is_wide[0:1, 0:1], min_val=0, max_val=1)
            with sp.If(wide):
                sync_program(sp, WIDE)
            with sp.Else():
                sync_program(sp, NARROW)

        def pool_program(pool, path):
            STEPS = path.steps
            def gather(dst_tile, table, index):
                return nc.gpsimd.indirect_dma_start(
                    out=dst_tile, out_offset=None, in_=table,
                    in_offset=bass.IndirectOffsetOnAxis(ap=index, axis=0))

            def gather_block(b):
                pool.wait_ge(col_ready, b + 1)
                if due(b):
                    pool.wait_ge(item_tr, b)
                    pool.wait_ge(rad_stored, 16 * b)
                pool.sem_inc(gathers_go, 1)
                gather(src_r, a["src"], tile_col[:]).then_inc(src_in, 16)
                gather(dst_r, a["dst"], tile_col[:]).then_inc(dst_in, 16)
                gather(attr_r[:, 0:7 * P], a["attr"], tile_col[:]).then_inc(attr_in, 16)
                gather(attr_r[:, 7 * P:15 * P], a["rad"], tile_col[:]).then_inc(rad_in, 16)

            if not path.narrow:
                gather_block(0)
                with pool.Fori(1, path.blocks) as b:
                    gather_block(b)

            def gather_sources(table, n, group_free):
                for q in range(4):
                    if q % 2 == 0:
                        pool.wait_ge(idx_loaded[q // 2], 16 * (n + 1))
                    group_free(q)
                    pool.sem_inc(gathers_go, 1)
                    for r in range(QUART):
                        s = QUART * q + r
                        gather(xg[:, s, :], table, idx[:, s:s + 1]).then_inc(x_in[q], 16)

            def window_totals(table, into, beside, done):
                by_half = table[0:NI, :].rearrange("i (h f) -> (i h) f", h=2)
                for b in range(WB):
                    if path.narrow:
                        for run, to in enumerate((into, beside)):
                            for h in range(2):
                                gather(to[:, b, ROW // 2 * h:ROW // 2 * (h + 1)], by_half,
                                       run_idx[:, run, b, h:h + 1]).then_inc(done[b], 16)
                    else:
                        gather(into[:, b, :], table[0:STEPS * STEP, :], last_idx[:, b:b + 1]).then_inc(done[b], 16)

            gather_sources(a["x"], 0, lambda q: None)
            with pool.Fori(1, STEPS) as i:
                gather_sources(a["x"], i, lambda q: pool.wait_ge(feat_ready[q // 2], i))
            pool.wait_ge(rows_stored, rows0(path))
            pool.wait_ge(part_ready, STEPS)
            if path.narrow:
                pool.wait_ge(run_idx_ready, 1)
            pool.sem_inc(gathers_go, 1)
            window_totals(cnt_rows, sq, x1, cnt_in)
            window_totals(agg_rows, agg, y, agg_in)
            for l in range(LAYERS):
                pool.wait_ge(x_stored, 16 * WB * (l + 1))
                gather_sources(x_rows, (l + 1) * STEPS,
                               lambda q: pool.wait_ge(xm_ready[2 * q + 1], l * STEPS) if l else None)
                with pool.Fori(1, STEPS) as i:
                    gather_sources(x_rows, (l + 1) * STEPS + i,
                                   lambda q: pool.wait_ge(xm_ready[2 * q + 1], l * STEPS + i))
                pool.wait_ge(rows_stored, rows0(path) + 16 * STEPS * (l + 1))
                pool.wait_ge(part_ready, (l + 2) * STEPS)
                window_totals(agg_rows, agg, y, agg_in)

        @block.gpsimd
        def _(pool):
            pool.wait_ge(span_ready, 1)
            wide = pool.value_load(is_wide[0:1, 0:1], min_val=0, max_val=1)
            with pool.If(wide):
                pool_program(pool, WIDE)
            with pool.Else():
                pool_program(pool, NARROW)

        def scalar_program(act, path):
            STEPS = path.steps
            act.wait_ge(loaded, LOADS)
            def copy_block(b):
                act.wait_ge(item_tr, b + 1)
                if due(b):
                    act.wait_ge(meta_stored, 16 * b)
                    act.wait_ge(src_stored, 16 * b)
                nc.scalar.copy(meta_t[:, :, 0:4, :].rearrange("p n c i -> p c n i"),
                               ps[:, 0, :].rearrange("p (c n i) -> p c n i", c=4, n=4)).then_inc(item_out, 1)
                nc.scalar.copy(meta_t[:, :, 4:8, :].rearrange("p n c i -> p c n i"),
                               ps[:, 1, :].rearrange("p (c n i) -> p c n i", c=4, n=4)).then_inc(item_out, 1)
                nc.scalar.copy(meta_t[:, :, 8, :], ps[:, 2, 0:P].rearrange("p (n i) -> p n i", n=4)
                               ).then_inc(item_out, 1)
                nc.scalar.copy(src_t, ps[:, 2, P:2 * P]).then_inc(item_out, 1)

            if not path.narrow:
                copy_block(0)
                with act.Fori(1, path.blocks) as b:
                    copy_block(b)

            def store_rows(n, kinds, bank, col, stored):
                act.wait_ge(rt_ready, n + 1)
                if due(stored):
                    act.wait_ge(rows_stored, stored)
                nc.scalar.copy(rts[:, 0:kinds, :], ps[:, bank, col:col + kinds * P].rearrange("p (k f) -> p k f", k=kinds)
                               ).then_inc(rt_out, 1)
                act.wait_ge(rt_out, n + 1)

            def rows_at(table, i):
                return table[ds(i * STEP, STEP), :].rearrange("i (g f) -> (i g) f", g=NG)

            def first_layer(i, f):
                act.wait_ge(h1_ready, 4 * i + f + 1)
                if due(4 * i + f):
                    act.wait_ge(h2_ready, 4 * i + f)
                nc.scalar.activation(h1_s, ps[:, 0, :], ACT.Silu, bias=b1[:, 0:1]).then_inc(h1_act, 1)

            def second_layer(i, f):
                act.wait_ge(h2_ready, 4 * i + f + 1)
                if due(4 * i + f - 1):
                    act.wait_ge(tpw_ready[3], 4 * i + f - 1)
                for h in range(2):
                    own = slice(HID * h, HID * h + HID)
                    nc.scalar.activation(h2_s[0:HID, f % 2, h, :], ps[own, 0, :], ACT.Silu,
                                         bias=b2[own, 0:1]).then_inc(h2_act, 1)

            def l0_step(i, groups):
                for f in range(4):
                    if f + 2 < groups:
                        second_layer(i, f + 2)
                    if f + 3 < groups:
                        first_layer(i, f + 3)

            def l0_rows(i):
                store_rows(i, 2, 7, 256, 32 * i)
                act.dma_start(rows_at(agg_rows, i), rts[:, 0, :]).then_inc(rows_stored, 16)
                act.dma_start(rows_at(cnt_rows, i), rts[:, 1, :]).then_inc(rows_stored, 16)

            first_layer(0, 0)
            for f in range(2):
                second_layer(0, f)
                first_layer(0, f + 1)
            l0_step(0, 7)
            l0_step(1, 7)
            l0_rows(0)
            with act.Fori(2, STEPS - 1) as i:
                l0_step(i, 7)
                l0_rows(i - 1)
            l0_step(STEPS - 1, 4)
            l0_rows(STEPS - 2)
            l0_rows(STEPS - 1)

            roots = [0]

            def square_root(col):
                roots[0] += 1
                act.wait_ge(root_in, roots[0])
                nc.scalar.activation(col, col, ACT.Sqrt).then_inc(root_out, 1)

            def node_copies(phase):
                for b in range(WB):
                    par = b % 2
                    done = uses(par, phase) + b // 2
                    act.wait_ge(nt_ready[par], done + 1)
                    if due(done):
                        act.wait_ge(nx_ready[par], done)
                    nc.scalar.copy(xt[:, par, :], ps[:, par, :]).then_inc(nt_out[par], 1)

            node_copies(0)
            for b in range(WB):
                square_root(stat[:, 1, J * b:J * b + J])

            def l1_step(l, i, par):
                for e in range(16):
                    bank = e % 4
                    if e == 0:
                        act.wait_ge(part_ready, (l + 1) * STEPS + i - 1)
                    act.wait_ge(s_done[bank], 4 * (l * STEPS + i) + e // 4 + 1)
                    nc.scalar.copy(S[:, par, 2 * e:2 * e + 2].rearrange("p n c g a -> p (n c g a)"), ps[:, bank, :]
                                   ).then_inc(s_out[bank], 1)

            def l1_rows(l, i):
                n = (l + 1) * STEPS + i
                store_rows(n, 1, 6, 0, rows0(path) + 16 * (n - STEPS))
                act.dma_start(rows_at(agg_rows, i), rts[:, 0, :]).then_inc(rows_stored, 16)

            for l in range(LAYERS):
                l1_step(l, 0, 0)
                l1_step(l, 1, 1)
                with act.Fori(2, pairs_end(path), 2) as i:
                    for par in range(2):
                        l1_step(l, i + par, par)
                        l1_rows(l, i + par - 2)
                for i in range(pairs_end(path), STEPS):
                    l1_step(l, i, i % 2)
                    l1_rows(l, i - 2)
                for i in (STEPS - 2, STEPS - 1):
                    l1_rows(l, i)
                node_copies(l + 1)
                square_root(bn[:, 2, :])
            for b in range(WB):
                square_root(stat[:, 1, J * b:J * b + J])

        @block.scalar
        def _(act):
            act.wait_ge(span_ready, 1)
            wide = act.value_load(is_wide[0:1, 0:1], min_val=0, max_val=1)
            with act.If(wide):
                scalar_program(act, WIDE)
            with act.Else():
                scalar_program(act, NARROW)

        def vector_program(dve, path, steps_before):
            STEPS = path.steps
            v = nc.vector
            steps = [steps_before]

            def link(ins):
                steps[0] += 1
                ins.then_inc(dve_step, 1)
                dve.wait_ge(dve_step, steps[0])

            def narrow_tables():
                dve.wait_ge(tables_in, 48)
                link(v.tensor_scalar(first_dst, first_dst, HALF.bit_length() - 1, (HALF // GROUP).bit_length() - 1,
                                     ALU.arith_shift_right, ALU.arith_shift_left))
                link(v.tensor_scalar(quarter_t.bitcast(I32), dst_i, NG.bit_length() - 1, None, ALU.arith_shift_right))
                link(v.tensor_tensor(quarter_t, quarter_t.bitcast(I32), first_dst, ALU.subtract))
                link(v.tensor_scalar(place_t.bitcast(I32), dst_i, NG - 1, None, ALU.bitwise_and))
                link(v.tensor_copy(place_t, place_t.bitcast(I32)))
                now, before = win_now[0:path.blocks].bitcast(I32), win_before[0:path.blocks].bitcast(I32)
                link(v.tensor_scalar(now, now, HALF.bit_length() - 1, None, ALU.arith_shift_right))
                link(v.tensor_scalar(before, before, HALF.bit_length() - 1, None, ALU.arith_shift_right))
                link(v.tensor_tensor(goes_on[0:path.blocks], now, before, ALU.is_equal))
                v.nop().then_inc(tables_ready, 1)
                for b in range(WB):
                    for h in range(2):
                        link(v.tensor_scalar(out=base_i.bitcast(F32), in0=base_f, scalar1=half_ids[:, b, h:h + 1],
                                             scalar2=0.0, op0=ALU.is_le, op1=ALU.add,
                                             accum_out=items_up_to[:, 0, b, h:h + 1]))
                v.nop().then_inc(runs_ready, 1)

            def run_ends():
                dve.wait_ge(runs_in, 32)
                nothing = float(2 * (NI - 1))
                link(v.tensor_tensor(run_exists[:], items_up_to[:, 0:2], items_up_to[:, 1:3], ALU.is_gt))
                for run in range(2):
                    link(v.tensor_scalar(run_last[:, run], items_up_to[:, run], 2.0, float(run - 2) - nothing,
                                         ALU.mult, ALU.add))
                link(v.tensor_tensor(run_last[:], run_last[:], run_exists[:], ALU.mult))
                link(v.tensor_scalar(run_last[:], run_last[:], nothing, None, ALU.add))
                link(v.tensor_copy(run_idx[:], run_last[:]))
                v.nop().then_inc(run_idx_ready, 1)

            if path.narrow:
                narrow_tables()
            else:
                dve.wait_ge(tile_end_in, 16)
                last_win_i = last_window.bitcast(I32)
                link(v.tensor_scalar(last_win_i, last_dst, J.bit_length() - 1, None, ALU.arith_shift_right))
                link(v.tensor_copy(last_dst.bitcast(F32), last_win_i))
                link(v.tensor_tensor(tile_end, tile_end, last_dst.bitcast(F32), ALU.add))
                ended = last_dst.bitcast(F32)
                for b in range(path.blocks):
                    v.tensor_scalar(out=last_window, in0=tile_end, scalar1=item_ids[:, b:b + 1], scalar2=0.0,
                                    op0=ALU.is_lt, op1=ALU.add, accum_out=tile_of[:, b:b + 1]).then_inc(dve_step, 1)
                    steps[0] += 1
                    dve.wait_ge(dve_step, steps[0])
                for b in range(WB):
                    link(v.tensor_scalar(out=last_window, in0=ended, scalar1=window_ids[:, b:b + 1], scalar2=0.0,
                                         op0=ALU.is_le, op1=ALU.add, accum_out=last_f[:, b:b + 1]))
                link(v.tensor_tensor(last_f[:], last_f[:], window_ids[:], ALU.add))
                link(v.tensor_scalar(last_idx[:], last_f[:], float(path.items - 1), None, ALU.min))
                used = slice(0, path.blocks)
                link(v.tensor_scalar(tile_idx[:, used], tile_of[:, used], float(TILES - 1), None, ALU.min))
                link(v.tensor_scalar(window4[:, used], tile_of[:, used], float(TILES), float(1 << 20), ALU.is_ge,
                                     ALU.mult))
                link(v.tensor_tensor(tile_of[:, used], item_ids[:, used], tile_of[:, used], ALU.subtract))
                v.scalar_tensor_tensor(window4[:, used], tile_of[:, used], float(NG), window4[:, used], ALU.mult,
                                       ALU.add).then_inc(count_ready, 1)
                dve.wait_ge(win_loaded, 32)
                v.tensor_tensor(goes_on[used], win_now[used], win_before[used], ALU.is_equal
                                ).then_inc(goes_ready, 1)
                dve.wait_ge(count_ready, 1)

                base = steps[0]
                LINKS = 4

                def table_block(b):
                    if due(b):
                        dve.wait_ge(attr_in, 16 * b)
                        dve.wait_ge(rad_in, 16 * b)
                        dve.wait_ge(rows_ready, 3 * b)
                    v.tensor_copy(w4_col[:], window4[:, ds(b, 1)]).then_inc(dve_step, 1)
                    v.tensor_copy(tile_col[:], tile_idx[:, ds(b, 1)]).then_inc(col_ready, 1)
                    dve.wait_ge(src_in, 16 * (b + 1))
                    dve.wait_ge(dst_in, 16 * (b + 1))
                    dve.wait_ge(attr_in, 16 * (b + 1))
                    if due(b):
                        dve.wait_ge(item_tr, b)
                    v.tensor_copy(src_f, src_r).then_inc(dve_step, 1)
                    v.tensor_scalar(slot_i[:, 0:P], dst_r, NG.bit_length() - 1, None, ALU.arith_shift_right
                                    ).then_inc(dve_step, 1)
                    v.tensor_scalar(slot_i[:, P:2 * P], dst_r, NG - 1, None, ALU.bitwise_and).then_inc(dve_step, 1)
                    v.tensor_copy(table_f[:, 0:3 * P], attr_r[:, 0:3 * P]).then_inc(rows_ready, 1)
                    dve.wait_ge(dve_step, base + b * LINKS + 4)
                    v.tensor_scalar(table_f[:, 3 * P:4 * P], slot_i[:, 0:P], w4_col[:, 0:1], None, ALU.subtract
                                    ).then_inc(rows_ready, 1)
                    v.tensor_copy(table_f[:, 4 * P:5 * P], slot_i[:, P:2 * P]).then_inc(rows_ready, 1)

                table_block(0)
                with dve.Fori(1, path.blocks) as b:
                    table_block(b)
                steps[0] += LINKS * path.blocks

            def scan(n, kinds):
                dve.wait_ge(part_ready, n + 1)
                dve.wait_ge(carry_loaded, 16 * (n + 1))
                if due(n):
                    dve.wait_ge(rt_ready, n)
                for kind in range(kinds):
                    part = ps[:, 7, kind * P:kind * P + P].rearrange("p (i g) -> p g i", g=NG)
                    to = R[:, kind, :].rearrange("p (i g) -> p g i", g=NG)
                    for g in range(NG):
                        v.tensor_tensor_scan(to[:, g, :], carry[:], part[:, g, :], last[:, kind, g:g + 1],
                                             ALU.mult, ALU.add).then_inc(dve_step, 1)

            def keep_last(kinds):
                return v.tensor_copy(last[:, 0:kinds, :], R[:, 0:kinds, (STEP - 1) * NG:STEP * NG])

            def slot_masks():
                v.tensor_tensor(group_hot[:], meta[:, 3, :].unsqueeze(2).to_broadcast([P, STEP, NG]),
                                slot_ids[:, 0:4].unsqueeze(1).to_broadcast([P, STEP, NG]), ALU.is_equal).then_inc(dve_step, 1)
                v.tensor_tensor(place_hot[:], meta[:, 4, :].unsqueeze(2).to_broadcast([P, STEP, GROUP]),
                                slot_ids[:, 0:4].unsqueeze(1).to_broadcast([P, STEP, GROUP]), ALU.is_equal
                                ).then_inc(dve_step, 1)

            dve.wait_ge(meta_loaded, 16)
            v.memset(h2_s[HID:HID + 1], 1.0).then_inc(w3_ready, 1)
            base0 = steps[0]
            MASKS = 1
            G0 = 4
            SCAN0 = 2 * NG + 1

            def sum_inputs(i, e):
                dve.wait_ge(q_done[(2 * e + 1) % 8], 2 * i + e // 4 + 1)
                if e == 0 and due(i):
                    dve.wait_ge(part_ready, i)
                four = ps[:, SUMS[e % 2], :].rearrange("p (s u w) -> p s w u", s=4, u=16)
                v.tensor_reduce(sums[:, e, :].rearrange("p (s w) -> p s w", s=4), four, AX.X, ALU.add
                                ).then_inc(q_out, 1)

            def l0_step(i, prior, with_scan):
                dve.wait_ge(meta_loaded, 16 * (i + 1))
                dve.wait_ge(attr_loaded, 16 * (i + 1))
                if due(i):
                    dve.wait_ge(onehot_ready, i)
                v.scalar_tensor_tensor(slot[:], meta[:, 3, :], float(GROUP), meta[:, 4, :], ALU.mult, ALU.add
                                       ).then_inc(dve_step, 1)
                at = prior + MASKS

                def features(half):
                    its = slice(2 * QUART * half, 2 * QUART * half + 2 * QUART)
                    for g in (2 * half, 2 * half + 1):
                        dve.wait_ge(x_in[g], 16 * QUART * (i + 1))
                    hs = xg[:, its, 0:MUL]
                    hv = xg[:, its, MUL:CH].rearrange("p n (u i) -> p n i u", i=3)
                    sh0 = meta[:, 5, its]
                    sh1 = meta[:, 6:9, its].rearrange("p i n -> p n i")
                    f_s = feat[:, its, :].rearrange("p n (s u) -> p n s u", s=4)
                    dot = dots.rearrange("p n (i u) -> p n i u", i=3)
                    v.tensor_tensor(f_s[:, :, 0, 0:MUL], hs, sh0.unsqueeze(2).to_broadcast([P, 2 * QUART, MUL]),
                                    ALU.mult).then_inc(dve_step, 1)
                    v.tensor_tensor(f_s[:, :, 1:4, MUL:2 * MUL], hv,
                                    sh0.unsqueeze(2).unsqueeze(3).to_broadcast([P, 2 * QUART, 3, MUL]),
                                    ALU.mult).then_inc(dve_step, 1)
                    v.tensor_tensor(f_s[:, :, 1:4, 0:MUL], hs.unsqueeze(2).to_broadcast([P, 2 * QUART, 3, MUL]),
                                    sh1.unsqueeze(3).to_broadcast([P, 2 * QUART, 3, MUL]), ALU.mult).then_inc(dve_step, 1)
                    v.tensor_tensor(dot, hv, sh1.unsqueeze(3).to_broadcast([P, 2 * QUART, 3, MUL]),
                                    ALU.mult).then_inc(dve_step, 1)
                    dve.wait_ge(dve_step, at)
                    v.tensor_reduce(f_s[:, :, 0, MUL:2 * MUL], dot.rearrange("p n i u -> p n u i"), AX.X,
                                    ALU.add).then_inc(feat_ready[half], 1)
                    dve.wait_ge(feat_ready[half], i + 1)
                    if half == 1:
                        v.nop().then_inc(meta_used, 1)

                for q4 in range(4):
                    if q4 % 2 == 0:
                        at = at + G0
                        features(q4 // 2)
                    if q4 == 0:
                        if due(i):
                            sum_inputs(i - 1, 7)
                        dve.wait_ge(dve_step, prior + MASKS)
                        if due(i):
                            dve.wait_ge(deg_done, i)
                        v.tensor_tensor(onehot[:, :, 0:J], slot[:].unsqueeze(2).to_broadcast([P, STEP, J]),
                                        slot_ids[:].unsqueeze(1).to_broadcast([P, STEP, J]), ALU.is_equal
                                        ).then_inc(onehot_ready, 1)
                    for q in range(4 * q4, 4 * q4 + 4):
                        dve.wait_ge(tpw_ready[q % 4], 4 * i + q4 + 1)
                        if due(2 * i + q // 8):
                            dve.wait_ge(q_done[q % 8], 2 * i + q // 8)
                        tpw = ps[:, TPW[q % 4], :].rearrange("p (h s u w) -> p h s u w", h=2, s=2, u=16)
                        two = feat[:, 2 * q:2 * q + 2, :].rearrange("p h (s u) -> p h s u", s=4)
                        pr = prod[:, q % 8].rearrange("p h (s u w) -> p h s u w", s=4, u=16)
                        v.tensor_tensor(pr[:, :, 0], tpw[:, :, 0], two[:, :, 0].unsqueeze(3)
                                        .to_broadcast([P, 2, 16, MUL]), ALU.mult).then_inc(prod_ready[q % 8], 1)
                        for h in range(2):
                            v.tensor_tensor(pr[:, h, 1:4], tpw[:, h, 1].unsqueeze(1).to_broadcast([P, 3, 16, MUL]),
                                            two[:, h, 1:4].unsqueeze(3).to_broadcast([P, 3, 16, MUL]),
                                            ALU.mult).then_inc(prod_ready[q % 8], 1)
                        if q >= 4 and q % 2 == 0:
                            sum_inputs(i, q // 2 - 2)
                    if q4 == 1 and with_scan:
                        scan(i - 1, 2)
                        dve.wait_ge(dve_step, at + 2 * NG)
                        keep_last(2).then_inc(dve_step, 1)
                        at = at + SCAN0
                        dve.wait_ge(dve_step, at)
                        v.nop().then_inc(R_ready, 1)
                sum_inputs(i, 6)

            l0_step(0, base0, False)
            l0_step(1, base0 + MASKS + 2 * G0, True)
            per0 = MASKS + 2 * G0 + SCAN0
            with dve.Fori(2, STEPS) as i:
                l0_step(i, i * per0 + (base0 - SCAN0), True)
            steps[0] = base0 - SCAN0 + STEPS * per0
            sum_inputs(STEPS - 1, 7)
            if path.narrow:
                run_ends()
            scan(STEPS - 1, 2)
            steps[0] += 2 * NG
            dve.wait_ge(dve_step, steps[0])
            link(keep_last(2))
            v.nop().then_inc(R_ready, 1)

            GATHERS = 4 if path.narrow else 1
            rooted = [0]

            def square_root(last_ins):
                last_ins.then_inc(root_in, 1)
                rooted[0] += 1
                dve.wait_ge(root_out, rooted[0])

            def nodes_of(tile_, b):
                return tile_[:, b, :].rearrange("p (j c) -> p j c", c=CH)

            def per_node(col):
                return col.unsqueeze(2).to_broadcast([P, J, CH])

            def per_channel(row):
                return row.unsqueeze(1).to_broadcast([P, J, CH])

            def by_channel(sums_of):
                return v.tensor_reduce(bn[:, 0, :], sums_of.rearrange("p (j c) -> p c j", c=CH), AX.X, ALU.add)

            def layer_norm(to, b):
                yn, qn = nodes_of(y, b), nodes_of(sq, b)
                mean, var, inv = (stat[:, k, J * b:J * b + J] for k in range(3))
                link(v.tensor_reduce(mean, yn, AX.X, ALU.add))
                link(v.tensor_scalar(mean, mean, 1.0 / CH, None, ALU.mult))
                link(v.tensor_tensor(yn, yn, per_node(mean), ALU.subtract))
                link(v.tensor_tensor(qn, yn, yn, ALU.mult))
                link(v.tensor_reduce(var, qn, AX.X, ALU.add))
                square_root(v.tensor_scalar(var, var, 1.0 / CH, EPS, ALU.mult, ALU.add))
                link(v.reciprocal(inv, var))
                return v.tensor_tensor(nodes_of(to, b), yn, per_node(inv), ALU.mult)

            for b in range(WB):
                par = b % 2
                dve.wait_ge(nx_ready[par], uses(par, 0) + b // 2 + 1)
                v.scalar_tensor_tensor(xw[:, b, :], ps[:, 2 + par, :], MUL ** -0.5, xw[:, b, :], ALU.mult,
                                       ALU.add).then_inc(nx_used[par], 1)
                dve.wait_ge(nx_used[par], uses(par, 0) + b // 2 + 1)
            for b in range(WB):
                dve.wait_ge(cnt_in[b], 16 * GATHERS)
                degree = rcnt[:, J * b:J * b + J]
                if path.narrow:
                    link(v.tensor_tensor(degree, nodes_of(sq, b)[:, :, 0], nodes_of(x1, b)[:, :, 0], ALU.add))
                else:
                    link(v.tensor_copy(degree, nodes_of(sq, b)[:, :, 0]))
            link(v.tensor_scalar(rcnt[:], rcnt[:], 1.0, None, ALU.max))
            link(v.reciprocal(rcnt[:], rcnt[:]))
            for b in range(WB):
                dve.wait_ge(agg_in[b], 16 * GATHERS)
                if path.narrow:
                    link(v.tensor_tensor(agg[:, b, :], agg[:, b, :], y[:, b, :], ALU.add))
                yb, xb, ab = nodes_of(y, b), nodes_of(xw, b), nodes_of(agg, b)
                v.tensor_tensor(yb[:, :, 0:MUL], xb[:, :, 0:MUL], ab[:, :, 0:MUL], ALU.add).then_inc(dve_step, 1)
                steps[0] += 1
                link(v.tensor_tensor(yb[:, :, MUL:CH].rearrange("p j (w s) -> p j s w", s=3),
                                     xb[:, :, MUL:CH].rearrange("p j (w s) -> p j s w", s=3),
                                     ab[:, :, MUL:CH].rearrange("p j (s w) -> p j s w", s=3), ALU.add))
                link(layer_norm(x1, b))
                v.tensor_copy(xw[:, b, :], x1[:, b, :]).then_inc(x_ready, 1)

            LINKS1 = 9
            SCAN1 = NG + 1

            def l1_step(l, i, prior, with_scan):
                n = (l + 1) * STEPS + i
                n1 = l * STEPS + i
                dve.wait_ge(meta_loaded, 16 * (n + 1))
                dve.wait_ge(attr_loaded, 16 * (n + 1))
                if due(n1):
                    for ch in range(8):
                        dve.wait_ge(bm_ready[ch], n1)
                        dve.wait_ge(xm_ready[ch], n1)
                slot_masks()
                coords = meta[:, 0:3, :].rearrange("p d n -> p n d")
                raw = meta[:, 0:3, :]
                v.tensor_scalar(raw, raw, 3.0, 0.0, ALU.mult, ALU.max).then_inc(dve_step, 1)
                dve.wait_ge(dve_step, prior + 3)
                v.tensor_scalar(raw, raw, 3.0, None, ALU.min).then_inc(dve_step, 1)
                dve.wait_ge(dve_step, prior + 4)
                v.tensor_tensor(hat[:], coords.unsqueeze(3).to_broadcast([P, STEP, 3, 4]),
                                slot_ids[:, 0:4].unsqueeze(1).unsqueeze(1).to_broadcast([P, STEP, 3, 4]),
                                ALU.subtract).then_inc(meta_used, 1)
                dve.wait_ge(meta_used, n + 1)
                v.scalar_tensor_tensor(hat2[:], hat[:], -1.0, hat[:], ALU.mult, ALU.max).then_inc(dve_step, 1)
                dve.wait_ge(dve_step, prior + 5)
                v.tensor_scalar(hat2[:], hat2[:], -1.0, 1.0, ALU.mult, ALU.add).then_inc(dve_step, 1)
                dve.wait_ge(dve_step, prior + 6)
                v.tensor_scalar(hat[:], hat2[:], 0.0, None, ALU.max).then_inc(dve_step, 1)
                dve.wait_ge(dve_step, prior + 7)
                v.tensor_tensor(b01[:].rearrange("p n (b a) -> p n b a", a=4),
                                hat[:, :, 1, :].unsqueeze(3).to_broadcast([P, STEP, 4, 4]),
                                hat[:, :, 0, :].unsqueeze(2).to_broadcast([P, STEP, 4, 4]),
                                ALU.mult).then_inc(dve_step, 1)
                dve.wait_ge(dve_step, prior + 8)
                v.tensor_tensor(b01_group[:], b01[:].unsqueeze(2).to_broadcast([P, STEP, NG, 16]),
                                group_hot[:].unsqueeze(3).to_broadcast([P, STEP, NG, 16]), ALU.mult
                                ).then_inc(dve_step, 1)
                dve.wait_ge(dve_step, prior + LINKS1)
                for ch in range(8):
                    its = slice(4 * ch, 4 * ch + 4)
                    ring = slice(4 * (ch % 4), 4 * (ch % 4) + 4)
                    if due(4 * n1 + 2 * (ch // 2) - 2):
                        dve.wait_ge(s_done[2 * (ch % 2) + 1], 4 * n1 + (ch - 4) // 2 + 1)
                    v.tensor_tensor(bm[:, ring].rearrange("p n c g a -> p n c (g a)"),
                                    b01_group[:, its].rearrange("p n g a -> p n (g a)").unsqueeze(2)
                                    .to_broadcast([P, 4, 4, NG * 16]),
                                    hat[:, its, 2, :].unsqueeze(3).to_broadcast([P, 4, 4, NG * 16]), ALU.mult
                                    ).then_inc(bm_ready[ch], 1)
                    dve.wait_ge(x_in[ch // 2], 16 * QUART * (n + 1))
                    v.tensor_tensor(xm[:, ring], xg[:, its, :].unsqueeze(2).to_broadcast([P, 4, GROUP, CH]),
                                    place_hot[:, its, :].unsqueeze(3).to_broadcast([P, 4, GROUP, CH]),
                                    ALU.mult).then_inc(xm_ready[ch], 1)
                    if ch == 3 and with_scan:
                        scan(n - 2, 1)
                        dve.wait_ge(dve_step, prior + LINKS1 + NG)
                        keep_last(1).then_inc(dve_step, 1)
                        dve.wait_ge(dve_step, prior + LINKS1 + SCAN1)
                        v.nop().then_inc(R_ready, 1)

            for l in range(LAYERS):
                base1 = steps[0]
                per1 = LINKS1 + SCAN1
                l1_step(l, 0, base1, False)
                l1_step(l, 1, base1 + LINKS1, False)
                with dve.Fori(2, STEPS) as i:
                    l1_step(l, i, i * per1 + (base1 - 2 * SCAN1), True)
                steps[0] = base1 + STEPS * per1 - 2 * SCAN1
                for n in ((l + 2) * STEPS - 2, (l + 2) * STEPS - 1):
                    scan(n, 1)
                    steps[0] += NG
                    dve.wait_ge(dve_step, steps[0])
                    link(keep_last(1))
                    v.nop().then_inc(R_ready, 1)

                for b in range(WB):
                    par = b % 2
                    done = uses(par, l + 1) + b // 2
                    dve.wait_ge(nx_ready[par], done + 1)
                    v.tensor_tensor(nodes_of(sq, b), ps[:, 2 + par, :].rearrange("p (j c) -> p j c", c=CH),
                                    per_channel(chan[:, l, 0, :]), ALU.add).then_inc(nx_used[par], 1)
                    dve.wait_ge(nx_used[par], done + 1)
                for b in range(WB):
                    yb = nodes_of(y, b)
                    dve.wait_ge(agg_in[b], 16 * GATHERS * (l + 2))
                    if path.narrow:
                        link(v.tensor_tensor(agg[:, b, :], agg[:, b, :], y[:, b, :], ALU.add))
                    link(v.tensor_tensor(yb, nodes_of(agg, b), per_node(rcnt[:, J * b:J * b + J]), ALU.mult))
                    link(v.tensor_tensor(y[:, b, :], y[:, b, :], sq[:, b, :], ALU.add))
                    if l < LAYERS - 1:
                        link(v.scalar_tensor_tensor(y[:, b, :], y[:, b, :], NEG, y[:, b, :], ALU.mult, ALU.max))
                    link(v.tensor_tensor(y[:, b, :], y[:, b, :], xw[:, b, :], ALU.add))
                    if b == WB - 1:
                        link(v.tensor_tensor(yb, yb, per_node(node_mask[:]), ALU.mult))
                    v.nop().then_inc(sum_ready, 1)

                dve.wait_ge(sum_done, 2 * l + 1)
                link(by_channel(ps[:, 4, :]))
                link(v.tensor_scalar(bn[:, 1, :], bn[:, 0, :], 1.0 / nodes, None, ALU.mult))
                for b in range(WB):
                    yb = nodes_of(y, b)
                    link(v.tensor_tensor(yb, yb, per_channel(bn[:, 1, :]), ALU.subtract))
                    if b == WB - 1:
                        link(v.tensor_tensor(yb, yb, per_node(node_mask[:]), ALU.mult))
                    v.tensor_tensor(sq[:, b, :], y[:, b, :], y[:, b, :], ALU.mult).then_inc(sum_ready, 1)
                dve.wait_ge(sum_done, 2 * l + 2)
                link(by_channel(ps[:, 4, :]))
                square_root(v.tensor_scalar(bn[:, 2, :], bn[:, 0, :], 1.0 / nodes, EPS, ALU.mult, ALU.add))
                link(v.reciprocal(bn[:, 3, :], bn[:, 2, :]))
                link(v.tensor_tensor(bn[:, 4, :], bn[:, 3, :], chan[:, l, 1, :], ALU.mult))
                for b in range(WB):
                    yb = nodes_of(y, b)
                    link(v.tensor_tensor(yb, yb, per_channel(bn[:, 4, :]), ALU.mult))
                    if l < LAYERS - 1:
                        v.tensor_tensor(nodes_of(xw, b), yb, per_channel(chan[:, l, 2, :]), ALU.add).then_inc(x_ready, 1)
                    else:
                        link(v.tensor_tensor(yb, yb, per_channel(chan[:, l, 2, :]), ALU.add))
                        link(v.tensor_tensor(y[:, b, :], y[:, b, :], x1[:, b, :], ALU.add))
                        layer_norm(xw, b).then_inc(out_ready, 1)
                if l < LAYERS - 1:
                    dve.wait_ge(x_ready, WB * (l + 2))

        @block.vector
        def _(dve):
            v = nc.vector
            steps = [0]

            def link(ins):
                steps[0] += 1
                ins.then_inc(dve_step, 1)
                dve.wait_ge(dve_step, steps[0])

            dve.wait_ge(loaded, LOADS)
            v.memset(minus[:], -1.0).then_inc(minus_ready, 1)
            v.memset(zeros[:], 0.0).then_inc(runs_ready, 1)
            link(v.memset(last[:], 0.0))
            v.tensor_tensor(w3[:], w3[:], w3_scale[:], ALU.mult).then_inc(w3_ready, 1)
            link(v.memset(onehot[:], 0.0))
            link(v.tensor_scalar(base_i, first_dst, HALF.bit_length() - 1, None, ALU.arith_shift_right))
            link(v.tensor_copy(base_f, base_i))
            link(v.tensor_copy(reach, last_dst))
            link(v.scalar_tensor_tensor(reach, base_f[:, 0:TILES], -float(HALF), reach, ALU.mult, ALU.add))
            link(v.tensor_reduce(span[:], reach, AX.X, ALU.max))
            link(v.tensor_scalar(span[:], span[:], float(J), None, ALU.is_ge))
            v.tensor_copy(is_wide[:], span[:]).then_inc(span_ready, 1)
            dve.wait_ge(span_ready, 1)
            wide = dve.value_load(is_wide[0:1, 0:1], min_val=0, max_val=1)
            with dve.If(wide):
                vector_program(dve, WIDE, steps[0])
            with dve.Else():
                vector_program(dve, NARROW, steps[0])

        def tensor_program(pe, path):
            STEPS = path.steps
            pe.wait_ge(loaded, LOADS)
            def transpose_block(b):
                pe.wait_ge(rows_ready, 3 * (b + 1))
                if due(b):
                    pe.wait_ge(item_out, 4 * b)
                for c in range(5):
                    nc.tensor.transpose(ps[:, c // 4, (c % 4) * P:(c % 4) * P + P], table_f[:, c * P:c * P + P],
                                        ident[:])
                for c in range(5, META):
                    nc.tensor.transpose(ps[:, c // 4, (c % 4) * P:(c % 4) * P + P],
                                        attr_r[:, (c - 2) * P:(c - 1) * P], ident[:])
                nc.tensor.transpose(ps[:, 2, P:2 * P], src_f, ident[:]).then_inc(item_tr, 1)

            if not path.narrow:
                transpose_block(0)
                with pe.Fori(1, path.blocks) as b:
                    transpose_block(b)

            def transpose_totals(n, kinds, bank, col):
                pe.wait_ge(R_ready, n + 1)
                if due(n):
                    pe.wait_ge(rt_out, n)
                for kind in range(kinds):
                    tr = nc.tensor.transpose(ps[:, bank, col + kind * P:col + kind * P + P], R[:, kind, :], ident[:])
                tr.then_inc(rt_ready, 1)

            def l0_spread(n):
                pe.wait_ge(q_out, 8 * (n + 1))
                if due(n):
                    pe.wait_ge(rt_out, n)
                for e in range(STEP // 4):
                    for jj in range(GROUP):
                        tr = nc.tensor.matmul(ps[CH * jj:CH * jj + CH, 7, J * e:J * e + J], sums[:, e, :],
                                              spread[:, jj, :], start=True, stop=True, tile_position=(0, CH * jj))
                tr.then_inc(part_ready, 1)

            def l0_degrees(i):
                for jj in range(GROUP):
                    tr = nc.tensor.matmul(ps[CH * jj:CH * jj + CH, 7, P:2 * P], ones[:, 0:CH],
                                          onehot[:, :, jj:jj + GROUP * (NG - 1) + 1:GROUP],
                                          start=True, stop=True, tile_position=(0, CH * jj))
                tr.then_inc(deg_done, 1)

            def first_layer(i, f, half):
                if half == 0:
                    pe.wait_ge(rad_loaded[f // 2 % 2], 16 * (i + f // 4 + 1))
                    if due(8 * i + 2 * f):
                        pe.wait_ge(h2_act, 8 * i + 2 * f)
                for p in (2 * half, 2 * half + 1):
                    q = 4 * (f % 4) + p
                    tr = nc.tensor.matmul(ps[:, 0, p * P:p * P + P], w1[:, q % 8, :], rad[:, q // 8, :],
                                          start=True, stop=True)
                if half == 1:
                    tr.then_inc(h1_ready, 1)

            def second_layer(i, f):
                pe.wait_ge(h1_act, 4 * i + f + 1)
                nc.tensor.matmul(ps[:, 0, :], w2[:], h1_s, start=True, stop=True).then_inc(h2_ready, 1)

            def third_layer(i, q):
                f, p = q // 4, q % 4
                if p == 0:
                    pe.wait_ge(h2_act, 8 * i + 2 * f + 2)
                if due(2 * i + (q + 4) // 8):
                    pe.wait_ge(prod_ready[(q + 4) % 8], 3 * (2 * i + (q + 4) // 8))
                for h in range(2):
                    tr = nc.tensor.matmul(ps[:, TPW[p], 256 * h:256 * h + 256],
                                          h2_s[0:HID + 1, f % 2, h, p * P:p * P + P], w3[:], start=True, stop=True)
                tr.then_inc(tpw_ready[p], 1)

            def l0_step(i, groups, with_totals):
                def item_sums(q):
                    par, e = q % 2, q // 2
                    if q == 0:
                        pe.wait_ge(onehot_ready, i + 1)
                    if par == 0 and due(8 * i + e - 1):
                        pe.wait_ge(q_out, 8 * i + e - 1)
                    pe.wait_ge(prod_ready[q % 8], 3 * (2 * i + q // 8 + 1))
                    for h in range(2):
                        m = 2 * par + h
                        tr = nc.tensor.matmul(ps[CH * m:CH * m + CH, SUMS[e % 2], :], onehot[:, 2 * q + h, :],
                                              prod[:, q % 8, h, :], start=True, stop=True, tile_position=(0, CH * m))
                    tr.then_inc(q_done[q % 8], 1)

                for q in range(16):
                    f = q // 4
                    if q == 0 and due(i):
                        l0_spread(i - 1)
                    if f + 1 < groups:
                        third_layer(i, q + 4)
                    if q % 2:
                        item_sums(q - 1)
                        item_sums(q)
                    if q % 4 == 0 and f + 2 < groups:
                        second_layer(i, f + 2)
                    if q % 4 >= 2 and f < 3 and f + 3 < groups:
                        first_layer(i, f + 3, q % 4 - 2)
                if due(i):
                    pe.wait_ge(R_ready, i)
                l0_degrees(i)
                if with_totals:
                    transpose_totals(i - 1, 2, 7, 256)
                if groups == 7:
                    for half in range(2):
                        first_layer(i, 6, half)

            pe.wait_ge(w3_ready, 2)
            for half in range(2):
                first_layer(0, 0, half)
            for f in range(2):
                second_layer(0, f)
                for half in range(2):
                    first_layer(0, f + 1, half)
            for q in range(4):
                third_layer(0, q)
            l0_step(0, 7, False)
            l0_step(1, 7, True)
            with pe.Fori(2, STEPS - 1) as i:
                l0_step(i, 7, True)
            l0_step(STEPS - 1, 4, True)
            l0_spread(STEPS - 1)
            transpose_totals(STEPS - 1, 2, 7, 256)

            def node_products(phase, weights):
                for b in range(WB):
                    par = b % 2
                    done = uses(par, phase) + b // 2
                    if due(done):
                        pe.wait_ge(nt_out[par], done)
                    for g in range(NG):
                        tr = nc.tensor.transpose(ps[:, par, g * P:g * P + P], xw[:, b, g * P:g * P + P], ident[:])
                    tr.then_inc(nt_ready[par], 1)
                    pe.wait_ge(nt_out[par], done + 1)
                    if due(done):
                        pe.wait_ge(nx_used[par], done)
                    for g in range(NG):
                        tr = nc.tensor.matmul(ps[:, 2 + par, g * P:g * P + P], xt[:, par, g * P:g * P + P], weights,
                                              start=True, stop=True)
                    tr.then_inc(nx_ready[par], 1)

            pe.wait_ge(x0_loaded, 16)
            node_products(0, w_self[:])

            def item_sums(l, i, ch):
                n1 = l * STEPS + i
                pe.wait_ge(bm_ready[ch], n1 + 1)
                pe.wait_ge(xm_ready[ch], n1 + 1)
                for pair in range(2):
                    e = 2 * ch + pair
                    bank = e % 4
                    if due(4 * n1 + e // 4):
                        pe.wait_ge(s_out[bank], 4 * n1 + e // 4)
                    for h in range(2):
                        r = (2 * e + h) % 16
                        tr = nc.tensor.matmul(ps[:, bank, 256 * h:256 * h + 256], xm[:, r].rearrange("p j c -> p (j c)"),
                                              bm[:, r].rearrange("p c g a -> p (c g a)"), start=True, stop=True)
                    tr.then_inc(s_done[bank], 1)

            def tap_products(l, i, par, part8):
                if part8 == 0:
                    for bank in range(4):
                        pe.wait_ge(s_out[bank], 4 * (l * STEPS + i + 1))
                    pe.wait_ge(R_ready, (l + 1) * STEPS + i)
                for k in range(8 * part8, 8 * part8 + 8):
                    tr = nc.tensor.matmul(ps[:, 7, 0:P], w_taps[:, k, :], S[:, par, :, k // 16, :, k % 16],
                                          start=(k == 0), stop=(k == TAPS - 1), skip_group_check=True)
                if part8 == 7:
                    tr.then_inc(part_ready, 1)

            def l1_step(l, i, par, with_taps, with_totals):
                for ch in range(8):
                    item_sums(l, i, ch)
                    if with_taps:
                        tap_products(l, i - 1, 1 - par, ch)
                if with_totals:
                    transpose_totals((l + 1) * STEPS + i - 2, 1, 6, 0)

            for l in range(LAYERS):
                pe.wait_ge(w_loaded, 16 * (l + 1))
                l1_step(l, 0, 0, False, False)
                l1_step(l, 1, 1, True, False)
                with pe.Fori(2, pairs_end(path), 2) as i:
                    for par in range(2):
                        l1_step(l, i + par, par, True, True)
                for i in range(pairs_end(path), STEPS):
                    l1_step(l, i, i % 2, True, True)
                transpose_totals((l + 2) * STEPS - 2, 1, 6, 0)
                for part8 in range(8):
                    tap_products(l, STEPS - 1, (STEPS - 1) % 2, part8)
                transpose_totals((l + 2) * STEPS - 1, 1, 6, 0)
                pe.wait_ge(x_ready, WB * (l + 1))
                node_products(l + 1, w_root[:, l, :])
                for half, values in enumerate((y, sq)):
                    for b in range(WB):
                        pe.wait_ge(sum_ready, WB * (2 * l + half) + b + 1)
                        tr = nc.tensor.matmul(ps[:, 4, :], ones[:], values[:, b, :], start=(b == 0), stop=(b == WB - 1))
                    tr.then_inc(sum_done, 1)

        @block.tensor
        def _(pe):
            pe.wait_ge(span_ready, 1)
            wide = pe.value_load(is_wide[0:1, 0:1], min_val=0, max_val=1)
            with pe.If(wide):
                tensor_program(pe, WIDE)
            with pe.Else():
                tensor_program(pe, NARROW)


def prepare(inputs):
    f = np.float32
    x, src, dst = (np.asarray(inputs[k]) for k in ("x", "src", "dst"))
    nodes, edges = x.shape[0], src.shape[0]
    tiles, wb, narrow, wide = sizes(nodes, edges)
    nb, ni = max(narrow.blocks, wide.blocks), narrow.steps * STEP
    d = {}
    d["x"] = np.zeros((wb * P * J, CH), f)
    d["x"][:nodes] = x
    d["src"] = src.reshape(tiles, P)
    d["dst"] = dst.reshape(tiles, P)
    d["last_dst"] = dst[P - 1::P].reshape(1, tiles)
    attr = np.concatenate([np.asarray(inputs[f"edge_attr_{k}"]) for k in (3, 4, 8)], axis=1)
    attr = attr.reshape(tiles, P, 15).transpose(0, 2, 1)
    d["attr"] = attr[:, :7].reshape(tiles, 7 * P)
    d["rad"] = np.zeros((ni, MUL * P), f)
    d["rad"][:tiles] = attr[:, 7:].reshape(tiles, MUL * P)
    far = 1 << 22
    first = np.concatenate([dst[0::P], np.full(nb * P - tiles, far, dst.dtype)])
    d["first_dst"] = first[None, :ni]
    d["first_now"] = first[:narrow.blocks * P].reshape(narrow.blocks, P)
    d["first_before"] = np.concatenate([[-HALF], first])[:narrow.blocks * P].astype(dst.dtype).reshape(narrow.blocks, P)
    for name, rows in (("src_t", d["src"]), ("dst_t", d["dst"])):
        d[name] = np.zeros((P, ni), rows.dtype)
        d[name][:, :tiles] = rows.T
    for name, c0, c1 in (("coord_t", 0, 3), ("sh_t", 3, 7)):
        by_lane = np.zeros((ni, c1 - c0, P), f)
        by_lane[:tiles] = attr[:, c0:c1]
        d[name] = by_lane.reshape(narrow.steps, STEP, c1 - c0, P).transpose(3, 0, 2, 1)
    g = lambda name: np.asarray(inputs[name])
    W1, W2, W3 = g("L0_gnn_W1"), g("L0_gnn_W2"), g("L0_gnn_W3")
    d["w1"] = np.zeros((P, 8, P), f)
    for q in range(8):
        for h in range(2):
            d["w1"][16 * q + 8 * h:16 * q + 8 * h + 8, q, HID * h:HID * h + HID] = W1
    d["w2"] = np.zeros((P, P), f)
    for h in range(2):
        d["w2"][HID * h:HID * h + HID, HID * h:HID * h + HID] = W2
    d["w3"] = np.concatenate([W3, g("L0_gnn_b3")[None]], axis=0)
    d["b1"] = np.concatenate([g("L0_gnn_b1")] * 2).reshape(P, 1)
    d["b2"] = np.concatenate([g("L0_gnn_b2")] * 2).reshape(P, 1)
    mean = 1.0 / np.sqrt(2.0 * MUL) / np.sqrt(16.0)
    d["w3_scale"] = np.full((HID + 1, 256), mean, f)
    d["w3_scale"][:, MUL * MUL:2 * MUL * MUL] = mean / np.sqrt(3.0)
    d["spread"] = np.zeros((P, GROUP, J), f)
    for q in range(4):
        for j in range(J):
            d["spread"][CH * q + j, j % GROUP, NG * q + j // GROUP] = 1.0
    one = np.zeros((CH, CH), f)
    one[:MUL, :MUL] = g("L0_gnn_Ws")
    for i in range(3):
        one[MUL + i::3, MUL + i::3] = g("L0_gnn_Wv")
    d["w_self"] = np.zeros((P, P), f)
    d["w_root"] = np.zeros((P, 3, P), f)
    for j in range(GROUP):
        own = slice(CH * j, CH * j + CH)
        d["w_self"][own, own] = one
        for l in range(3):
            d["w_root"][own, l, own] = g(f"L1_gnn_R{l + 1}")
    for l in range(3):
        taps = np.zeros((P, TAPS, P), f)
        for j in range(GROUP):
            taps[CH * j:CH * j + CH, :, CH * j:CH * j + CH] = g(f"L1_gnn_W{l + 1}").transpose(1, 0, 2)
        d[f"w_taps{l}"] = taps
    d["chan"] = np.stack([np.stack([g(f"L1_gnn_{k}{l + 1}") for k in ("b", "g", "be")]) for l in range(3)])[None]
    rows = np.ones((P, 1), f)
    d["ident"] = np.eye(P, dtype=f)
    d["ones"] = np.ones((P, P), f)
    d["slot_ids"] = rows * np.arange(J, dtype=f)
    d["item_ids"] = np.arange(nb * P, dtype=f).reshape(nb, P).T
    d["half_ids"] = (2 * np.arange(wb * P, dtype=f).reshape(wb, P).T[:, :, None] + np.arange(2, dtype=f))
    d["window_ids"] = np.arange(wb * P, dtype=f).reshape(wb, P).T
    d["tile_ids"] = np.arange(tiles, dtype=f).reshape(1, tiles)
    node = ((wb - 1) * P + np.arange(P)[:, None]) * J + np.arange(J)
    d["node_mask"] = (node < nodes).astype(f)
    return nodes, edges, {k: np.ascontiguousarray(v_) for k, v_ in d.items()}


def kernel(**inputs):
    import concourse.bacc as bacc
    from concourse.bass_utils import run_bass_kernel_spmd

    nodes, edges, data = prepare(inputs)
    nc = bacc.Bacc("TRN2", target_bir_lowering=False, num_devices=1)
    arrays, args = {}, {}
    for name, v_ in data.items():
        arrays[f"in_{name}"] = v_
        args[name] = nc.dram_tensor(f"in_{name}", v_.shape, mybir.dt.from_np(v_.dtype), kind="ExternalInput").ap()
    out = nc.dram_tensor("out_nodes", data["x"].shape, mybir.dt.float32, kind="ExternalOutput").ap()
    graph_kernel(nc, nodes, edges, args, out)
    got = run_bass_kernel_spmd(nc, [arrays], core_ids=[0])
    return got.results[0]["out_nodes"][:nodes]
```
